# Optimizing a Trainium2 kernel written in Bass

```python
import numpy as np
import jax
import jax.numpy as jnp

def _softmax(x, axis=-1):
    return jax.nn.softmax(x, axis=axis)

def _gelu(x):
    return jax.nn.gelu(x, approximate=True)

def _silu(x):
    return jax.nn.silu(x)

def _sigmoid(x):
    return jax.nn.sigmoid(x)

def _layernorm(x, axis=-1, eps=1e-05):
    m = jnp.mean(x, axis=axis, keepdims=True)
    v = jnp.var(x, axis=axis, keepdims=True)
    return (x - m) / jnp.sqrt(v + eps)

def _scatter_add(tgt, idx, src, axis=0):
    return tgt.at[idx].add(src)

def _segment_sum(src, seg, n):
    return jax.ops.segment_sum(src, seg, n)
kernel_name = 'mk_gnn_ffn_d2_gnn_r16_1f936d'

def setup_inputs(seed: int=0):
    np.random.seed(seed)
    _w = jnp.asarray

    def _rec_inputs():
        import jax
        import jax.numpy as jnp
        _gk = jax.random.key(seed)
        x = -7.329e-05 + 0.9999 * jax.random.normal(jax.random.fold_in(_gk, 1), (625, 512), jnp.float32)
        src = jax.random.randint(jax.random.fold_in(_gk, 2), (20000,), 0, 625, jnp.int32)
        dst = jax.random.randint(jax.random.fold_in(_gk, 3), (20000,), 0, 625, jnp.int32)
        _o = jnp.argsort(dst, stable=True)
        src = src[_o]
        dst = dst[_o]
        return (x, src, dst)
    x, src, dst = _rec_inputs()

    def _L0_gnn_setup():
        import jax, jax.numpy as jnp
        import numpy as np
        N_NODES = 6250
        N_EDGES = 100000
        IN_CH = 512
        HID_CH = 128

        def _gcn_conv(x, edge_index, W_conv, b_conv):
            N = x.shape[0]
            loop = jnp.arange(N, dtype=edge_index.dtype)
            row = jnp.concatenate([edge_index[0], loop])
            col = jnp.concatenate([edge_index[1], loop])
            ones = jnp.ones(row.shape[0], dtype=x.dtype)
            deg = jax.ops.segment_sum(ones, col, num_segments=N)
            deg_inv_sqrt = jnp.where(deg > 0, jax.lax.rsqrt(deg), 0.0)
            norm = deg_inv_sqrt[row] * deg_inv_sqrt[col]
            h = x @ W_conv
            msg = h[row] * norm[:, None]
            out = jax.ops.segment_sum(msg, col, num_segments=N)
            return out + b_conv
        key = jax.random.key(seed)
        k1, k2, k3, k4, k5, k6 = jax.random.split(key, 6)
        x = jax.random.normal(k1, (N_NODES, IN_CH), dtype=jnp.float32)
        edge_index = jax.random.randint(k2, (2, N_EDGES), 0, N_NODES, dtype=jnp.int64)
        W_conv = jax.random.normal(k3, (IN_CH, HID_CH), dtype=jnp.float32) / np.sqrt(IN_CH)
        b_conv = jnp.zeros((HID_CH,), dtype=jnp.float32)
        W_lin = jax.random.normal(k4, (HID_CH, IN_CH), dtype=jnp.float32) / np.sqrt(HID_CH)
        b_lin = jnp.zeros((IN_CH,), dtype=jnp.float32)
        return {'x': x, 'edge_index': edge_index, 'W_conv': W_conv, 'b_conv': b_conv, 'W_lin': W_lin, 'b_lin': b_lin}
    _L0_gnn_all = _L0_gnn_setup()
    _L0_gnn_in = {k: v for k, v in _L0_gnn_all.items() if k in ('W_conv', 'b_conv', 'W_lin', 'b_lin')}
    del _L0_gnn_all

    def _L0_ffn_setup():
        import jax, jax.numpy as jnp
        import numpy as np
        MARK_AX, OP_ADD, OP_SUB = (0, 1, 2)
        ALU_LO, ALU_HI = (16, 32)
        AX_CARRY_LO, AX_CARRY_HI = (48, 64)
        OPCODE_BASE = 80
        OUTPUT_LO, OUTPUT_HI, CARRY = (128, 144, 160)
        NIB_A, NIB_B, OP_START = (0, 1, 10)
        RESULT, CARRY_OUT = (100, 101)
        GE_POS, GE_DIM = (8, 160)
        OPC_ADD, OPC_SUB = (25, 26)
        B, S, D = (8, 256, 512)

        def _decode_nibble(x, base):
            return jnp.argmax(x[..., base:base + 16] > 0.5, axis=-1).astype(x.dtype)

        def _pipeline(h, W, b):
            for i in range(3):
                h = jnp.einsum('bspd,od->bspo', h, W[i]) + b[i]
                if i < 2:
                    h = jax.nn.relu(h)
            return h
        key = jax.random.key(seed)
        kx, k1, k2, k3, k4 = jax.random.split(key, 5)
        x_bd = jax.random.uniform(kx, (B, S, D), dtype=jnp.float32)
        Wa = jax.random.normal(k1, (3, GE_DIM, GE_DIM), dtype=jnp.float32) * 0.05
        ba = jax.random.normal(k2, (3, GE_DIM), dtype=jnp.float32) * 0.05
        Ws = jax.random.normal(k3, (3, GE_DIM, GE_DIM), dtype=jnp.float32) * 0.05
        bs = jax.random.normal(k4, (3, GE_DIM), dtype=jnp.float32) * 0.05
        return {'x_bd': x_bd, 'Wa': Wa, 'ba': ba, 'Ws': Ws, 'bs': bs}
    _L0_ffn_all = _L0_ffn_setup()
    _L0_ffn_in = {k: v for k, v in _L0_ffn_all.items() if k in ('Wa', 'ba', 'Ws', 'bs')}
    del _L0_ffn_all

    def _L1_gnn_setup():
        import jax, jax.numpy as jnp
        import numpy as np
        N_NODES = 3125
        N_EDGES = 50000
        HIDDEN = 512
        LAYERS = 3
        key = jax.random.key(seed)
        k1, k2, k3 = jax.random.split(key, 3)
        x = jax.random.normal(k1, (N_NODES, HIDDEN), dtype=jnp.float32)
        edge_index = jax.random.randint(k2, (2, N_EDGES), 0, N_NODES, dtype=jnp.int64)
        W = jax.random.normal(k3, (LAYERS, HIDDEN, HIDDEN), dtype=jnp.float32) / np.float32(np.sqrt(HIDDEN))
        b = jnp.zeros((LAYERS, HIDDEN), dtype=jnp.float32)
        return {'x': x, 'edge_index': edge_index, 'W': W, 'b': b}
    _L1_gnn_all = _L1_gnn_setup()
    _L1_gnn_in = {k: v for k, v in _L1_gnn_all.items() if k in ('W', 'b')}
    del _L1_gnn_all

    def _L1_ffn_setup():
        import jax, jax.numpy as jnp
        import numpy as np
        DIM = 512
        DEPTH = 4
        E = 2 ** DEPTH
        HID = 4 * DIM
        B, S = (8, 256)

        def _fff_forward(x, Wr, br, W1, b1, W2, b2):
            Bb, Ss, D = x.shape
            E_ = W1.shape[0]
            depth = int(np.log2(E_))
            xf = x.reshape(-1, D)
            N = xf.shape[0]
            leaf = jnp.zeros((N,), jnp.int32)
            for d in range(depth):
                off = 2 ** d - 1
                cnt = 2 ** d
                logits = xf @ Wr[off:off + cnt].T + br[off:off + cnt]
                sel = jnp.take_along_axis(logits, leaf[:, None], axis=1)[:, 0]
                leaf = leaf * 2 + (sel > 0).astype(jnp.int32)
            onehot = jax.nn.one_hot(leaf, E_, dtype=xf.dtype)

            def body(acc, params):
                w1, bb1, w2, bb2, m = params
                h = jax.nn.gelu(xf @ w1 + bb1, approximate=False)
                y = h @ w2 + bb2
                return (acc + m[:, None] * y, None)
            out, _ = jax.lax.scan(body, jnp.zeros_like(xf), (W1, b1, W2, b2, onehot.T))
            return out.reshape(Bb, Ss, D)
        key = jax.random.key(seed)
        ks = jax.random.split(key, 7)
        sc_in = 1.0 / np.sqrt(DIM)
        sc_hid = 1.0 / np.sqrt(HID)
        return {'x': jax.random.normal(ks[0], (B, S, DIM), jnp.float32), 'Wr': jax.random.normal(ks[1], (E - 1, DIM), jnp.float32) * sc_in, 'br': jax.random.normal(ks[2], (E - 1,), jnp.float32) * 0.01, 'W1': jax.random.normal(ks[3], (E, DIM, HID), jnp.float32) * sc_in, 'b1': jax.random.normal(ks[4], (E, HID), jnp.float32) * 0.01, 'W2': jax.random.normal(ks[5], (E, HID, DIM), jnp.float32) * sc_hid, 'b2': jax.random.normal(ks[6], (E, DIM), jnp.float32) * 0.01}
    _L1_ffn_all = _L1_ffn_setup()
    _L1_ffn_in = {k: v for k, v in _L1_ffn_all.items() if k in ('Wr', 'br', 'W1', 'b1', 'W2', 'b2')}
    del _L1_ffn_all
    return {'x': x, 'src': src, 'dst': dst, 'L0_gnn_W_conv': _L0_gnn_in['W_conv'], 'L0_gnn_b_conv': _L0_gnn_in['b_conv'], 'L0_gnn_W_lin': _L0_gnn_in['W_lin'], 'L0_gnn_b_lin': _L0_gnn_in['b_lin'], 'L0_ffn_Wa': _L0_ffn_in['Wa'], 'L0_ffn_ba': _L0_ffn_in['ba'], 'L0_ffn_Ws': _L0_ffn_in['Ws'], 'L0_ffn_bs': _L0_ffn_in['bs'], 'L1_gnn_W': _L1_gnn_in['W'], 'L1_gnn_b': _L1_gnn_in['b'], 'L1_ffn_Wr': _L1_ffn_in['Wr'], 'L1_ffn_br': _L1_ffn_in['br'], 'L1_ffn_W1': _L1_ffn_in['W1'], 'L1_ffn_b1': _L1_ffn_in['b1'], 'L1_ffn_W2': _L1_ffn_in['W2'], 'L1_ffn_b2': _L1_ffn_in['b2']}

def reference(x, src, dst, L0_gnn_W_conv, L0_gnn_b_conv, L0_gnn_W_lin, L0_gnn_b_lin, L0_ffn_Wa, L0_ffn_ba, L0_ffn_Ws, L0_ffn_bs, L1_gnn_W, L1_gnn_b, L1_ffn_Wr, L1_ffn_br, L1_ffn_W1, L1_ffn_b1, L1_ffn_W2, L1_ffn_b2):
    import jax
    import jax.numpy as jnp

    def _L0_gnn_ref(x, edge_index, W_conv, b_conv, W_lin, b_lin):
        import jax, jax.numpy as jnp
        import numpy as np
        N_NODES = 6250
        N_EDGES = 100000
        IN_CH = 512
        HID_CH = 128

        def _gcn_conv(x, edge_index, W_conv, b_conv):
            N = x.shape[0]
            loop = jnp.arange(N, dtype=edge_index.dtype)
            row = jnp.concatenate([edge_index[0], loop])
            col = jnp.concatenate([edge_index[1], loop])
            ones = jnp.ones(row.shape[0], dtype=x.dtype)
            deg = jax.ops.segment_sum(ones, col, num_segments=N)
            deg_inv_sqrt = jnp.where(deg > 0, jax.lax.rsqrt(deg), 0.0)
            norm = deg_inv_sqrt[row] * deg_inv_sqrt[col]
            h = x @ W_conv
            msg = h[row] * norm[:, None]
            out = jax.ops.segment_sum(msg, col, num_segments=N)
            return out + b_conv
        h = _gcn_conv(x, edge_index, W_conv, b_conv)
        return h @ W_lin + b_lin

    def _L0_ffn_ref(x_bd, Wa, ba, Ws, bs):
        import jax, jax.numpy as jnp
        import numpy as np
        MARK_AX, OP_ADD, OP_SUB = (0, 1, 2)
        ALU_LO, ALU_HI = (16, 32)
        AX_CARRY_LO, AX_CARRY_HI = (48, 64)
        OPCODE_BASE = 80
        OUTPUT_LO, OUTPUT_HI, CARRY = (128, 144, 160)
        NIB_A, NIB_B, OP_START = (0, 1, 10)
        RESULT, CARRY_OUT = (100, 101)
        GE_POS, GE_DIM = (8, 160)
        OPC_ADD, OPC_SUB = (25, 26)
        B, S, D = (8, 256, 512)

        def _decode_nibble(x, base):
            return jnp.argmax(x[..., base:base + 16] > 0.5, axis=-1).astype(x.dtype)

        def _pipeline(h, W, b):
            for i in range(3):
                h = jnp.einsum('bspd,od->bspo', h, W[i]) + b[i]
                if i < 2:
                    h = jax.nn.relu(h)
            return h
        x = x_bd
        Bsz, seq, _ = x.shape
        x_ge = jnp.zeros((Bsz, seq, GE_POS, GE_DIM), dtype=x.dtype)
        x_ge = x_ge.at[..., 0, NIB_A].set(_decode_nibble(x, ALU_LO))
        x_ge = x_ge.at[..., 1, NIB_A].set(_decode_nibble(x, ALU_HI))
        x_ge = x_ge.at[..., 0, NIB_B].set(_decode_nibble(x, AX_CARRY_LO))
        x_ge = x_ge.at[..., 1, NIB_B].set(_decode_nibble(x, AX_CARRY_HI))
        x_ge = x_ge.at[..., :, OP_START + OPC_ADD].set(x[..., OPCODE_BASE + OPC_ADD][..., None])
        x_ge = x_ge.at[..., :, OP_START + OPC_SUB].set(x[..., OPCODE_BASE + OPC_SUB][..., None])
        mark = x[..., MARK_AX] > 0.5
        m_add = mark & (x[..., OP_ADD] > 0.5)
        m_sub = mark & ~(x[..., OP_ADD] > 0.5) & (x[..., OP_SUB] > 0.5)
        active = (m_add | m_sub).astype(x.dtype)
        y_add = _pipeline(x_ge, Wa, ba)
        y_sub = _pipeline(x_ge, Ws, bs)
        y = jnp.where(m_add[..., None, None], y_add, jnp.where(m_sub[..., None, None], y_sub, x_ge))
        res_lo = jnp.clip(jnp.round(y[..., 0, RESULT]), 0, 15).astype(jnp.int32)
        res_hi = jnp.clip(jnp.round(y[..., 1, RESULT]), 0, 15).astype(jnp.int32)
        oh_lo = jax.nn.one_hot(res_lo, 16, dtype=x.dtype) * active[..., None]
        oh_hi = jax.nn.one_hot(res_hi, 16, dtype=x.dtype) * active[..., None]
        carry = (jnp.round(y[..., 1, CARRY_OUT]) > 0.5).astype(x.dtype) * active
        out = x
        out = out.at[..., OUTPUT_LO:OUTPUT_LO + 16].add(2.0 * oh_lo)
        out = out.at[..., OUTPUT_HI:OUTPUT_HI + 16].add(2.0 * oh_hi)
        out = out.at[..., CARRY].add(carry)
        return out

    def _L1_gnn_ref(x, edge_index, W, b):
        import jax, jax.numpy as jnp
        import numpy as np
        N_NODES = 3125
        N_EDGES = 50000
        HIDDEN = 512
        LAYERS = 3
        n = x.shape[0]
        loops = jnp.arange(n, dtype=edge_index.dtype)
        src = jnp.concatenate([edge_index[0], loops])
        dst = jnp.concatenate([edge_index[1], loops])
        deg = jax.ops.segment_sum(jnp.ones_like(dst, dtype=x.dtype), dst, num_segments=n)
        dis = jax.lax.rsqrt(jnp.maximum(deg, 1.0))
        norm = (dis[src] * dis[dst])[:, None]
        for l in range(W.shape[0]):
            h = x @ W[l]
            msg = h[src] * norm
            agg = jax.ops.segment_sum(msg, dst, num_segments=n) + b[l]
            x = jax.nn.relu(agg)
        return x

    def _L1_ffn_ref(x, Wr, br, W1, b1, W2, b2):
        import jax, jax.numpy as jnp
        import numpy as np
        DIM = 512
        DEPTH = 4
        E = 2 ** DEPTH
        HID = 4 * DIM
        B, S = (8, 256)

        def _fff_forward(x, Wr, br, W1, b1, W2, b2):
            Bb, Ss, D = x.shape
            E_ = W1.shape[0]
            depth = int(np.log2(E_))
            xf = x.reshape(-1, D)
            N = xf.shape[0]
            leaf = jnp.zeros((N,), jnp.int32)
            for d in range(depth):
                off = 2 ** d - 1
                cnt = 2 ** d
                logits = xf @ Wr[off:off + cnt].T + br[off:off + cnt]
                sel = jnp.take_along_axis(logits, leaf[:, None], axis=1)[:, 0]
                leaf = leaf * 2 + (sel > 0).astype(jnp.int32)
            onehot = jax.nn.one_hot(leaf, E_, dtype=xf.dtype)

            def body(acc, params):
                w1, bb1, w2, bb2, m = params
                h = jax.nn.gelu(xf @ w1 + bb1, approximate=False)
                y = h @ w2 + bb2
                return (acc + m[:, None] * y, None)
            out, _ = jax.lax.scan(body, jnp.zeros_like(xf), (W1, b1, W2, b2, onehot.T))
            return out.reshape(Bb, Ss, D)
        return _fff_forward(x, Wr, br, W1, b1, W2, b2)
    edge_index = jnp.stack([src, dst])
    x = x + _L0_gnn_ref(_layernorm(x, axis=-1), edge_index, L0_gnn_W_conv, L0_gnn_b_conv, L0_gnn_W_lin, L0_gnn_b_lin)
    x = x + _L0_ffn_ref(_layernorm(x, axis=-1)[None], L0_ffn_Wa, L0_ffn_ba, L0_ffn_Ws, L0_ffn_bs)[0]
    x = x + _L1_gnn_ref(_layernorm(x, axis=-1), edge_index, L1_gnn_W, L1_gnn_b)
    x = x + _L1_ffn_ref(_layernorm(x, axis=-1)[None], L1_ffn_Wr, L1_ffn_br, L1_ffn_W1, L1_ffn_b1, L1_ffn_W2, L1_ffn_b2)[0]
    return x

_drawn_inputs = setup_inputs


def setup_inputs(seed=0):
    import zlib

    import numpy as np

    out = dict(_drawn_inputs(seed))
    spreads = {'L0_gnn_b_conv': (0.0, 0.1), 'L0_gnn_b_lin': (0.0, 0.1), 'L1_gnn_b': (0.0, 0.1)}
    factors = {'L1_ffn_b1': 8.0, 'L1_ffn_b2': 8.0}
    for name, (base, spread) in spreads.items():
        noise = np.random.default_rng([zlib.crc32(name.encode()), seed]).standard_normal(out[name].shape)
        drawn = base * np.exp(spread * noise) if base else spread * noise
        out[name] = jnp.asarray(drawn.astype(out[name].dtype))
    for name, factor in factors.items():
        out[name] = (out[name] * factor).astype(out[name].dtype)
    return out
```

```python
from contextlib import ExitStack

import numpy as np
import concourse.bass as bass
from concourse import mybir

F32 = mybir.dt.float32
BF16 = mybir.dt.bfloat16
F16 = mybir.dt.float16
I32 = mybir.dt.int32
U32 = mybir.dt.uint32
ALU = mybir.AluOpType
ACT = mybir.ActivationFunctionType
AX = mybir.AxisListType

N_NODES, DIM, N_EDGES = 625, 512, 20000
NCH = 5
NC = N_NODES // NCH
KD = DIM // 128
HALF = (N_NODES + 1) // 2
NPAD = 2 * HALF
HALVES = ((0, HALF), (HALF, N_NODES))
EPS = 1e-5

ET = N_EDGES // NC
RUNS = 5
RUN_TILES = ET // RUNS
RING = 4
GROUPS = RUN_TILES // RING
PACK = 4096.0
HIGH_BIAS = RUN_TILES * NC / 2 / PACK

GE = 160
GH = GE // 2
NF = 5
RESULT = 100

NE, HID = 16, 2048
MH = HID // 128
SLOTS = 80
MORE = -(-N_NODES // SLOTS) - 1
MAX_PAIRS = NE // 2 + -(-MORE // 2)
TAB = 2 * MAX_PAIRS
NB = MH + KD
ROUND = 12582912.0


def build(nc, x, src, dst, Wconv, bconv, Wlin, blin, Wa, ba, Ws, bs, Wg, bg, Wr, br, W1, b1, W2, b2, out):
    ctx = ExitStack()
    with ctx:
        ctx.enter_context(nc.allow_non_contiguous_dma(reason="small bias columns"))

        def sb(name, shape, dt=F32):
            return ctx.enter_context(nc.sbuf_tensor(name, shape, dt))

        def sem(name):
            return ctx.enter_context(nc.semaphore(name))

        w1_sb = [sb(f"w1_{b}", [128, KD, HID]) for b in range(2)]
        w2_sb = [sb(f"w2_{b}", [128, MH, DIM]) for b in range(2)]
        xs = sb("xs", [128, NCH, DIM])
        xn = sb("xn", [128, NCH, DIM])
        XT = sb("XT", [128, 4 * NPAD])
        H = sb("H", [128, NCH * DIM])
        FB = sb("FB", [128, 4 * NPAD])
        C = sb("C", [128, NCH, NPAD])
        G = sb("G", [128, KD * DIM])
        ident = sb("ident", [128, 128])
        ones = sb("ones", [128, 128])
        ones16 = sb("ones16", [128, 128], BF16)
        tri16 = sb("tri16", [128, 128], BF16)
        iota_i = FB[:, 0:NPAD].bitcast(I32)
        rev_i = FB[:, NPAD:NPAD + NCH * 64].bitcast(I32)
        iota = sb("iota", [128, NPAD], F16)
        rev = sb("rev", [128, NCH, 64], F16)
        stats = sb("stats", [128, NCH, 6])
        mv = sb("mv", [128, NCH, 2])
        rstd = sb("rstd", [128, NCH])
        bconv_c = sb("bconv_c", [128, 1])
        bg_c = sb("bg_c", [128, 2, KD])
        bf_c = sb("bf_c", [128, 2, 2])
        b3_b = sb("b3_b", [128, 2, 2])
        br_b = sb("br_b", [128, 15])
        wr_T = sb("wr_T", [128, KD, 15])
        dis_c = sb("dis_c", [128, NCH])
        w3_T = sb("w3_T", [128, 2, 2, 2])
        feat = sb("feat", [128, NCH, NF, 2])
        small = sb("small", [128, 728])
        gidx = sb("gidx", [128, NCH], U32)
        tab = sb("tab", [1, TAB], I32)
        npairs_t = sb("npairs_t", [1, 1], I32)
        thr_i = sb("thr_i", [128, 16], I32)
        thr = sb("thr", [128, 16])
        keyrel = sb("keyrel", [128, NCH])
        P = ctx.enter_context(nc.psum_tensor("P", [128, 8, 512], F32))

        S = H[:, 0:RING * HALF].bitcast(BF16).rearrange("p (r n) -> p r n", r=RING)
        D = H[:, 1252:1252 + RING * 157].bitcast(BF16).rearrange("p (r n) -> p r n", r=RING)
        v_sb = FB[:, 0:NCH * HALF].rearrange("p (m n) -> p m n", m=NCH)
        hi_sb = G[:, 0:3 * HALF].rearrange("p (m n) -> p m n", m=3)
        wconv = H[:, 1880:1880 + DIM].rearrange("p (k n) -> p k n", k=KD)
        h0 = FB[:, 1764:1764 + NCH * 128].rearrange("p (c n) -> p c n", c=NCH)
        ei = G[:, 0:2 * ET].bitcast(I32).rearrange("p (s t) -> p s t", s=2)
        blin_b = H[:, 640:640 + DIM]
        ef = small[:, 0:3 * ET].rearrange("p (s t) -> p s t", s=3)
        eg = small[:, 3 * ET:4 * ET]
        dis_r = FB[:, 0:NPAD]
        XTn = XT[:, :].rearrange("p (k n) -> p k n", k=KD)
        FBn = FB[:, :].rearrange("p (k n) -> p k n", k=KD)
        Hn = H[:, :].rearrange("p (c n) -> p c n", c=NCH)
        Gw = G[:, :].rearrange("p (k n) -> p k n", k=KD)
        wlin = XT[:, 0:DIM]
        wnat = XT[:, 640:640 + 4 * GE].rearrange("p (q m i) -> p q m i", q=2, m=2)
        wmid = sb("wmid", [128, 2, 2, GE])
        win = G[:, 1024:1024 + 4 * GE].rearrange("p (q s o) -> p q s o", q=2, s=2)
        fT = G[:, 0:N_NODES]
        hid1 = [XT, H]
        hid2 = [FB, XT]

        agg0 = H[:, 0:N_NODES]

        def ffn_group(g):
            layer, q, s, m, h = g // 16, g // 8 % 2, g // 4 % 2, g // 2 % 2, g % 2
            a, b = HALVES[h]
            dst_ap = ffn_view((hid2 if layer else hid1)[q])[0:GH, m, s, a:b]
            return layer, q, m, s, dst_ap, a, b

        def ffn_view(t):
            return t[:, 0:4 * N_NODES].rearrange("p (m s n) -> p m s n", m=2, s=2)

        bg2_b = FB[:, 0:DIM]
        wr_nat = XT[0:15, 1280:1280 + DIM]
        hT = [H[:, b * MH * SLOTS:(b + 1) * MH * SLOTS].rearrange("p (m s) -> p m s", m=MH) for b in range(2)]
        disp = [FB[:, b * NCH * SLOTS:(b + 1) * NCH * SLOTS].rearrange("p (c s) -> p c s", c=NCH) for b in range(2)]
        xe = [FB[:, 800 + b * KD * SLOTS:800 + (b + 1) * KD * SLOTS].rearrange("p (k s) -> p k s", k=KD) for b in range(2)]
        yT = [FB[:, 1440 + b * KD * SLOTS:1440 + (b + 1) * KD * SLOTS].rearrange("p (k s) -> p k s", k=KD) for b in range(2)]
        y_sb = [G[:, b * DIM:(b + 1) * DIM] for b in range(2)]
        brow = [G[0:NB, 1024 + b * 128:1024 + (b + 1) * 128] for b in range(2)]
        bT = [G[:, 1280 + b * NB:1280 + (b + 1) * NB] for b in range(2)]
        y_dram = nc.dram_tensor("y_rows", [TAB * SLOTS, DIM], F32, kind="Internal").ap()

        def sv(at, *dims):
            n = int(np.prod(dims))
            v = small[:, at:at + n]
            names = " ".join(f"d{i}" for i in range(len(dims)))
            if len(dims) > 1:
                v = v.rearrange(f"p ({names}) -> p {names}", **{f"d{i}": d for i, d in enumerate(dims)})
            return v

        leaf = sv(150, NCH, NE)
        oh16 = small[:, 230:230 + NCH * NE // 2].bitcast(BF16).rearrange("p (c e) -> p c e", e=NE)

        s_edges, s_x, s_wconv, s_blin, s_cols = (sem(n) for n in ("edges_in", "x_in", "wconv_in", "blin_in", "cols_in"))
        s_wlin, s_ffnw, s_win, s_gw, s_bg2 = (sem(n) for n in ("wlin_in", "ffnw_in", "win_in", "gnnw_in", "bg2_in"))
        s_w1 = [sem(f"w1_in{b}") for b in range(2)]
        s_w2 = [[sem(f"w2_in{b}_{q}") for q in range(4)] for b in range(2)]
        s_brow = [sem(f"brow_in{b}") for b in range(2)]
        s_iota, s_ident, s_rev, s_ones, s_c0, s_winz, s_xb = (sem(n) for n in
            ("iota_ready", "ident_ready", "rev_ready", "ones_ready", "counts_cleared", "win_cleared", "x_plus_blin"))
        s_pool = sem("pool_chain")
        s_zero, s_yz = sem("zeros_ready"), sem("zeros_stored")
        s_dve = sem("dve_chain")
        s_act = sem("act_chain")
        s_var, s_std, s_ln = sem("var_ready"), sem("std_ready"), sem("layernorm_ready")
        s_tp, s_tpc = sem("transposed"), sem("transposed_copied")
        s_h0, s_h0c = sem("h0_ready"), sem("h0_copied")
        s_onehot, s_used = sem("onehot_ready"), sem("onehot_used")
        s_cnt, s_cntc, s_high, s_acc = (sem(n) for n in ("count_bank_done", "count_bank_free", "count_high_ready", "count_added"))
        s_deg, s_sq, s_dis, s_disc, s_A = (sem(n) for n in ("degree_ready", "sqrt_degree_ready", "dis_ready", "dis_col", "adjacency_ready"))
        s_dcp = sem("dis_col_product")
        s_agg0, s_agg0c, s_lin, s_x1 = sem("agg0_ready"), sem("agg0_copied"), sem("lin_ready"), sem("x1_ready")
        s_feat, s_fT, s_fTc, s_wmid, s_wmidc = (sem(n) for n in ("feat_ready", "featT", "featT_copied", "wmid_T", "wmid_copied"))
        s_fm, s_fd, s_fa, s_y3 = sem("ffn_mm"), sem("ffn_dve_copied"), sem("ffn_act_copied"), sem("ffn_out_ready")
        s_xsum = sem("x1_plus_norm")
        s_gh, s_ghc, s_ga, s_gac, s_x3 = (sem(n) for n in ("gnn_h", "gnn_h_copied", "gnn_agg", "gnn_agg_copied", "x3_ready"))
        s_wrT, s_wrTc, s_lg, s_oh, s_rank, s_table = (sem(n) for n in ("wr_T", "wr_T_copied", "logits", "onehot16", "ranks", "table_ready"))
        s_P, s_xe, s_xec = sem("dispatch_ready"), sem("xe_ready"), sem("xe_copied")
        s_ht, s_gelu, s_l2 = sem("hidden_ready"), sem("gelu_done"), sem("expert_out_ready")
        s_bT, s_bTc, s_yT, s_ytp, s_ycp = sem("biasT"), sem("biasT_copied"), sem("yT_ready"), sem("y_transposed"), sem("y_copied")
        s_yst = [sem(f"y_stored{b}") for b in range(2)]
        s_ech = sem("expert_dve_chain")
        s_gat, s_fin, s_out, s_stored = [sem(f"y_gathered{c}") for c in range(NCH)], sem("final_ready"), sem("out_stored"), sem("all_tiles_stored")

        block = ctx.enter_context(nc.Block())

        def rows16(n):
            return ((0, n // 16 * 16), (n // 16 * 16, n))

        @block.sync
        def _(sp):
            sp.dma_start(ei[0:NC, 1, :], dst.rearrange("(p t) -> p t", t=ET)).then_inc(s_edges, 16)
            sp.dma_start(ei[0:NC, 0, :], src.rearrange("(p t) -> p t", t=ET)).then_inc(s_edges, 16)
            xv = x.rearrange("(c p) d -> p c d", p=NC)
            for a, b in rows16(NC):
                sp.dma_start(xs[a:b, :, :], xv[a:b]).then_inc(s_x, 16)
            sp.dma_start(wconv, Wconv.rearrange("(k p) n -> p k n", p=128)).then_inc(s_wconv, 16)
            sp.wait_ge(s_zero, 1)
            sp.dma_start(y_dram[NE * SLOTS:TAB * SLOTS, :].rearrange("(p c) n -> p c n", p=128), xn[:, :, :]).then_inc(s_yz, 16)
            sp.dma_start(bconv_c[:, :], bconv.rearrange("(p a) -> p a", a=1)).then_inc(s_cols, 16)
            for l in range(2):
                sp.dma_start(bg_c[:, l, :], bg[l, :].rearrange("(k p) -> p k", p=128)).then_inc(s_cols, 16)
            sp.dma_start(br_b[0:NC, :], br.rearrange("(a n) -> a n", a=1).to_broadcast([NC, 15])).then_inc(s_cols, 16)
            for q, (w, b) in enumerate(((Wa, ba), (Ws, bs))):
                sp.dma_start(wnat[0:GH, q, :, :], w[1].rearrange("(m p) i -> p m i", p=GH)).then_inc(s_ffnw, 16)
                sp.dma_start(bf_c[0:GH, q, :], b[1, :].rearrange("(m p) -> p m", p=GH)).then_inc(s_ffnw, 16)
                sp.dma_start(b3_b[0:NC, q, :], b[2:3, RESULT:RESULT + 2].to_broadcast([NC, 2])).then_inc(s_ffnw, 16)
                for r in range(2):
                    sp.dma_start(w3_T[0:GH, q, :, r], w[2, RESULT + r, :].rearrange("(m p) -> p m", p=GH)).then_inc(s_ffnw, 16)
            sp.dma_start(wr_nat, Wr).then_inc(s_ffnw, 16)
            for b in range(2):
                for k in range(KD):
                    sp.dma_start(w1_sb[b][:, k, :], W1[b, k * 128:(k + 1) * 128, :]).then_inc(s_w1[b], 16)
                for q in range(4):
                    sp.dma_start(w2_sb[b][:, 4 * q:4 * q + 4, :],
                                 W2[b, q * DIM:(q + 1) * DIM, :].rearrange("(m p) n -> p m n", p=128)).then_inc(s_w2[b][q], 16)
            sp.wait_ge(s_used, ET)
            sp.dma_start(blin_b[0:NC, :], blin.rearrange("(a n) -> a n", a=1).to_broadcast([NC, DIM])).then_inc(s_blin, 16)
            sp.wait_ge(s_h0, 2)
            sp.dma_start(wlin, Wlin).then_inc(s_wlin, 16)
            sp.wait_ge(s_winz, 1)
            for q, (w, b) in enumerate(((Wa, ba), (Ws, bs))):
                for s in range(2):
                    for f0, i0 in ((0, 0), (2, 35)):
                        for f in range(2):
                            r = 2 * (f0 + f) + s
                            sp.dma_start(win[r:r + 1, q, s, :], w[0, :, i0 + f:i0 + f + 1].rearrange("o a -> a o")).then_inc(s_win, 16)
                    sp.dma_start(win[8 + s:9 + s, q, s, :], b[0:1, :]).then_inc(s_win, 16)
            sp.wait_ge(s_y3, 1)
            for l in range(3):
                if l:
                    sp.wait_ge(s_gh, NCH * l)
                sp.dma_start(Gw, Wg[l].rearrange("(k p) n -> p k n", p=128)).then_inc(s_gw, 16)
                if l == 0:
                    sp.dma_start(bg2_b[0:NC, :], bg[2:3, :].to_broadcast([NC, DIM])).then_inc(s_bg2, 16)
            sp.wait_ge(s_gh, NCH * 3)

            def load_brow(b, e):
                sp.dma_start(brow[b][0:MH, :], b1[e].rearrange("a (m p) -> (a m) p", p=128)).then_inc(s_brow[b], 16)
                sp.dma_start(brow[b][MH:NB, :], b2[e].rearrange("a (m p) -> (a m) p", p=128)).then_inc(s_brow[b], 16)

            for b in range(2):
                load_brow(b, slice(b, b + 1))
            sp.wait_ge(s_table, 1)
            pairs = sp.value_load(npairs_t[0:1, 0:1], min_val=NE // 2, max_val=MAX_PAIRS)
            with sp.Fori(0, pairs - 1) as p:
                for b in range(2):
                    done = 2 * p + b + 1
                    e = sp.value_load(tab[0:1, bass.ds(done + 1, 1)], min_val=0, max_val=NE - 1)
                    sp.wait_ge(s_bT, done)
                    load_brow(b, bass.ds(e, 1))
                    sp.wait_ge(s_ht, done * 4)
                    for k in range(KD):
                        sp.dma_start(w1_sb[b][:, k, :], W1[bass.ds(e, 1), k * 128:(k + 1) * 128, :].rearrange("a p n -> (a p) n")).then_inc(s_w1[b], 16)
                    sp.wait_ge(s_l2, done)
                    for q in range(4):
                        sp.dma_start(w2_sb[b][:, 4 * q:4 * q + 4, :],
                                     W2[bass.ds(e, 1), q * DIM:(q + 1) * DIM, :].rearrange("a (m p) n -> p (a m) n", p=128)).then_inc(s_w2[b][q], 16)
            sp.wait_ge(s_xe, 2 * pairs)
            load_brow(0, slice(0, 1))
            for c in range(NCH):
                sp.wait_ge(s_fin, c + 1)
                for i, (a, b) in enumerate(rows16(NC)):
                    sp.dma_start(out[c * NC + a:c * NC + b, :], xs[a:b, c, :]).then_inc(s_out, 16)
            sp.wait_ge(s_out, 16 * 2 * NCH)

        @block.gpsimd
        def _(pool):
            n = [0]

            def link(ins):
                n[0] += 1
                ins.then_inc(s_pool, 1)
                pool.wait_ge(s_pool, n[0])

            nc.gpsimd.iota(iota_i[:, :], pattern=[[1, NPAD]], base=0, channel_multiplier=0).then_inc(s_iota, 1)
            nc.gpsimd.iota(rev_i, pattern=[[0, NCH * 4], [-1, 16]], base=16, channel_multiplier=0).then_inc(s_rev, 1)
            nc.gpsimd.memset(xn[:, :, :], 0.0).then_inc(s_zero, 1)
            link(nc.gpsimd.memset(ident[:, :], 0.0))
            nc.gpsimd.affine_select(out=ident[:, :], in_=ident[:, :], compare_op=ALU.not_equal, fill=1.0, base=0,
                                    pattern=[[-1, 128]], channel_multiplier=1).then_inc(s_ident, 1)
            nc.gpsimd.iota(thr_i[:, :], pattern=[[SLOTS, 16]], base=SLOTS, channel_multiplier=0).then_inc(s_iota, 1)
            nc.gpsimd.memset(ones16[:, :], 1.0).then_inc(s_ones, 1)
            link(nc.gpsimd.memset(ones[:, :], 1.0))
            nc.gpsimd.affine_select(out=tri16[:, :], in_=ones[:, :], compare_op=ALU.is_gt, fill=0.0, base=0,
                                    pattern=[[1, 128]], channel_multiplier=-1).then_inc(s_ones, 1)
            link(nc.gpsimd.memset(C[:, :, :], 0.0))
            nc.gpsimd.affine_select(out=C[0:NC, :, :], in_=C[0:NC, :, :], compare_op=ALU.not_equal, fill=1.0, base=0,
                                    pattern=[[NC, NCH], [-1, NPAD]], channel_multiplier=1).then_inc(s_c0, 1)
            pool.wait_ge(s_onehot, 1)
            nc.gpsimd.memset(G[:, 1024:1024 + 4 * GE], 0.0).then_inc(s_winz, 1)
            pool.wait_ge(s_c0, 1)
            pool.sem_inc(s_acc, 1)
            n0 = n[0]
            with pool.Fori(0, RUNS) as r:
                for m in range(NCH):
                    step = n0 + (r * NCH + m) * 2
                    v, hi = v_sb[0:NC, m, :], hi_sb[0:NC, m % 3, :]
                    pool.wait_ge(s_high, r * NCH + m + 1)
                    nc.gpsimd.tensor_tensor(C[0:NC, m, HALF:NPAD], C[0:NC, m, HALF:NPAD], hi, ALU.add)
                    nc.gpsimd.tensor_scalar(hi, hi, -PACK, None, ALU.mult).then_inc(s_pool, 1)
                    pool.wait_ge(s_pool, step + 1)
                    nc.gpsimd.tensor_tensor(v, v, hi, ALU.add).then_inc(s_pool, 1)
                    pool.wait_ge(s_pool, step + 2)
                    nc.gpsimd.tensor_tensor(C[0:NC, m, 0:HALF], C[0:NC, m, 0:HALF], v, ALU.add).then_inc(s_acc, 1)
            pool.wait_ge(s_blin, 16)
            pool.wait_ge(s_ln, 1)
            nc.gpsimd.tensor_tensor(xs[0:NC, :, :], xs[0:NC, :, :],
                                    blin_b[0:NC, :].unsqueeze(1).to_broadcast([NC, NCH, DIM]), ALU.add).then_inc(s_xb, 1)
            pool.wait_ge(s_ln, 2)
            nc.gpsimd.tensor_tensor(xs[0:NC, :, :], xs[0:NC, :, :], xn[0:NC, :, :], ALU.add).then_inc(s_xsum, 1)
            pool.wait_ge(s_table, 1)
            pairs = pool.value_load(npairs_t[0:1, 0:1], min_val=NE // 2, max_val=MAX_PAIRS)
            for b in range(2):
                pool.wait_ge(s_yst[b], 16 * pairs + 16)
            pool.sem_inc(s_stored, 1)
            pool.wait_ge(s_stored, 1)
            for c in range(NCH):
                nc.gpsimd.indirect_dma_start(out=xn[0:NC, c, :], out_offset=None, in_=y_dram[:, :],
                                             in_offset=bass.IndirectOffsetOnAxis(ap=gidx[0:NC, c:c + 1], axis=0)).then_inc(s_gat[c], 16)
            for c in range(NCH):
                pool.wait_ge(s_gat[c], 16)

        @block.scalar
        def _(act):
            ln_no = [0]

            def sqrt_var():
                ln_no[0] += 1
                act.wait_ge(s_var, ln_no[0])
                nc.scalar.activation(rstd[0:NC, :], rstd[0:NC, :], ACT.Sqrt).then_inc(s_std, 1)

            tp_no = [0]

            def copy_transposed():
                for c in range(NCH):
                    tp_no[0] += 1
                    act.wait_ge(s_tp, tp_no[0])
                    nc.scalar.activation(XTn[:, :, c * NC:(c + 1) * NC], P[:, c, 0:KD * NC].rearrange("p (k n) -> p k n", k=KD),
                                         ACT.Copy).then_inc(s_tpc, 1)

            act.sem_inc(s_cntc, NCH)
            with act.Fori(0, RUNS) as r:
                act.wait_ge(s_acc, r * NCH + 1)
                for m in range(NCH):
                    if m < NCH - 1:
                        act.wait_ge(s_cnt, r * (NCH - 1) + m + 1)
                    else:
                        act.wait_ge(s_used, (r + 1) * RUN_TILES)
                    nc.scalar.activation(v_sb[0:NC, m, :], P[0:NC, m, 0:HALF], ACT.Copy).then_inc(s_cntc, 1)
                for m in range(NCH):
                    hi = hi_sb[0:NC, m % 3, :]
                    step = (r * NCH + m) * 2
                    act.wait_ge(s_cntc, r * NCH + NCH + m + 1)
                    if m >= 3:
                        act.wait_ge(s_acc, r * NCH + m - 1)
                    nc.scalar.activation(hi, v_sb[0:NC, m, :], ACT.Copy, bias=-HIGH_BIAS, scale=1.0 / PACK).then_inc(s_act, 1)
                    act.wait_ge(s_act, step + 1)
                    nc.scalar.activation(hi, hi, ACT.Copy, bias=ROUND).then_inc(s_act, 1)
                    act.wait_ge(s_act, step + 2)
                    nc.scalar.activation(hi, hi, ACT.Copy, bias=-ROUND).then_inc(s_high, 1)
            act.wait_ge(s_wmid, 1)
            for q in range(2):
                nc.scalar.activation(wmid[0:GH, q, :, :], P[0:GH, 6 + q, 128:128 + 2 * GE].rearrange("p (k o) -> p k o", k=2),
                                     ACT.Copy).then_inc(s_wmidc, 1)
            nc.scalar.activation(wr_T[:, :, :], P[:, 7, 0:KD * 15].rearrange("p (k o) -> p k o", k=KD), ACT.Copy).then_inc(s_wmidc, 1)
            sqrt_var()
            copy_transposed()
            act.wait_ge(s_h0, 1)
            nc.scalar.activation(h0[0:NC, 0:4, :], P[0:NC, 5, :].rearrange("p (c n) -> p c n", c=4), ACT.Copy).then_inc(s_h0c, 1)
            act.wait_ge(s_h0, 2)
            nc.scalar.activation(h0[0:NC, 4, :], P[0:NC, 6, 0:128], ACT.Copy).then_inc(s_h0c, 1)
            for i, (a, b) in enumerate(HALVES):
                act.wait_ge(s_deg, i + 1)
                nc.scalar.activation(dis_r[:, a:b], P[:, i, 0:b - a], ACT.Sqrt).then_inc(s_sq, 1)
            act.wait_ge(s_cols, 16 * 4)
            for i, (a, b) in enumerate(HALVES):
                act.wait_ge(s_agg0, i + 1)
                nc.scalar.activation(agg0[:, a:b], P[:, 2 + i, 0:b - a], ACT.Identity, bias=bconv_c[:, 0:1]).then_inc(s_agg0c, 1)
            sqrt_var()
            act.wait_ge(s_ffnw, 16 * 11)
            for g in range(1, 32, 2):
                layer, q, m, s, dst_ap, a, b = ffn_group(g)
                act.wait_ge(s_fm, g + 1)
                nc.scalar.activation(dst_ap, P[0:GH, g % 8, 0:b - a], ACT.Relu,
                                     bias=(bf_c[0:GH, q, m:m + 1] if layer else 0.0)).then_inc(s_fa, 1)
            sqrt_var()
            copy_transposed()
            for l in range(2):
                for g in range(2 * KD):
                    m, (a, b) = g // 2, HALVES[g % 2]
                    act.wait_ge(s_ga, l * (2 * KD) + g + 1)
                    nc.scalar.activation(XTn[:, m, a:b], P[:, (5 + g) % 8, 0:b - a], ACT.Relu,
                                         bias=bg_c[:, l, m:m + 1]).then_inc(s_gac, 1)
            sqrt_var()
            copy_transposed()
            act.sem_inc(s_ycp, 1)
            for b in range(2):
                act.sem_inc(s_yst[b], 16)
            act.wait_ge(s_table, 1)
            pairs = act.value_load(npairs_t[0:1, 0:1], min_val=NE // 2, max_val=MAX_PAIRS)
            with act.Fori(0, pairs) as p:
                for b in range(2):
                    i = 2 * p + b
                    act.wait_ge(s_bTc, i + 1)
                    for m in range(MH):
                        if m % 4 == 0:
                            act.wait_ge(s_ht, i * 4 + m // 4 + 1)
                        nc.scalar.activation(hT[b][:, m, :], P[:, (m // 4) % 2, (m % 4) * SLOTS:(m % 4 + 1) * SLOTS], ACT.Gelu,
                                             bias=bT[b][:, m:m + 1]).then_inc(s_gelu, 1)
                    act.wait_ge(s_ytp, i + 1)
                    act.wait_ge(s_yst[b], 16 * p + 16)
                    nc.scalar.activation(y_sb[b][0:SLOTS, :], P[0:SLOTS, 7, :], ACT.Copy).then_inc(s_ycp, 1)
                    act.wait_ge(s_ycp, i + 2)
                    act.dma_start(y_dram[bass.ds(i * SLOTS, SLOTS), :], y_sb[b][0:SLOTS, :]).then_inc(s_yst[b], 16)

        @block.tensor
        def _(pe):
            def count_tile(r, tile, j, first=False, last=False):
                pe.wait_ge(s_onehot, tile + 1)
                for m in range(NCH):
                    if first:
                        pe.wait_ge(s_cntc, r * NCH + m + 1)
                    mm = nc.tensor.matmul(P[0:NC, m, 0:HALF], S[0:NC, j, m * NC:(m + 1) * NC], D[0:NC, j, 0:HALF],
                                          start=first, stop=last, skip_group_check=True)
                    if last and m < NCH - 1:
                        mm.then_inc(s_cnt, 1)
                mm.then_inc(s_used, 1)

            with pe.Fori(0, RUNS) as r:
                for j in range(RING):
                    count_tile(r, r * RUN_TILES + j, j, first=(j == 0))
                with pe.Fori(1, GROUPS - 1) as g:
                    for j in range(RING):
                        count_tile(r, r * RUN_TILES + g * RING + j, j)
                for j in range(RING):
                    count_tile(r, r * RUN_TILES + (GROUPS - 1) * RING + j, j, last=(j == RING - 1))

            pe.wait_ge(s_ident, 1)
            pe.wait_ge(s_ffnw, 16 * 11)
            for q in range(2):
                for k in range(2):
                    for m in range(2):
                        at = 128 + k * GE + m * GH
                        nc.tensor.transpose(P[0:GH, 6 + q, at:at + GH], wnat[0:GH, q, m, k * GH:(k + 1) * GH], ident[0:GH, 0:GH])
            for k in range(KD):
                t = nc.tensor.transpose(P[:, 7, k * 15:(k + 1) * 15], wr_nat[:, k * 128:(k + 1) * 128], ident[0:15, 0:15])
            t.then_inc(s_wmid, 1)

            ln_no = [0]

            def transpose_norm():
                ln_no[0] += 1
                pe.wait_ge(s_ln, ln_no[0])
                for c in range(NCH):
                    for k in range(KD):
                        t = nc.tensor.transpose(P[:, c, k * NC:(k + 1) * NC], xn[0:NC, c, k * 128:(k + 1) * 128], ident[0:NC, 0:NC])
                    t.then_inc(s_tp, 1)

            pe.wait_ge(s_cntc, NCH * (RUNS + 1))
            transpose_norm()
            pe.wait_ge(s_wmidc, 3)
            pe.wait_ge(s_wconv, 16)
            for c in range(NCH):
                pe.wait_ge(s_tpc, c + 1)
                for k in range(KD):
                    mm = nc.tensor.matmul(P[0:NC, 5 + c // 4, (c % 4) * 128:(c % 4 + 1) * 128], XTn[:, k, c * NC:(c + 1) * NC],
                                          wconv[:, k, :], start=(k == 0), stop=(k == KD - 1))
                if c >= 3:
                    mm.then_inc(s_h0, 1)
            pe.wait_ge(s_ones, 2)
            for c in range(NCH):
                pe.wait_ge(s_acc, NCH * (RUNS - 1) + c + 2)
                for i, (a, b) in enumerate(HALVES):
                    mm = nc.tensor.matmul(P[:, i, 0:b - a], ones[0:NC, :], C[0:NC, c, a:b], start=(c == 0), stop=(c == NCH - 1))
                    if c == NCH - 1:
                        mm.then_inc(s_deg, 1)
            pe.wait_ge(s_dis, 2)
            for c in range(NCH):
                mm = nc.tensor.matmul(P[0:NC, 7, 400 + c:401 + c], dis_r[0:1, c * NC:(c + 1) * NC], ones[0:1, 0:1], start=True, stop=True)
            mm.then_inc(s_dcp, 1)
            pe.wait_ge(s_h0c, 2)
            for c in range(NCH):
                pe.wait_ge(s_A, c + 1)
                for i, (a, b) in enumerate(HALVES):
                    mm = nc.tensor.matmul(P[:, 2 + i, 0:b - a], h0[0:NC, c, :], C[0:NC, c, a:b], start=(c == 0), stop=(c == NCH - 1))
                    if c == NCH - 1:
                        mm.then_inc(s_agg0, 1)
            pe.wait_ge(s_agg0c, 2)
            pe.wait_ge(s_wlin, 16)
            for c in range(NCH):
                nc.tensor.matmul(P[0:NC, c, :], agg0[:, c * NC:(c + 1) * NC], wlin, start=True, stop=True).then_inc(s_lin, 1)
            pe.wait_ge(s_feat, 1)
            for c in range(NCH):
                t = nc.tensor.transpose(P[0:2 * NF, c // 4, (c % 4) * NC:(c % 4 + 1) * NC],
                                        feat[0:NC, c, :, :].rearrange("p f s -> p (f s)"), ident[0:NC, 0:NC])
            t.then_inc(s_fT, 1)
            pe.wait_ge(s_fTc, 1)
            pe.wait_ge(s_win, 16 * 20)
            for g in range(32):
                layer, q, s, m, dst_ap, a, b = ffn_group(g)
                if g >= 8:
                    pe.wait_ge(s_fa if g % 2 else s_fd, (g - 8) // 2 + 1)
                if layer and g % 8 == 0:
                    pe.wait_ge(s_fd, 4 * (q + 1))
                    pe.wait_ge(s_fa, 4 * (q + 1))
                bank = P[0:GH, g % 8, 0:b - a]
                if layer == 0:
                    mm = nc.tensor.matmul(bank, win[0:2 * NF, q, s, m * GH:(m + 1) * GH], fT[0:2 * NF, a:b], start=True, stop=True)
                else:
                    for k in range(2):
                        mm = nc.tensor.matmul(bank, wmid[0:GH, q, k, m * GH:(m + 1) * GH], ffn_view(hid1[q])[0:GH, k, s, a:b],
                                              start=(k == 0), stop=(k == 1))
                mm.then_inc(s_fm, 1)
            for q in range(2):
                pe.wait_ge(s_fd, 12 + 4 * q)
                pe.wait_ge(s_fa, 12 + 4 * q)
                if q == 0:
                    pe.wait_ge(s_fd, 13)
                for c in range(NCH):
                    for s in range(2):
                        at = ((q * NCH + c) * 2 + s) * 2
                        for k in range(2):
                            mm = nc.tensor.matmul(P[0:NC, 0, at:at + 2], ffn_view(hid2[q])[0:GH, k, s, c * NC:(c + 1) * NC],
                                                  w3_T[0:GH, q, k, :], start=(k == 0), stop=(k == 1))
            mm.then_inc(s_y3, 1)

            ln_no[0] += 1
            transpose_norm()

            def gnn_h(l):
                pe.wait_ge(s_gw, 16 * (l + 1))
                for c in range(NCH):
                    for k in range(KD):
                        mm = nc.tensor.matmul(P[0:NC, c, :], XTn[:, k, c * NC:(c + 1) * NC], Gw[:, k, :], start=(k == 0), stop=(k == KD - 1))
                    mm.then_inc(s_gh, 1)

            pe.wait_ge(s_tpc, 2 * NCH)
            with pe.Fori(0, 2) as l:
                gnn_h(l)
                pe.wait_ge(s_ghc, l * NCH + NCH)
                for g in range(2 * KD):
                    m, (a, b) = g // 2, HALVES[g % 2]
                    for c in range(NCH):
                        mm = nc.tensor.matmul(P[:, (5 + g) % 8, 0:b - a], Hn[0:NC, c, m * 128:(m + 1) * 128], C[0:NC, c, a:b],
                                              start=(c == 0), stop=(c == NCH - 1))
                    mm.then_inc(s_ga, 1)
                pe.wait_ge(s_gac, l * (2 * KD) + 2 * KD)
            gnn_h(2)
            pe.wait_ge(s_ghc, 3 * NCH)
            for t in range(NCH):
                for c in range(NCH):
                    mm = nc.tensor.matmul(P[0:NC, (5 + t) % 8, :], C[0:NC, c, t * NC:(t + 1) * NC], Hn[0:NC, c, :],
                                          start=(c == 0), stop=(c == NCH - 1))
                mm.then_inc(s_ga, 1)

            pe.wait_ge(s_x3, NCH)
            transpose_norm()
            for c in range(NCH):
                pe.wait_ge(s_tpc, 2 * NCH + c + 1)
                for k in range(KD):
                    mm = nc.tensor.matmul(P[0:NC, 7, c * 15:(c + 1) * 15], XTn[:, k, c * NC:(c + 1) * NC], wr_T[:, k, :],
                                          start=(k == 0), stop=(k == KD - 1))
            mm.then_inc(s_lg, 1)
            pe.wait_ge(s_oh, 1)
            for c in range(NCH):
                for j in range(c + 1):
                    nc.tensor.matmul(P[0:NC, 6, c * NE:(c + 1) * NE], (tri16 if j == c else ones16)[0:NC, 0:NC], oh16[0:NC, j, :],
                                     start=(j == 0), stop=(j == c))
            for c in range(NCH):
                mm = nc.tensor.matmul(P[0:NC, 6, 128:128 + NE], ones16[0:NC, 0:NC], oh16[0:NC, c, :], start=(c == 0), stop=(c == NCH - 1))
            mm.then_inc(s_rank, 1)

            def dispatch(i, b):
                pe.wait_ge(s_P, i + 1)
                for k in range(KD):
                    for c in range(NCH):
                        mm = nc.tensor.matmul(P[:, 2, k * SLOTS:(k + 1) * SLOTS], xn[0:NC, c, k * 128:(k + 1) * 128],
                                              disp[b][0:NC, c, :], start=(c == 0), stop=(c == NCH - 1))
                mm.then_inc(s_xe, 1)

            def transpose_bias(i, use, b):
                pe.wait_ge(s_xec, i + 1)
                pe.wait_ge(s_brow[b], 32 * use)
                nc.tensor.matmul(P[:, 2, KD * SLOTS:KD * SLOTS + NB], brow[b], ident[0:NB, 0:NB], start=True, stop=True).then_inc(s_bT, 1)

            dispatch(0, 0)
            transpose_bias(0, 1, 0)
            pairs = pe.value_load(npairs_t[0:1, 0:1], min_val=NE // 2, max_val=MAX_PAIRS)
            with pe.Fori(0, pairs) as p:
                for b in range(2):
                    i = 2 * p + b
                    pe.wait_ge(s_xec, i + 1)
                    pe.wait_ge(s_w1[b], 16 * KD * (p + 1))
                    for m in range(MH):
                        if m >= 8 and m % 4 == 0:
                            pe.wait_ge(s_gelu, i * MH + m - 4)
                        for k in range(KD):
                            mm = nc.tensor.matmul(P[:, (m // 4) % 2, (m % 4) * SLOTS:(m % 4 + 1) * SLOTS],
                                                  w1_sb[b][:, k, m * 128:(m + 1) * 128], xe[b][:, k, :], start=(k == 0), stop=(k == KD - 1))
                        if m % 4 == 3:
                            mm.then_inc(s_ht, 1)
                    dispatch(i + 1, 1 - b)
                    for q in range(4):
                        pe.wait_ge(s_w2[b][q], 16 * (p + 1))
                        pe.wait_ge(s_gelu, i * MH + 4 * q + 4)
                        for n in range(KD):
                            for m in range(4 * q, 4 * q + 4):
                                mm = nc.tensor.matmul(P[:, 3 + n, 0:SLOTS], w2_sb[b][:, m, n * 128:(n + 1) * 128], hT[b][:, m, :],
                                                      start=(m == 0), stop=(m == MH - 1))
                    mm.then_inc(s_l2, 1)
                    transpose_bias(i + 1, p + 1 + b, 1 - b)
                    pe.wait_ge(s_yT, i + 1)
                    pe.wait_ge(s_ycp, i + 1)
                    for n in range(KD):
                        t = nc.tensor.transpose(P[0:SLOTS, 7, n * 128:(n + 1) * 128], yT[b][:, n, :], ident[:, :])
                    t.then_inc(s_ytp, 1)

        @block.vector
        def _(dve):
            n = [0]

            def link(ins):
                n[0] += 1
                ins.then_inc(s_dve, 1)
                dve.wait_ge(s_dve, n[0])

            tt, ts, stt = nc.vector.tensor_tensor, nc.vector.tensor_scalar, nc.vector.scalar_tensor_tensor

            dve.wait_ge(s_edges, 32)
            nc.vector.tensor_copy(ef[0:NC, 0, :], ei[0:NC, 0, :])
            link(nc.vector.tensor_copy(ef[0:NC, 1, :], ei[0:NC, 1, :]))
            link(ts(eg[0:NC, :], ef[0:NC, 1, :], float(HALF), None, ALU.is_ge))
            ts(ef[0:NC, 2, :], eg[0:NC, :], PACK - 1.0, 1.0, ALU.mult, ALU.add)
            link(stt(ef[0:NC, 1, :], eg[0:NC, :], -float(HALF), ef[0:NC, 1, :], ALU.mult, ALU.add))
            dve.wait_ge(s_iota, 2)
            nc.vector.tensor_copy(thr[:, :], thr_i[:, :])
            link(nc.vector.tensor_copy(iota[:, :], iota_i[:, :]))
            dve.wait_ge(s_rev, 1)
            nc.vector.tensor_copy(rev[:, :, :].rearrange("p c n -> p (c n)"), rev_i[:, 0:NCH * 64])

            def onehot(tile, j):
                nc.vector.tensor_scalar(S[0:NC, j, :], iota[0:NC, :], ef[0:NC, 0, bass.ds(tile, 1)], None, ALU.is_equal)
                ts(D[0:NC, j, 0:HALF + 1], iota[0:NC, 0:HALF + 1], ef[0:NC, 1, bass.ds(tile, 1)], ef[0:NC, 2, bass.ds(tile, 1)],
                   ALU.is_equal, ALU.mult).then_inc(s_onehot, 1)

            for j in range(RING):
                onehot(j, j)
            with dve.Fori(0, ET // RING - 1) as g:
                for j in range(RING):
                    dve.wait_ge(s_used, g * RING + j + 1)
                    onehot(g * RING + RING + j, j)

            ln_no = [0]

            def norm(chunk_ready=None):
                for c in range(NCH):
                    if chunk_ready:
                        chunk_ready(c)
                    last = nc.vector.bn_stats(stats[0:NC, c, :], xs[0:NC, c, :])
                link(last)
                for c in range(NCH):
                    last = nc.vector.bn_aggr(mv[0:NC, c, :], stats[0:NC, c, :])
                link(last)
                ts(rstd[0:NC, :], mv[0:NC, :, 1], EPS, None, ALU.add).then_inc(s_var, 1)
                ln_no[0] += 1
                dve.wait_ge(s_std, ln_no[0])
                link(nc.vector.reciprocal(rstd[0:NC, :], rstd[0:NC, :]))
                for c in range(NCH):
                    last = ts(xn[0:NC, c, :], xs[0:NC, c, :], mv[0:NC, c, 0:1], rstd[0:NC, c:c + 1], ALU.subtract, ALU.mult)
                last.then_inc(s_ln, 1)

            dve.wait_ge(s_x, 32)
            dve.wait_ge(s_yz, 16)
            norm()
            for i, (a, b) in enumerate(HALVES):
                dve.wait_ge(s_sq, i + 1)
                nc.vector.reciprocal(dis_r[:, a:b], dis_r[:, a:b]).then_inc(s_dis, 1)
            dve.wait_ge(s_dcp, 1)
            nc.vector.tensor_copy(dis_c[0:NC, :], P[0:NC, 7, 400:400 + NCH]).then_inc(s_disc, 1)
            dve.wait_ge(s_disc, 1)
            for c in range(NCH):
                stt(C[0:NC, c, 0:N_NODES], C[0:NC, c, 0:N_NODES], dis_c[0:NC, c:c + 1], dis_r[0:NC, 0:N_NODES],
                    ALU.mult, ALU.mult).then_inc(s_A, 1)

            dve.wait_ge(s_xb, 1)

            def x1_chunk(c):
                dve.wait_ge(s_lin, c + 1)
                tt(xs[0:NC, c, :], xs[0:NC, c, :], P[0:NC, c, :], ALU.add).then_inc(s_x1, 1)
                dve.wait_ge(s_x1, c + 1)

            norm(x1_chunk)
            dve.wait_ge(s_ln, 2)

            gt, mx, t1 = sv(0, NCH, 64), sv(320, 4 * NCH), sv(340, 4 * NCH)
            m3, madd, msub, act2, nadd = sv(380, NCH, 3), sv(400, NCH), sv(405, NCH), sv(410, NCH), sv(415, NCH)
            stt(gt[0:NC], xn[0:NC, :, 16:80], 0.5, rev[0:NC, :, :], ALU.is_gt, ALU.mult)
            ts(m3[0:NC], xn[0:NC, :, 0:3], 0.5, None, ALU.is_gt)
            nc.vector.memset(feat[0:NC, :, 4, :], 1.0)
            link(nc.vector.tensor_copy(feat[0:NC, :, 2:4, :], xn[0:NC, :, 105:107].unsqueeze(3).to_broadcast([NC, NCH, 2, 2])))
            link(nc.vector.tensor_reduce(mx[0:NC, :], gt[0:NC].rearrange("p c (g n) -> p (c g) n", n=16), AX.X, ALU.max))
            link(ts(t1[0:NC, :], mx[0:NC, :], -1.0, 16.0, ALU.mult, ALU.add))
            stt(feat[0:NC, :, 0:2, :].rearrange("p c f s -> p c (f s)"), mx[0:NC, :].rearrange("p (c g) -> p c g", g=4), 0.0,
                t1[0:NC, :].rearrange("p (c g) -> p c g", g=4), ALU.is_gt, ALU.mult).then_inc(s_feat, 1)
            link(tt(madd[0:NC, :], m3[0:NC, :, 0], m3[0:NC, :, 1], ALU.mult))
            link(tt(nadd[0:NC, :], m3[0:NC, :, 0], madd[0:NC, :], ALU.subtract))
            link(tt(msub[0:NC, :], nadd[0:NC, :], m3[0:NC, :, 2], ALU.mult))
            link(tt(act2[0:NC, :], madd[0:NC, :], msub[0:NC, :], ALU.add))
            dve.wait_ge(s_fT, 1)
            nc.vector.tensor_copy(fT[0:2 * NF, 0:4 * NC], P[0:2 * NF, 0, 0:4 * NC])
            nc.vector.tensor_copy(fT[0:2 * NF, 4 * NC:N_NODES], P[0:2 * NF, 1, 0:NC]).then_inc(s_fTc, 1)
            dve.wait_ge(s_ffnw, 16 * 11)
            for g in range(0, 32, 2):
                layer, q, s, m, dst_ap, a, b = ffn_group(g)
                dve.wait_ge(s_fm, g + 1)
                ts(dst_ap, P[0:GH, g % 8, 0:b - a], bf_c[0:GH, q, m:m + 1] if layer else 0.0, 0.0, ALU.add, ALU.max).then_inc(s_fd, 1)
            y3, ya, ys, ysel = sv(420, 2, NCH * 2, 2), sv(460, NCH, 4), sv(480, NCH, 4), sv(500, NCH, 4)
            res, oh, car = sv(520, NCH, 2), sv(540, NCH * 2, 16), sv(700, NCH)
            dve.wait_ge(s_y3, 1)
            link(tt(y3[0:NC], P[0:NC, 0, 0:8 * NCH].rearrange("p (q n r) -> p q n r", q=2, r=2),
                    b3_b[0:NC, :, :].unsqueeze(2).to_broadcast([NC, 2, NCH * 2, 2]), ALU.add))
            tt(ya[0:NC], y3[0:NC, 0].rearrange("p (c s) r -> p c (s r)", s=2), madd[0:NC, :].unsqueeze(2).to_broadcast([NC, NCH, 4]), ALU.mult)
            link(tt(ys[0:NC], y3[0:NC, 1].rearrange("p (c s) r -> p c (s r)", s=2), msub[0:NC, :].unsqueeze(2).to_broadcast([NC, NCH, 4]), ALU.mult))
            link(tt(ysel[0:NC], ya[0:NC], ys[0:NC], ALU.add))
            link(ts(res[0:NC], ysel[0:NC].rearrange("p c (s r) -> p c s r", s=2)[:, :, :, 0], 0.0, 15.0, ALU.max, ALU.min))
            link(ts(res[0:NC], res[0:NC], ROUND, None, ALU.add))
            link(ts(res[0:NC], res[0:NC], -ROUND, None, ALU.add))
            stt(car[0:NC, :], ysel[0:NC, :, 3], 0.5, act2[0:NC, :], ALU.is_gt, ALU.mult)
            link(ts(act2[0:NC, :], act2[0:NC, :], 2.0, None, ALU.mult))
            link(tt(oh[0:NC], iota[0:NC, 0:16].unsqueeze(1).to_broadcast([NC, NCH * 2, 16]),
                    res[0:NC].rearrange("p c s -> p (c s)").unsqueeze(2).to_broadcast([NC, NCH * 2, 16]), ALU.is_equal))
            link(tt(oh[0:NC].rearrange("p (c s) n -> p c (s n)", s=2), oh[0:NC].rearrange("p (c s) n -> p c (s n)", s=2),
                    act2[0:NC, :].unsqueeze(2).to_broadcast([NC, NCH, 32]), ALU.mult))
            dve.wait_ge(s_xsum, 1)
            tt(xs[0:NC, :, 128:160], xs[0:NC, :, 128:160], oh[0:NC].rearrange("p (c s) n -> p c (s n)", s=2), ALU.add)
            link(tt(xs[0:NC, :, 160:161], xs[0:NC, :, 160:161], car[0:NC, :].unsqueeze(2), ALU.add))
            norm()

            with dve.Fori(0, 3) as l:
                for c in range(NCH):
                    dve.wait_ge(s_gh, l * NCH + c + 1)
                    nc.vector.tensor_copy(Hn[0:NC, c, :], P[0:NC, c, :]).then_inc(s_ghc, 1)
            dve.wait_ge(s_bg2, 16)

            def x3_chunk(c):
                dve.wait_ge(s_ga, 4 * KD + c + 1)
                link(tt(xn[0:NC, c, :], P[0:NC, (5 + c) % 8, :], bg2_b[0:NC, :], ALU.add))
                stt(xs[0:NC, c, :], xn[0:NC, c, :], 0.0, xs[0:NC, c, :], ALU.max, ALU.add).then_inc(s_x3, 1)
                dve.wait_ge(s_x3, c + 1)

            norm(x3_chunk)

            bits = sv(0, NCH, 15)
            level = [None, sv(80, NCH, 2), sv(90, NCH, 4), sv(110, NCH, 8), leaf]
            dve.wait_ge(s_lg, 1)
            dve.wait_ge(s_cols, 16 * 4)
            link(tt(bits[0:NC], P[0:NC, 7, 0:NCH * 15].rearrange("p (c n) -> p c n", n=15),
                    br_b[0:NC, :].unsqueeze(1).to_broadcast([NC, NCH, 15]), ALU.add))
            link(ts(bits[0:NC], bits[0:NC], 0.0, None, ALU.is_gt))
            for d in range(4):
                w = 2 ** d
                right = level[d + 1][0:NC].rearrange("p c (j t) -> p c j t", t=2)
                here = bits[0:NC, :, w - 1:2 * w - 1]
                if d == 0:
                    nc.vector.tensor_copy(right[:, :, :, 1], here)
                    link(ts(right[:, :, :, 0], here, -1.0, 1.0, ALU.mult, ALU.add))
                else:
                    link(tt(right[:, :, :, 1], level[d][0:NC], here, ALU.mult))
                    link(tt(right[:, :, :, 0], level[d][0:NC], right[:, :, :, 1], ALU.subtract))
            nc.vector.tensor_copy(oh16[0:NC], leaf[0:NC]).then_inc(s_oh, 1)

            cmp, extra, cum, cumx = sv(290, NE, MORE), sv(402, NE), sv(418, NE), sv(434, NE)
            pick, rk, ce, le, ge, key = sv(450, NCH, NE), sv(530, NCH), sv(535, NCH), sv(540, NCH), sv(545, NCH), sv(550, NCH)
            cmpq, eid, more = sv(560, TAB - NE, NE), sv(690, TAB), sv(720, 5)
            dve.wait_ge(s_rank, 1)
            link(nc.vector.tensor_copy(cum[0:NC, :], P[0:NC, 6, 128:128 + NE]))
            link(tt(cmp[0:NC], cum[0:NC, :].unsqueeze(2).to_broadcast([NC, NE, MORE]),
                    thr[0:NC, 0:MORE].unsqueeze(1).to_broadcast([NC, NE, MORE]), ALU.is_gt))
            link(nc.vector.tensor_reduce(extra[0:NC, :], cmp[0:NC], AX.X, ALU.add))
            link(nc.vector.tensor_tensor_scan(cum[0:NC, :], ones[0:NC, 0:NE], extra[0:NC, :], 0.0, ALU.mult, ALU.add))
            link(stt(cumx[0:NC, :], cum[0:NC, :], float(NE - 1), extra[0:NC, :], ALU.add, ALU.subtract))

            def picked(to, values):
                link(tt(pick[0:NC], leaf[0:NC], values, ALU.mult))
                link(nc.vector.tensor_reduce(to[0:NC, :], pick[0:NC], AX.X, ALU.add))

            picked(rk, P[0:NC, 6, 0:NCH * NE].rearrange("p (c e) -> p c e", e=NE))
            picked(ce, cumx[0:NC, :].unsqueeze(1).to_broadcast([NC, NCH, NE]))
            picked(le, iota[0:NC, 0:NE].unsqueeze(1).to_broadcast([NC, NCH, NE]))
            link(tt(ce[0:NC, :], ce[0:NC, :], le[0:NC, :], ALU.subtract))
            link(stt(ge[0:NC, :], rk[0:NC, :], float(SLOTS), ce[0:NC, :], ALU.is_ge, ALU.mult))
            link(tt(ge[0:NC, :], ge[0:NC, :], le[0:NC, :], ALU.add))
            link(stt(keyrel[0:NC, :], ge[0:NC, :], float(SLOTS), rk[0:NC, :], ALU.mult, ALU.add))
            nc.vector.tensor_copy(gidx[0:NC, :], keyrel[0:NC, :])
            nc.vector.tensor_copy(eid[0:1, 0:NE], iota[0:1, 0:NE])
            link(tt(cmpq[0:1], cum[0:1, :].unsqueeze(1).to_broadcast([1, TAB - NE, NE]),
                    iota[0:1, 0:TAB - NE].unsqueeze(2).to_broadcast([1, TAB - NE, NE]), ALU.is_le))
            link(nc.vector.tensor_reduce(eid[0:1, NE:TAB], cmpq[0:1], AX.X, ALU.add))
            ts(tab[0:1, :], eid[0:1, :], float(NE - 1), None, ALU.min)
            link(ts(more[0:1, 0:4], iota[0:1, 0:4], 2.0, cum[0:1, NE - 1:NE], ALU.mult, ALU.is_lt))
            link(nc.vector.tensor_reduce(more[0:1, 4:5], more[0:1, 0:4], AX.X, ALU.add))
            ts(npairs_t[0:1, :], more[0:1, 4:5], float(NE // 2), None, ALU.add).then_inc(s_table, 1)

            def dispatch_onehot(i, b):
                tt(disp[b][0:NC], iota[0:NC, 0:SLOTS].unsqueeze(1).to_broadcast([NC, NCH, SLOTS]),
                   keyrel[0:NC, :].unsqueeze(2).to_broadcast([NC, NCH, SLOTS]), ALU.is_equal).then_inc(s_P, 1)
                dve.wait_ge(s_P, i + 1)
                ts(keyrel[0:NC, :], keyrel[0:NC, :], -float(SLOTS), None, ALU.add).then_inc(s_ech, 1)

            def copy_inputs(i, b):
                dve.wait_ge(s_xe, i + 1)
                nc.vector.tensor_copy(xe[b], P[:, 2, 0:KD * SLOTS].rearrange("p (k s) -> p k s", k=KD)).then_inc(s_xec, 1)

            def copy_bias(i, b):
                dve.wait_ge(s_bT, i + 1)
                nc.vector.tensor_copy(bT[b], P[:, 2, KD * SLOTS:KD * SLOTS + NB]).then_inc(s_bTc, 1)

            dispatch_onehot(0, 0)
            copy_inputs(0, 0)
            copy_bias(0, 0)
            dve.wait_ge(s_table, 1)
            pairs = dve.value_load(npairs_t[0:1, 0:1], min_val=NE // 2, max_val=MAX_PAIRS)
            with dve.Fori(0, pairs) as p:
                for b in range(2):
                    i = 2 * p + b
                    dve.wait_ge(s_ech, i + 1)
                    dispatch_onehot(i + 1, 1 - b)
                    copy_inputs(i + 1, 1 - b)
                    dve.wait_ge(s_l2, i + 1)
                    dve.wait_ge(s_bTc, i + 1)
                    tt(yT[b], P[:, 3:3 + KD, 0:SLOTS], bT[b][:, MH:NB].unsqueeze(2).to_broadcast([128, KD, SLOTS]),
                       ALU.add).then_inc(s_yT, 1)
                    copy_bias(i + 1, 1 - b)
            for c in range(NCH):
                dve.wait_ge(s_gat[c], 16)
                tt(xs[0:NC, c, :], xs[0:NC, c, :], xn[0:NC, c, :], ALU.add).then_inc(s_fin, 1)


_INS = ["x", "src", "dst", "L0_gnn_W_conv", "L0_gnn_b_conv", "L0_gnn_W_lin", "L0_gnn_b_lin", "L0_ffn_Wa", "L0_ffn_ba",
        "L0_ffn_Ws", "L0_ffn_bs", "L1_gnn_W", "L1_gnn_b", "L1_ffn_Wr", "L1_ffn_br", "L1_ffn_W1", "L1_ffn_b1",
        "L1_ffn_W2", "L1_ffn_b2"]


def kernel(**inputs):
    import numpy as _np
    import concourse.bacc as _bacc
    from concourse import mybir as _mybir
    from concourse.bass_utils import run_bass_kernel_spmd as _run

    nc = _bacc.Bacc("TRN2", target_bir_lowering=False, num_devices=1)
    arrays, args = {}, []
    for name in _INS:
        a = _np.ascontiguousarray(inputs[name])
        arrays[f"in_{name}"] = a
        args.append(nc.dram_tensor(f"in_{name}", a.shape, _mybir.dt.from_np(a.dtype), kind="ExternalInput").ap())
    args.append(nc.dram_tensor("out_0", (N_NODES, DIM), _mybir.dt.float32, kind="ExternalOutput").ap())
    build(nc, *args)
    r = _run(nc, [arrays], core_ids=[0])
    return r.results[0]["out_0"]
```

```python
from contextlib import ExitStack

import numpy as np
import concourse.bass as bass
from concourse import mybir

F32 = mybir.dt.float32
BF16 = mybir.dt.bfloat16
F16 = mybir.dt.float16
I32 = mybir.dt.int32
U32 = mybir.dt.uint32
ALU = mybir.AluOpType
ACT = mybir.ActivationFunctionType
AX = mybir.AxisListType

N_NODES, DIM, N_EDGES = 625, 512, 20000
NCH = 5
NC = N_NODES // NCH
KD = DIM // 128
HALF = (N_NODES + 1) // 2
NPAD = 2 * HALF
HALVES = ((0, HALF), (HALF, N_NODES))
EPS = 1e-5

ET = N_EDGES // NC
RUNS = 5
RUN_TILES = ET // RUNS
RING = 4
GROUPS = RUN_TILES // RING
PACK = 4096.0
HIGH_BIAS = RUN_TILES * NC / 2 / PACK

GE = 160
GH = GE // 2
NF = 5
RESULT = 100

NE, HID = 16, 2048
MH = HID // 128
SA, SB_ = 64, 32
SLOTS = SA + SB_
MORE = (N_NODES - 1) // SLOTS
MAX_PAIRS = NE // 2 + -(-MORE // 2)
TAB = 2 * MAX_PAIRS
ROUND = 12582912.0


def build(nc, x, src, dst, Wconv, bconv, Wlin, blin, Wa, ba, Ws, bs, Wg, bg, Wr, br, W1, b1, W2, b2, out):
    ctx = ExitStack()
    with ctx:
        ctx.enter_context(nc.allow_non_contiguous_dma(reason="small bias columns"))

        def sb(name, shape, dt=F32):
            return ctx.enter_context(nc.sbuf_tensor(name, shape, dt))

        def sem(name):
            return ctx.enter_context(nc.semaphore(name))

        w1_sb = [sb(f"w1_{b}", [128, KD, HID]) for b in range(2)]
        w2_sb = [sb(f"w2_{b}", [128, MH, DIM]) for b in range(2)]
        xs = sb("xs", [128, NCH, DIM])
        xn = sb("xn", [128, NCH, DIM])
        XT = sb("XT", [128, 4 * NPAD])
        H = sb("H", [128, NCH * DIM])
        FB = sb("FB", [128, 4 * NPAD])
        C = sb("C", [128, NCH, NPAD])
        G = sb("G", [128, KD * DIM])
        ident = sb("ident", [128, 128])
        ones = sb("ones", [128, 128])
        ones16 = sb("ones16", [128, 128], BF16)
        tri16 = sb("tri16", [128, 128], BF16)
        iota_i = FB[:, 0:NPAD].bitcast(I32)
        rev_i = FB[:, NPAD:NPAD + NCH * 64].bitcast(I32)
        iota = sb("iota", [128, NPAD], F16)
        rev = sb("rev", [128, NCH, 64], F16)
        stats = sb("stats", [128, NCH, 6])
        mv = sb("mv", [128, NCH, 2])
        rstd = sb("rstd", [128, NCH])
        bconv_c = sb("bconv_c", [128, 1])
        bg_c = sb("bg_c", [128, 2, KD])
        bf_c = sb("bf_c", [128, 2, 2])
        b3_b = sb("b3_b", [128, 2, 2])
        br_b = sb("br_b", [128, 15])
        wr_T = sb("wr_T", [128, KD, 15])
        dis_c = sb("dis_c", [128, NCH])
        w3_T = sb("w3_T", [128, 2, 2, 2])
        feat = sb("feat", [128, NCH, NF, 2])
        small = sb("small", [128, 728])
        gidx = sb("gidx", [128, NCH], U32)
        tab = sb("tab", [1, TAB], I32)
        npairs_t = sb("npairs_t", [1, 1], I32)
        thr_i = sb("thr_i", [128, 16], I32)
        thr = sb("thr", [128, 16])
        lidx = sb("lidx", [128, NCH], U32)
        P = ctx.enter_context(nc.psum_tensor("P", [128, 8, 512], F32))

        S = H[:, 0:RING * HALF].bitcast(BF16).rearrange("p (r n) -> p r n", r=RING)
        D = H[:, 1252:1252 + RING * 157].bitcast(BF16).rearrange("p (r n) -> p r n", r=RING)
        v_sb = FB[:, 0:NCH * HALF].rearrange("p (m n) -> p m n", m=NCH)
        hi_sb = G[:, 0:3 * HALF].rearrange("p (m n) -> p m n", m=3)
        wconv = H[:, 1880:1880 + DIM].rearrange("p (k n) -> p k n", k=KD)
        h0 = FB[:, 1764:1764 + NCH * 128].rearrange("p (c n) -> p c n", c=NCH)
        ei = G[:, 0:2 * ET].bitcast(I32).rearrange("p (s t) -> p s t", s=2)
        blin_b = H[:, 640:640 + DIM]
        ef = small[:, 0:3 * ET].rearrange("p (s t) -> p s t", s=3)
        eg = small[:, 3 * ET:4 * ET]
        dis_r = FB[:, 0:NPAD]
        XTn = XT[:, :].rearrange("p (k n) -> p k n", k=KD)
        FBn = FB[:, :].rearrange("p (k n) -> p k n", k=KD)
        Hn = H[:, :].rearrange("p (c n) -> p c n", c=NCH)
        Gw = G[:, :].rearrange("p (k n) -> p k n", k=KD)
        wlin = XT[:, 0:DIM]
        wnat = XT[:, 640:640 + 4 * GE].rearrange("p (q m i) -> p q m i", q=2, m=2)
        wmid = sb("wmid", [128, 2, 2, GE])
        win = G[:, 1024:1024 + 4 * GE].rearrange("p (q s o) -> p q s o", q=2, s=2)
        fT = G[:, 0:N_NODES]
        hid1 = [XT, H]
        hid2 = [FB, XT]

        agg0 = H[:, 0:N_NODES]

        def ffn_group(g):
            layer, q, s, m, h = g // 16, g // 8 % 2, g // 4 % 2, g // 2 % 2, g % 2
            a, b = HALVES[h]
            dst_ap = ffn_view((hid2 if layer else hid1)[q])[0:GH, m, s, a:b]
            return layer, q, m, s, dst_ap, a, b

        def ffn_view(t):
            return t[:, 0:4 * N_NODES].rearrange("p (m s n) -> p m s n", m=2, s=2)

        bg2_b = FB[:, 0:DIM]
        wr_nat = XT[0:15, 1280:1280 + DIM]
        h_sb = H[:, 0:3 * DIM].rearrange("p (t n) -> p t n", t=3)
        xT = [H[:, 1536 + b * KD * SLOTS:1536 + (b + 1) * KD * SLOTS].rearrange("p (k s) -> p k s", k=KD) for b in range(2)]
        hT = FB[:, 0:MH * SLOTS].rearrange("p (m s) -> p m s", m=MH)
        xr = [XT[0:SLOTS, b * DIM:(b + 1) * DIM] for b in range(2)]
        y_sb = [XT[:, 1024 + b * 384:1024 + (b + 1) * 384] for b in range(2)]
        b1_nat = G[:, 0:256].rearrange("p (h n) -> p h n", h=2)
        b1T = G[:, 256:512]
        bT = [G[:, 512 + b * MH:512 + (b + 1) * MH] for b in range(2)]
        b2g = C[0:NC, :, 0:DIM]
        x_dram = nc.dram_tensor("x_rows", [(TAB + 1) * SLOTS, DIM], F32, kind="Internal").ap()
        y_dram = nc.dram_tensor("y_rows", [TAB * SLOTS, DIM], F32, kind="Internal").ap()

        def sv(at, *dims):
            n = int(np.prod(dims))
            v = small[:, at:at + n]
            names = " ".join(f"d{i}" for i in range(len(dims)))
            if len(dims) > 1:
                v = v.rearrange(f"p ({names}) -> p {names}", **{f"d{i}": d for i, d in enumerate(dims)})
            return v

        leaf = sv(150, NCH, NE)
        oh16 = small[:, 230:230 + NCH * NE // 2].bitcast(BF16).rearrange("p (c e) -> p c e", e=NE)

        s_edges, s_x, s_wconv, s_blin, s_cols = (sem(n) for n in ("edges_in", "x_in", "wconv_in", "blin_in", "cols_in"))
        s_wlin, s_ffnw, s_win, s_gw, s_bg2 = (sem(n) for n in ("wlin_in", "ffnw_in", "win_in", "gnnw_in", "bg2_in"))
        s_w1 = [sem(f"w1_in{b}") for b in range(2)]
        s_w2 = [[sem(f"w2_in{b}_{q}") for q in range(4)] for b in range(2)]
        s_xr = [sem(f"tile_rows_in{b}") for b in range(2)]
        s_iota, s_ident, s_rev, s_ones, s_c0, s_winz, s_xb = (sem(n) for n in
            ("iota_ready", "ident_ready", "rev_ready", "ones_ready", "counts_cleared", "win_cleared", "x_plus_blin"))
        s_pool = sem("pool_chain")
        s_zero, s_yz = sem("zeros_ready"), sem("zeros_stored")
        s_dve = sem("dve_chain")
        s_act = sem("act_chain")
        s_var, s_std, s_ln = sem("var_ready"), sem("std_ready"), sem("layernorm_ready")
        s_tp, s_tpc = sem("transposed"), sem("transposed_copied")
        s_h0, s_h0c = sem("h0_ready"), sem("h0_copied")
        s_onehot, s_used = sem("onehot_ready"), sem("onehot_used")
        s_cnt, s_cntc, s_high, s_acc = (sem(n) for n in ("count_bank_done", "count_bank_free", "count_high_ready", "count_added"))
        s_deg, s_sq, s_dis, s_disc, s_A = (sem(n) for n in ("degree_ready", "sqrt_degree_ready", "dis_ready", "dis_col", "adjacency_ready"))
        s_dcp = sem("dis_col_product")
        s_agg0, s_agg0c, s_lin, s_x1 = sem("agg0_ready"), sem("agg0_copied"), sem("lin_ready"), sem("x1_ready")
        s_feat, s_fT, s_fTc, s_wmid, s_wmidc = (sem(n) for n in ("feat_ready", "featT", "featT_copied", "wmid_T", "wmid_copied"))
        s_fm, s_fd, s_fa, s_y3 = sem("ffn_mm"), sem("ffn_dve_copied"), sem("ffn_act_copied"), sem("ffn_out_ready")
        s_xsum = sem("x1_plus_norm")
        s_gh, s_ghc, s_ga, s_gac, s_x3 = (sem(n) for n in ("gnn_h", "gnn_h_copied", "gnn_agg", "gnn_agg_copied", "x3_ready"))
        s_wrT, s_wrTc, s_lg, s_oh, s_rank, s_table = (sem(n) for n in ("wr_T", "wr_T_copied", "logits", "onehot16", "ranks", "table_ready"))
        s_scat, s_b2g, s_b1, s_b1T, s_b1Tc, s_x3b = (sem(n) for n in
            ("rows_scattered", "b2_gathered", "b1_in", "b1_transposed", "b1_copied", "x3_plus_b2"))
        s_xT, s_xTc = sem("tile_transposed"), sem("tile_copied")
        s_h, s_hc, s_hT, s_gelu, s_l2 = (sem(n) for n in ("hidden_bank", "hidden_copied", "hidden_transposed", "gelu_done", "expert_out"))
        s_bTc, s_ycp = sem("tile_bias_copied"), sem("y_copied")
        s_yst = [sem(f"y_stored{b}") for b in range(2)]
        s_gat, s_fin, s_out, s_stored = [sem(f"y_gathered{c}") for c in range(NCH)], sem("final_ready"), sem("out_stored"), sem("all_tiles_stored")

        block = ctx.enter_context(nc.Block())

        def rows16(n):
            return ((0, n // 16 * 16), (n // 16 * 16, n))

        n_zero = [0]

        @block.sync
        def _(sp):
            sp.dma_start(ei[0:NC, 1, :], dst.rearrange("(p t) -> p t", t=ET)).then_inc(s_edges, 16)
            sp.dma_start(ei[0:NC, 0, :], src.rearrange("(p t) -> p t", t=ET)).then_inc(s_edges, 16)
            xv = x.rearrange("(c p) d -> p c d", p=NC)
            for a, b in rows16(NC):
                sp.dma_start(xs[a:b, :, :], xv[a:b]).then_inc(s_x, 16)
            sp.dma_start(wconv, Wconv.rearrange("(k p) n -> p k n", p=128)).then_inc(s_wconv, 16)
            sp.wait_ge(s_zero, 1)
            blk = SLOTS * NCH
            for rows, first in ((x_dram, 0), (y_dram, NE * SLOTS)):
                for at in range(first, rows.shape[0], blk):
                    k = min(blk, rows.shape[0] - at) // SLOTS
                    sp.dma_start(rows[at:at + k * SLOTS, :].rearrange("(p c) n -> p c n", p=SLOTS), xn[0:SLOTS, 0:k, :]).then_inc(s_yz, 16)
                    n_zero[0] += 16
            sp.dma_start(bconv_c[:, :], bconv.rearrange("(p a) -> p a", a=1)).then_inc(s_cols, 16)
            for l in range(2):
                sp.dma_start(bg_c[:, l, :], bg[l, :].rearrange("(k p) -> p k", p=128)).then_inc(s_cols, 16)
            sp.dma_start(br_b[0:NC, :], br.rearrange("(a n) -> a n", a=1).to_broadcast([NC, 15])).then_inc(s_cols, 16)
            for q, (w, b) in enumerate(((Wa, ba), (Ws, bs))):
                sp.dma_start(wnat[0:GH, q, :, :], w[1].rearrange("(m p) i -> p m i", p=GH)).then_inc(s_ffnw, 16)
                sp.dma_start(bf_c[0:GH, q, :], b[1, :].rearrange("(m p) -> p m", p=GH)).then_inc(s_ffnw, 16)
                sp.dma_start(b3_b[0:NC, q, :], b[2:3, RESULT:RESULT + 2].to_broadcast([NC, 2])).then_inc(s_ffnw, 16)
                for r in range(2):
                    sp.dma_start(w3_T[0:GH, q, :, r], w[2, RESULT + r, :].rearrange("(m p) -> p m", p=GH)).then_inc(s_ffnw, 16)
            sp.dma_start(wr_nat, Wr).then_inc(s_ffnw, 16)
            for b in range(2):
                for k in range(KD):
                    sp.dma_start(w1_sb[b][:, k, :], W1[b, k * 128:(k + 1) * 128, :]).then_inc(s_w1[b], 16)
                for q in range(4):
                    sp.dma_start(w2_sb[b][:, 4 * q:4 * q + 4, :],
                                 W2[b, q * DIM:(q + 1) * DIM, :].rearrange("(m p) n -> p m n", p=128)).then_inc(s_w2[b][q], 16)
            sp.wait_ge(s_used, ET)
            sp.dma_start(blin_b[0:NC, :], blin.rearrange("(a n) -> a n", a=1).to_broadcast([NC, DIM])).then_inc(s_blin, 16)
            sp.wait_ge(s_h0, 2)
            sp.dma_start(wlin, Wlin).then_inc(s_wlin, 16)
            sp.wait_ge(s_winz, 1)
            for q, (w, b) in enumerate(((Wa, ba), (Ws, bs))):
                for s in range(2):
                    for f0, i0 in ((0, 0), (2, 35)):
                        for f in range(2):
                            r = 2 * (f0 + f) + s
                            sp.dma_start(win[r:r + 1, q, s, :], w[0, :, i0 + f:i0 + f + 1].rearrange("o a -> a o")).then_inc(s_win, 16)
                    sp.dma_start(win[8 + s:9 + s, q, s, :], b[0:1, :]).then_inc(s_win, 16)
            sp.wait_ge(s_y3, 1)
            for l in range(3):
                if l:
                    sp.wait_ge(s_gh, NCH * l)
                sp.dma_start(Gw, Wg[l].rearrange("(k p) n -> p k n", p=128)).then_inc(s_gw, 16)
                if l == 0:
                    sp.dma_start(bg2_b[0:NC, :], bg[2:3, :].to_broadcast([NC, DIM])).then_inc(s_bg2, 16)
            sp.wait_ge(s_gh, NCH * 3)
            sp.dma_start(b1_nat, b1.rearrange("e (m p) -> (e m) p", p=128).rearrange("(h r) p -> r h p", h=2)).then_inc(s_b1, 16)

            def load_rows(b, i):
                sp.dma_start(xr[b], x_dram[bass.ds(i * SLOTS, SLOTS), :]).then_inc(s_xr[b], 16)

            sp.wait_ge(s_scat, 16 * NCH)
            load_rows(0, 0)
            load_rows(1, 1)
            sp.wait_ge(s_xT, 1)
            load_rows(0, 2)
            pairs = sp.value_load(npairs_t[0:1, 0:1], min_val=NE // 2, max_val=MAX_PAIRS)
            with sp.Fori(0, pairs - 1) as p:
                for b in range(2):
                    done = 2 * p + b + 1
                    e = sp.value_load(tab[0:1, bass.ds(done + 1, 1)], min_val=0, max_val=NE - 1)
                    sp.wait_ge(s_h, done * 3)
                    for k in range(KD):
                        sp.dma_start(w1_sb[b][:, k, :], W1[bass.ds(e, 1), k * 128:(k + 1) * 128, :].rearrange("a p n -> (a p) n")).then_inc(s_w1[b], 16)
                    sp.wait_ge(s_xT, done + 1)
                    load_rows(1 - b, done + 2)
                    sp.wait_ge(s_l2, done)
                    for q in range(4):
                        sp.dma_start(w2_sb[b][:, 4 * q:4 * q + 4, :],
                                     W2[bass.ds(e, 1), q * DIM:(q + 1) * DIM, :].rearrange("a (m p) n -> p (a m) n", p=128)).then_inc(s_w2[b][q], 16)
            for c in range(NCH):
                sp.wait_ge(s_fin, c + 1)
                for i, (a, b) in enumerate(rows16(NC)):
                    sp.dma_start(out[c * NC + a:c * NC + b, :], xs[a:b, c, :]).then_inc(s_out, 16)
            sp.wait_ge(s_out, 16 * 2 * NCH)

        @block.gpsimd
        def _(pool):
            n = [0]

            def link(ins):
                n[0] += 1
                ins.then_inc(s_pool, 1)
                pool.wait_ge(s_pool, n[0])

            nc.gpsimd.iota(iota_i[:, :], pattern=[[1, NPAD]], base=0, channel_multiplier=0).then_inc(s_iota, 1)
            nc.gpsimd.iota(rev_i, pattern=[[0, NCH * 4], [-1, 16]], base=16, channel_multiplier=0).then_inc(s_rev, 1)
            nc.gpsimd.memset(xn[:, :, :], 0.0).then_inc(s_zero, 1)
            link(nc.gpsimd.memset(ident[:, :], 0.0))
            nc.gpsimd.affine_select(out=ident[:, :], in_=ident[:, :], compare_op=ALU.not_equal, fill=1.0, base=0,
                                    pattern=[[-1, 128]], channel_multiplier=1).then_inc(s_ident, 1)
            nc.gpsimd.iota(thr_i[:, :], pattern=[[SLOTS, 16]], base=SLOTS, channel_multiplier=0).then_inc(s_iota, 1)
            nc.gpsimd.memset(ones16[:, :], 1.0).then_inc(s_ones, 1)
            link(nc.gpsimd.memset(ones[:, :], 1.0))
            nc.gpsimd.affine_select(out=tri16[:, :], in_=ones[:, :], compare_op=ALU.is_gt, fill=0.0, base=0,
                                    pattern=[[1, 128]], channel_multiplier=-1).then_inc(s_ones, 1)
            link(nc.gpsimd.memset(C[:, :, :], 0.0))
            nc.gpsimd.affine_select(out=C[0:NC, :, :], in_=C[0:NC, :, :], compare_op=ALU.not_equal, fill=1.0, base=0,
                                    pattern=[[NC, NCH], [-1, NPAD]], channel_multiplier=1).then_inc(s_c0, 1)
            pool.wait_ge(s_onehot, 1)
            nc.gpsimd.memset(G[:, 1024:1024 + 4 * GE], 0.0).then_inc(s_winz, 1)
            pool.wait_ge(s_c0, 1)
            pool.sem_inc(s_acc, 1)
            n0 = n[0]
            with pool.Fori(0, RUNS) as r:
                for m in range(NCH):
                    step = n0 + (r * NCH + m) * 2
                    v, hi = v_sb[0:NC, m, :], hi_sb[0:NC, m % 3, :]
                    pool.wait_ge(s_high, r * NCH + m + 1)
                    nc.gpsimd.tensor_tensor(C[0:NC, m, HALF:NPAD], C[0:NC, m, HALF:NPAD], hi, ALU.add)
                    nc.gpsimd.tensor_scalar(hi, hi, -PACK, None, ALU.mult).then_inc(s_pool, 1)
                    pool.wait_ge(s_pool, step + 1)
                    nc.gpsimd.tensor_tensor(v, v, hi, ALU.add).then_inc(s_pool, 1)
                    pool.wait_ge(s_pool, step + 2)
                    nc.gpsimd.tensor_tensor(C[0:NC, m, 0:HALF], C[0:NC, m, 0:HALF], v, ALU.add).then_inc(s_acc, 1)
            pool.wait_ge(s_blin, 16)
            pool.wait_ge(s_ln, 1)
            nc.gpsimd.tensor_tensor(xs[0:NC, :, :], xs[0:NC, :, :],
                                    blin_b[0:NC, :].unsqueeze(1).to_broadcast([NC, NCH, DIM]), ALU.add).then_inc(s_xb, 1)
            pool.wait_ge(s_ln, 2)
            nc.gpsimd.tensor_tensor(xs[0:NC, :, :], xs[0:NC, :, :], xn[0:NC, :, :], ALU.add).then_inc(s_xsum, 1)
            pool.wait_ge(s_table, 1)
            for c in range(NCH):
                nc.gpsimd.indirect_dma_start(out=x_dram[:, :], out_offset=bass.IndirectOffsetOnAxis(ap=gidx[0:NC, c:c + 1], axis=0),
                                             in_=xn[0:NC, c, :], in_offset=None).then_inc(s_scat, 16)
            for c in range(NCH):
                nc.gpsimd.indirect_dma_start(out=b2g[:, c, :], out_offset=None, in_=b2,
                                             in_offset=bass.IndirectOffsetOnAxis(ap=lidx[0:NC, c:c + 1], axis=0)).then_inc(s_b2g, 16)
            pool.wait_ge(s_b2g, 16 * NCH)
            nc.gpsimd.tensor_tensor(xs[0:NC, :, :], xs[0:NC, :, :], b2g, ALU.add).then_inc(s_x3b, 1)
            pairs = pool.value_load(npairs_t[0:1, 0:1], min_val=NE // 2, max_val=MAX_PAIRS)
            for b in range(2):
                pool.wait_ge(s_yst[b], 96 * pairs + 96)
            pool.sem_inc(s_stored, 1)
            pool.wait_ge(s_stored, 1)
            for c in range(NCH):
                nc.gpsimd.indirect_dma_start(out=xn[0:NC, c, :], out_offset=None, in_=y_dram[:, :],
                                             in_offset=bass.IndirectOffsetOnAxis(ap=gidx[0:NC, c:c + 1], axis=0)).then_inc(s_gat[c], 16)
            for c in range(NCH):
                pool.wait_ge(s_gat[c], 16)

        @block.scalar
        def _(act):
            ln_no = [0]

            def sqrt_var():
                ln_no[0] += 1
                act.wait_ge(s_var, ln_no[0])
                nc.scalar.activation(rstd[0:NC, :], rstd[0:NC, :], ACT.Sqrt).then_inc(s_std, 1)

            tp_no = [0]

            def copy_transposed():
                for c in range(NCH):
                    tp_no[0] += 1
                    act.wait_ge(s_tp, tp_no[0])
                    nc.scalar.activation(XTn[:, :, c * NC:(c + 1) * NC], P[:, c, 0:KD * NC].rearrange("p (k n) -> p k n", k=KD),
                                         ACT.Copy).then_inc(s_tpc, 1)

            act.sem_inc(s_cntc, NCH)
            with act.Fori(0, RUNS) as r:
                act.wait_ge(s_acc, r * NCH + 1)
                for m in range(NCH):
                    if m < NCH - 1:
                        act.wait_ge(s_cnt, r * (NCH - 1) + m + 1)
                    else:
                        act.wait_ge(s_used, (r + 1) * RUN_TILES)
                    nc.scalar.activation(v_sb[0:NC, m, :], P[0:NC, m, 0:HALF], ACT.Copy).then_inc(s_cntc, 1)
                for m in range(NCH):
                    hi = hi_sb[0:NC, m % 3, :]
                    step = (r * NCH + m) * 2
                    act.wait_ge(s_cntc, r * NCH + NCH + m + 1)
                    if m >= 3:
                        act.wait_ge(s_acc, r * NCH + m - 1)
                    nc.scalar.activation(hi, v_sb[0:NC, m, :], ACT.Copy, bias=-HIGH_BIAS, scale=1.0 / PACK).then_inc(s_act, 1)
                    act.wait_ge(s_act, step + 1)
                    nc.scalar.activation(hi, hi, ACT.Copy, bias=ROUND).then_inc(s_act, 1)
                    act.wait_ge(s_act, step + 2)
                    nc.scalar.activation(hi, hi, ACT.Copy, bias=-ROUND).then_inc(s_high, 1)
            act.wait_ge(s_wmid, 1)
            for q in range(2):
                nc.scalar.activation(wmid[0:GH, q, :, :], P[0:GH, 6 + q, 128:128 + 2 * GE].rearrange("p (k o) -> p k o", k=2),
                                     ACT.Copy).then_inc(s_wmidc, 1)
            nc.scalar.activation(wr_T[:, :, :], P[:, 7, 0:KD * 15].rearrange("p (k o) -> p k o", k=KD), ACT.Copy).then_inc(s_wmidc, 1)
            sqrt_var()
            copy_transposed()
            act.wait_ge(s_h0, 1)
            nc.scalar.activation(h0[0:NC, 0:4, :], P[0:NC, 5, :].rearrange("p (c n) -> p c n", c=4), ACT.Copy).then_inc(s_h0c, 1)
            act.wait_ge(s_h0, 2)
            nc.scalar.activation(h0[0:NC, 4, :], P[0:NC, 6, 0:128], ACT.Copy).then_inc(s_h0c, 1)
            for i, (a, b) in enumerate(HALVES):
                act.wait_ge(s_deg, i + 1)
                nc.scalar.activation(dis_r[:, a:b], P[:, i, 0:b - a], ACT.Sqrt).then_inc(s_sq, 1)
            act.wait_ge(s_cols, 16 * 4)
            for i, (a, b) in enumerate(HALVES):
                act.wait_ge(s_agg0, i + 1)
                nc.scalar.activation(agg0[:, a:b], P[:, 2 + i, 0:b - a], ACT.Identity, bias=bconv_c[:, 0:1]).then_inc(s_agg0c, 1)
            sqrt_var()
            act.wait_ge(s_ffnw, 16 * 11)
            for g in range(1, 32, 2):
                layer, q, m, s, dst_ap, a, b = ffn_group(g)
                act.wait_ge(s_fm, g + 1)
                nc.scalar.activation(dst_ap, P[0:GH, g % 8, 0:b - a], ACT.Relu,
                                     bias=(bf_c[0:GH, q, m:m + 1] if layer else 0.0)).then_inc(s_fa, 1)
            sqrt_var()
            copy_transposed()
            for l in range(2):
                for g in range(2 * KD):
                    m, (a, b) = g // 2, HALVES[g % 2]
                    act.wait_ge(s_ga, l * (2 * KD) + g + 1)
                    nc.scalar.activation(XTn[:, m, a:b], P[:, (5 + g) % 8, 0:b - a], ACT.Relu,
                                         bias=bg_c[:, l, m:m + 1]).then_inc(s_gac, 1)
            sqrt_var()
            copy_transposed()
            act.sem_inc(s_ycp, 1)
            for b in range(2):
                act.sem_inc(s_yst[b], 96)
            act.wait_ge(s_table, 1)
            pairs = act.value_load(npairs_t[0:1, 0:1], min_val=NE // 2, max_val=MAX_PAIRS)
            with act.Fori(0, pairs) as p:
                for b in range(2):
                    i = 2 * p + b
                    act.wait_ge(s_bTc, i + 1)
                    for q in range(4):
                        act.wait_ge(s_hT, 4 * i + q + 1)
                        for m in range(4 * q, 4 * q + 4):
                            g = nc.scalar.activation(hT[:, m, :], P[:, 3 + q, (m % 4) * SLOTS:(m % 4 + 1) * SLOTS], ACT.Gelu,
                                                     bias=bT[b][:, m:m + 1])
                        g.then_inc(s_gelu, 1)
                    act.wait_ge(s_l2, i + 1)
                    act.wait_ge(s_yst[b], 96 * p + 96)
                    nc.scalar.activation(y_sb[b], P[:, 7, 0:384], ACT.Copy).then_inc(s_ycp, 1)
                    act.wait_ge(s_ycp, i + 2)
                    for g in range(2):
                        act.dma_start(y_dram[bass.ds(i * SLOTS, SA), g * 256:(g + 1) * 256], y_sb[b][g * SA:(g + 1) * SA, 0:256]).then_inc(s_yst[b], 16)
                    for g in range(4):
                        act.dma_start(y_dram[bass.ds(i * SLOTS + SA, SB_), g * 128:(g + 1) * 128], y_sb[b][g * SB_:(g + 1) * SB_, 256:384]).then_inc(s_yst[b], 16)

        @block.tensor
        def _(pe):
            def count_tile(r, tile, j, first=False, last=False):
                pe.wait_ge(s_onehot, tile + 1)
                for m in range(NCH):
                    if first:
                        pe.wait_ge(s_cntc, r * NCH + m + 1)
                    mm = nc.tensor.matmul(P[0:NC, m, 0:HALF], S[0:NC, j, m * NC:(m + 1) * NC], D[0:NC, j, 0:HALF],
                                          start=first, stop=last, skip_group_check=True)
                    if last and m < NCH - 1:
                        mm.then_inc(s_cnt, 1)
                mm.then_inc(s_used, 1)

            with pe.Fori(0, RUNS) as r:
                for j in range(RING):
                    count_tile(r, r * RUN_TILES + j, j, first=(j == 0))
                with pe.Fori(1, GROUPS - 1) as g:
                    for j in range(RING):
                        count_tile(r, r * RUN_TILES + g * RING + j, j)
                for j in range(RING):
                    count_tile(r, r * RUN_TILES + (GROUPS - 1) * RING + j, j, last=(j == RING - 1))

            pe.wait_ge(s_ident, 1)
            pe.wait_ge(s_ffnw, 16 * 11)
            for q in range(2):
                for k in range(2):
                    for m in range(2):
                        at = 128 + k * GE + m * GH
                        nc.tensor.transpose(P[0:GH, 6 + q, at:at + GH], wnat[0:GH, q, m, k * GH:(k + 1) * GH], ident[0:GH, 0:GH])
            for k in range(KD):
                t = nc.tensor.transpose(P[:, 7, k * 15:(k + 1) * 15], wr_nat[:, k * 128:(k + 1) * 128], ident[0:15, 0:15])
            t.then_inc(s_wmid, 1)

            ln_no = [0]

            def transpose_norm():
                ln_no[0] += 1
                pe.wait_ge(s_ln, ln_no[0])
                for c in range(NCH):
                    for k in range(KD):
                        t = nc.tensor.transpose(P[:, c, k * NC:(k + 1) * NC], xn[0:NC, c, k * 128:(k + 1) * 128], ident[0:NC, 0:NC])
                    t.then_inc(s_tp, 1)

            pe.wait_ge(s_cntc, NCH * (RUNS + 1))
            transpose_norm()
            pe.wait_ge(s_wmidc, 3)
            pe.wait_ge(s_wconv, 16)
            for c in range(NCH):
                pe.wait_ge(s_tpc, c + 1)
                for k in range(KD):
                    mm = nc.tensor.matmul(P[0:NC, 5 + c // 4, (c % 4) * 128:(c % 4 + 1) * 128], XTn[:, k, c * NC:(c + 1) * NC],
                                          wconv[:, k, :], start=(k == 0), stop=(k == KD - 1))
                if c >= 3:
                    mm.then_inc(s_h0, 1)
            pe.wait_ge(s_ones, 2)
            for c in range(NCH):
                pe.wait_ge(s_acc, NCH * (RUNS - 1) + c + 2)
                for i, (a, b) in enumerate(HALVES):
                    mm = nc.tensor.matmul(P[:, i, 0:b - a], ones[0:NC, :], C[0:NC, c, a:b], start=(c == 0), stop=(c == NCH - 1))
                    if c == NCH - 1:
                        mm.then_inc(s_deg, 1)
            pe.wait_ge(s_dis, 2)
            for c in range(NCH):
                mm = nc.tensor.matmul(P[0:NC, 7, 400 + c:401 + c], dis_r[0:1, c * NC:(c + 1) * NC], ones[0:1, 0:1], start=True, stop=True)
            mm.then_inc(s_dcp, 1)
            pe.wait_ge(s_h0c, 2)
            for c in range(NCH):
                pe.wait_ge(s_A, c + 1)
                for i, (a, b) in enumerate(HALVES):
                    mm = nc.tensor.matmul(P[:, 2 + i, 0:b - a], h0[0:NC, c, :], C[0:NC, c, a:b], start=(c == 0), stop=(c == NCH - 1))
                    if c == NCH - 1:
                        mm.then_inc(s_agg0, 1)
            pe.wait_ge(s_agg0c, 2)
            pe.wait_ge(s_wlin, 16)
            for c in range(NCH):
                nc.tensor.matmul(P[0:NC, c, :], agg0[:, c * NC:(c + 1) * NC], wlin, start=True, stop=True).then_inc(s_lin, 1)
            pe.wait_ge(s_feat, 1)
            for c in range(NCH):
                t = nc.tensor.transpose(P[0:2 * NF, c // 4, (c % 4) * NC:(c % 4 + 1) * NC],
                                        feat[0:NC, c, :, :].rearrange("p f s -> p (f s)"), ident[0:NC, 0:NC])
            t.then_inc(s_fT, 1)
            pe.wait_ge(s_fTc, 1)
            pe.wait_ge(s_win, 16 * 20)
            for g in range(32):
                layer, q, s, m, dst_ap, a, b = ffn_group(g)
                if g >= 8:
                    pe.wait_ge(s_fa if g % 2 else s_fd, (g - 8) // 2 + 1)
                if layer and g % 8 == 0:
                    pe.wait_ge(s_fd, 4 * (q + 1))
                    pe.wait_ge(s_fa, 4 * (q + 1))
                bank = P[0:GH, g % 8, 0:b - a]
                if layer == 0:
                    mm = nc.tensor.matmul(bank, win[0:2 * NF, q, s, m * GH:(m + 1) * GH], fT[0:2 * NF, a:b], start=True, stop=True)
                else:
                    for k in range(2):
                        mm = nc.tensor.matmul(bank, wmid[0:GH, q, k, m * GH:(m + 1) * GH], ffn_view(hid1[q])[0:GH, k, s, a:b],
                                              start=(k == 0), stop=(k == 1))
                mm.then_inc(s_fm, 1)
            for q in range(2):
                pe.wait_ge(s_fd, 12 + 4 * q)
                pe.wait_ge(s_fa, 12 + 4 * q)
                if q == 0:
                    pe.wait_ge(s_fd, 13)
                for c in range(NCH):
                    for s in range(2):
                        at = ((q * NCH + c) * 2 + s) * 2
                        for k in range(2):
                            mm = nc.tensor.matmul(P[0:NC, 0, at:at + 2], ffn_view(hid2[q])[0:GH, k, s, c * NC:(c + 1) * NC],
                                                  w3_T[0:GH, q, k, :], start=(k == 0), stop=(k == 1))
            mm.then_inc(s_y3, 1)

            ln_no[0] += 1
            transpose_norm()

            def gnn_h(l):
                pe.wait_ge(s_gw, 16 * (l + 1))
                for c in range(NCH):
                    for k in range(KD):
                        mm = nc.tensor.matmul(P[0:NC, c, :], XTn[:, k, c * NC:(c + 1) * NC], Gw[:, k, :], start=(k == 0), stop=(k == KD - 1))
                    mm.then_inc(s_gh, 1)

            pe.wait_ge(s_tpc, 2 * NCH)
            with pe.Fori(0, 2) as l:
                gnn_h(l)
                pe.wait_ge(s_ghc, l * NCH + NCH)
                for g in range(2 * KD):
                    m, (a, b) = g // 2, HALVES[g % 2]
                    for c in range(NCH):
                        mm = nc.tensor.matmul(P[:, (5 + g) % 8, 0:b - a], Hn[0:NC, c, m * 128:(m + 1) * 128], C[0:NC, c, a:b],
                                              start=(c == 0), stop=(c == NCH - 1))
                    mm.then_inc(s_ga, 1)
                pe.wait_ge(s_gac, l * (2 * KD) + 2 * KD)
            gnn_h(2)
            pe.wait_ge(s_ghc, 3 * NCH)
            for t in range(NCH):
                for c in range(NCH):
                    mm = nc.tensor.matmul(P[0:NC, (5 + t) % 8, :], C[0:NC, c, t * NC:(t + 1) * NC], Hn[0:NC, c, :],
                                          start=(c == 0), stop=(c == NCH - 1))
                mm.then_inc(s_ga, 1)

            pe.wait_ge(s_x3, NCH)
            transpose_norm()
            for c in range(NCH):
                pe.wait_ge(s_tpc, 2 * NCH + c + 1)
                for k in range(KD):
                    mm = nc.tensor.matmul(P[0:NC, 7, c * 15:(c + 1) * 15], XTn[:, k, c * NC:(c + 1) * NC], wr_T[:, k, :],
                                          start=(k == 0), stop=(k == KD - 1))
            mm.then_inc(s_lg, 1)
            pe.wait_ge(s_oh, 1)
            for c in range(NCH):
                for j in range(c + 1):
                    nc.tensor.matmul(P[0:NC, 6, c * NE:(c + 1) * NE], (tri16 if j == c else ones16)[0:NC, 0:NC], oh16[0:NC, j, :],
                                     start=(j == 0), stop=(j == c))
            for c in range(NCH):
                mm = nc.tensor.matmul(P[0:NC, 6, 128:128 + NE], ones16[0:NC, 0:NC], oh16[0:NC, c, :], start=(c == 0), stop=(c == NCH - 1))
            mm.then_inc(s_rank, 1)

            pe.wait_ge(s_b1, 16)
            for h in range(2):
                t = nc.tensor.transpose(P[:, 5, h * 128:(h + 1) * 128], b1_nat[:, h, :], ident[:, :])
            t.then_inc(s_b1T, 1)

            def transpose_rows(use, b):
                pe.wait_ge(s_xr[b], 16 * use)
                for k in range(KD):
                    t = nc.tensor.transpose(P[:, 7, k * SLOTS:(k + 1) * SLOTS], xr[b][:, k * 128:(k + 1) * 128], ident[0:SLOTS, 0:SLOTS])
                t.then_inc(s_xT, 1)

            pe.wait_ge(s_table, 1)
            transpose_rows(1, 0)
            pairs = pe.value_load(npairs_t[0:1, 0:1], min_val=NE // 2, max_val=MAX_PAIRS)
            with pe.Fori(0, pairs) as p:
                for b in range(2):
                    i = 2 * p + b
                    pe.wait_ge(s_xTc, i + 1)
                    pe.wait_ge(s_w1[b], 16 * KD * (p + 1))
                    w1v = w1_sb[b][:, :, :].rearrange("p k (j r n) -> p k r j n", j=4, r=4)
                    for rd in range(2):
                        for k in range(KD):
                            for g in range(2):
                                mm = nc.tensor.matmul(P[g * SA:(g + 1) * SA, rd, :], xT[b][:, k, 0:SA], w1v[:, k, 2 * rd + g],
                                                      start=(k == 0), stop=(k == KD - 1))
                        mm.then_inc(s_h, 1)
                    for k in range(KD):
                        for g in range(4):
                            mm = nc.tensor.matmul(P[g * SB_:(g + 1) * SB_, 2, :], xT[b][:, k, SA:SLOTS], w1v[:, k, g],
                                                  start=(k == 0), stop=(k == KD - 1))
                    mm.then_inc(s_h, 1)
                    pe.wait_ge(s_ycp, i + 1)
                    transpose_rows(p + 1 + b, 1 - b)
                    for rd in range(2):
                        pe.wait_ge(s_hc, 3 * i + rd + 1)
                        for j in range(4):
                            out_ap = P[:, 3 + j, 0:4 * SLOTS].rearrange("p (r s) -> p r s", r=4)[:, 2 * rd:2 * rd + 2, 0:SA]
                            nc.tensor.transpose(out_ap, h_sb[:, rd, j * 128:(j + 1) * 128], ident[:, :])
                    pe.wait_ge(s_hc, 3 * i + 3)
                    for j in range(4):
                        out_ap = P[:, 3 + j, 0:4 * SLOTS].rearrange("p (r s) -> p r s", r=4)[:, :, SA:SLOTS]
                        nc.tensor.transpose(out_ap, h_sb[:, 2, j * 128:(j + 1) * 128], ident[:, :]).then_inc(s_hT, 1)
                    pe.wait_ge(s_xTc, i + 2)
                    for q in range(4):
                        pe.wait_ge(s_w2[b][q], 16 * (p + 1))
                        pe.wait_ge(s_gelu, 4 * i + q + 1)
                        for m in range(4 * q, 4 * q + 4):
                            for g in range(2):
                                nc.tensor.matmul(P[g * SA:(g + 1) * SA, 7, 0:256], hT[:, m, 0:SA], w2_sb[b][:, m, g * 256:(g + 1) * 256],
                                                 start=(m == 0), stop=(m == MH - 1))
                    for m in range(MH):
                        for g in range(4):
                            mm = nc.tensor.matmul(P[g * SB_:(g + 1) * SB_, 7, 256:384], hT[:, m, SA:SLOTS], w2_sb[b][:, m, g * 128:(g + 1) * 128],
                                                  start=(m == 0), stop=(m == MH - 1))
                    mm.then_inc(s_l2, 1)

        @block.vector
        def _(dve):
            n = [0]

            def link(ins):
                n[0] += 1
                ins.then_inc(s_dve, 1)
                dve.wait_ge(s_dve, n[0])

            tt, ts, stt = nc.vector.tensor_tensor, nc.vector.tensor_scalar, nc.vector.scalar_tensor_tensor

            dve.wait_ge(s_edges, 32)
            nc.vector.tensor_copy(ef[0:NC, 0, :], ei[0:NC, 0, :])
            link(nc.vector.tensor_copy(ef[0:NC, 1, :], ei[0:NC, 1, :]))
            link(ts(eg[0:NC, :], ef[0:NC, 1, :], float(HALF), None, ALU.is_ge))
            ts(ef[0:NC, 2, :], eg[0:NC, :], PACK - 1.0, 1.0, ALU.mult, ALU.add)
            link(stt(ef[0:NC, 1, :], eg[0:NC, :], -float(HALF), ef[0:NC, 1, :], ALU.mult, ALU.add))
            dve.wait_ge(s_iota, 2)
            nc.vector.tensor_copy(thr[:, :], thr_i[:, :])
            link(nc.vector.tensor_copy(iota[:, :], iota_i[:, :]))
            dve.wait_ge(s_rev, 1)
            nc.vector.tensor_copy(rev[:, :, :].rearrange("p c n -> p (c n)"), rev_i[:, 0:NCH * 64])

            def onehot(tile, j):
                nc.vector.tensor_scalar(S[0:NC, j, :], iota[0:NC, :], ef[0:NC, 0, bass.ds(tile, 1)], None, ALU.is_equal)
                ts(D[0:NC, j, 0:HALF + 1], iota[0:NC, 0:HALF + 1], ef[0:NC, 1, bass.ds(tile, 1)], ef[0:NC, 2, bass.ds(tile, 1)],
                   ALU.is_equal, ALU.mult).then_inc(s_onehot, 1)

            for j in range(RING):
                onehot(j, j)
            with dve.Fori(0, ET // RING - 1) as g:
                for j in range(RING):
                    dve.wait_ge(s_used, g * RING + j + 1)
                    onehot(g * RING + RING + j, j)

            ln_no = [0]

            def norm(chunk_ready=None):
                for c in range(NCH):
                    if chunk_ready:
                        chunk_ready(c)
                    last = nc.vector.bn_stats(stats[0:NC, c, :], xs[0:NC, c, :])
                link(last)
                for c in range(NCH):
                    last = nc.vector.bn_aggr(mv[0:NC, c, :], stats[0:NC, c, :])
                link(last)
                ts(rstd[0:NC, :], mv[0:NC, :, 1], EPS, None, ALU.add).then_inc(s_var, 1)
                ln_no[0] += 1
                dve.wait_ge(s_std, ln_no[0])
                link(nc.vector.reciprocal(rstd[0:NC, :], rstd[0:NC, :]))
                for c in range(NCH):
                    last = ts(xn[0:NC, c, :], xs[0:NC, c, :], mv[0:NC, c, 0:1], rstd[0:NC, c:c + 1], ALU.subtract, ALU.mult)
                last.then_inc(s_ln, 1)

            dve.wait_ge(s_x, 32)
            dve.wait_ge(s_yz, n_zero[0])
            norm()
            for i, (a, b) in enumerate(HALVES):
                dve.wait_ge(s_sq, i + 1)
                nc.vector.reciprocal(dis_r[:, a:b], dis_r[:, a:b]).then_inc(s_dis, 1)
            dve.wait_ge(s_dcp, 1)
            nc.vector.tensor_copy(dis_c[0:NC, :], P[0:NC, 7, 400:400 + NCH]).then_inc(s_disc, 1)
            dve.wait_ge(s_disc, 1)
            for c in range(NCH):
                stt(C[0:NC, c, 0:N_NODES], C[0:NC, c, 0:N_NODES], dis_c[0:NC, c:c + 1], dis_r[0:NC, 0:N_NODES],
                    ALU.mult, ALU.mult).then_inc(s_A, 1)

            dve.wait_ge(s_xb, 1)

            def x1_chunk(c):
                dve.wait_ge(s_lin, c + 1)
                tt(xs[0:NC, c, :], xs[0:NC, c, :], P[0:NC, c, :], ALU.add).then_inc(s_x1, 1)
                dve.wait_ge(s_x1, c + 1)

            norm(x1_chunk)
            dve.wait_ge(s_ln, 2)

            gt, mx, t1 = sv(0, NCH, 64), sv(320, 4 * NCH), sv(340, 4 * NCH)
            m3, madd, msub, act2, nadd = sv(380, NCH, 3), sv(400, NCH), sv(405, NCH), sv(410, NCH), sv(415, NCH)
            stt(gt[0:NC], xn[0:NC, :, 16:80], 0.5, rev[0:NC, :, :], ALU.is_gt, ALU.mult)
            ts(m3[0:NC], xn[0:NC, :, 0:3], 0.5, None, ALU.is_gt)
            nc.vector.memset(feat[0:NC, :, 4, :], 1.0)
            link(nc.vector.tensor_copy(feat[0:NC, :, 2:4, :], xn[0:NC, :, 105:107].unsqueeze(3).to_broadcast([NC, NCH, 2, 2])))
            link(nc.vector.tensor_reduce(mx[0:NC, :], gt[0:NC].rearrange("p c (g n) -> p (c g) n", n=16), AX.X, ALU.max))
            link(ts(t1[0:NC, :], mx[0:NC, :], -1.0, 16.0, ALU.mult, ALU.add))
            stt(feat[0:NC, :, 0:2, :].rearrange("p c f s -> p c (f s)"), mx[0:NC, :].rearrange("p (c g) -> p c g", g=4), 0.0,
                t1[0:NC, :].rearrange("p (c g) -> p c g", g=4), ALU.is_gt, ALU.mult).then_inc(s_feat, 1)
            link(tt(madd[0:NC, :], m3[0:NC, :, 0], m3[0:NC, :, 1], ALU.mult))
            link(tt(nadd[0:NC, :], m3[0:NC, :, 0], madd[0:NC, :], ALU.subtract))
            link(tt(msub[0:NC, :], nadd[0:NC, :], m3[0:NC, :, 2], ALU.mult))
            link(tt(act2[0:NC, :], madd[0:NC, :], msub[0:NC, :], ALU.add))
            dve.wait_ge(s_fT, 1)
            nc.vector.tensor_copy(fT[0:2 * NF, 0:4 * NC], P[0:2 * NF, 0, 0:4 * NC])
            nc.vector.tensor_copy(fT[0:2 * NF, 4 * NC:N_NODES], P[0:2 * NF, 1, 0:NC]).then_inc(s_fTc, 1)
            dve.wait_ge(s_ffnw, 16 * 11)
            for g in range(0, 32, 2):
                layer, q, s, m, dst_ap, a, b = ffn_group(g)
                dve.wait_ge(s_fm, g + 1)
                ts(dst_ap, P[0:GH, g % 8, 0:b - a], bf_c[0:GH, q, m:m + 1] if layer else 0.0, 0.0, ALU.add, ALU.max).then_inc(s_fd, 1)
            y3, ya, ys, ysel = sv(420, 2, NCH * 2, 2), sv(460, NCH, 4), sv(480, NCH, 4), sv(500, NCH, 4)
            res, oh, car = sv(520, NCH, 2), sv(540, NCH * 2, 16), sv(700, NCH)
            dve.wait_ge(s_y3, 1)
            link(tt(y3[0:NC], P[0:NC, 0, 0:8 * NCH].rearrange("p (q n r) -> p q n r", q=2, r=2),
                    b3_b[0:NC, :, :].unsqueeze(2).to_broadcast([NC, 2, NCH * 2, 2]), ALU.add))
            tt(ya[0:NC], y3[0:NC, 0].rearrange("p (c s) r -> p c (s r)", s=2), madd[0:NC, :].unsqueeze(2).to_broadcast([NC, NCH, 4]), ALU.mult)
            link(tt(ys[0:NC], y3[0:NC, 1].rearrange("p (c s) r -> p c (s r)", s=2), msub[0:NC, :].unsqueeze(2).to_broadcast([NC, NCH, 4]), ALU.mult))
            link(tt(ysel[0:NC], ya[0:NC], ys[0:NC], ALU.add))
            link(ts(res[0:NC], ysel[0:NC].rearrange("p c (s r) -> p c s r", s=2)[:, :, :, 0], 0.0, 15.0, ALU.max, ALU.min))
            link(ts(res[0:NC], res[0:NC], ROUND, None, ALU.add))
            link(ts(res[0:NC], res[0:NC], -ROUND, None, ALU.add))
            stt(car[0:NC, :], ysel[0:NC, :, 3], 0.5, act2[0:NC, :], ALU.is_gt, ALU.mult)
            link(ts(act2[0:NC, :], act2[0:NC, :], 2.0, None, ALU.mult))
            link(tt(oh[0:NC], iota[0:NC, 0:16].unsqueeze(1).to_broadcast([NC, NCH * 2, 16]),
                    res[0:NC].rearrange("p c s -> p (c s)").unsqueeze(2).to_broadcast([NC, NCH * 2, 16]), ALU.is_equal))
            link(tt(oh[0:NC].rearrange("p (c s) n -> p c (s n)", s=2), oh[0:NC].rearrange("p (c s) n -> p c (s n)", s=2),
                    act2[0:NC, :].unsqueeze(2).to_broadcast([NC, NCH, 32]), ALU.mult))
            dve.wait_ge(s_xsum, 1)
            tt(xs[0:NC, :, 128:160], xs[0:NC, :, 128:160], oh[0:NC].rearrange("p (c s) n -> p c (s n)", s=2), ALU.add)
            link(tt(xs[0:NC, :, 160:161], xs[0:NC, :, 160:161], car[0:NC, :].unsqueeze(2), ALU.add))
            norm()

            with dve.Fori(0, 3) as l:
                for c in range(NCH):
                    dve.wait_ge(s_gh, l * NCH + c + 1)
                    nc.vector.tensor_copy(Hn[0:NC, c, :], P[0:NC, c, :]).then_inc(s_ghc, 1)
            dve.wait_ge(s_bg2, 16)

            def x3_chunk(c):
                dve.wait_ge(s_ga, 4 * KD + c + 1)
                link(tt(xn[0:NC, c, :], P[0:NC, (5 + c) % 8, :], bg2_b[0:NC, :], ALU.add))
                stt(xs[0:NC, c, :], xn[0:NC, c, :], 0.0, xs[0:NC, c, :], ALU.max, ALU.add).then_inc(s_x3, 1)
                dve.wait_ge(s_x3, c + 1)

            norm(x3_chunk)

            bits = sv(0, NCH, 15)
            level = [None, sv(80, NCH, 2), sv(90, NCH, 4), sv(110, NCH, 8), leaf]
            dve.wait_ge(s_lg, 1)
            dve.wait_ge(s_cols, 16 * 4)
            link(tt(bits[0:NC], P[0:NC, 7, 0:NCH * 15].rearrange("p (c n) -> p c n", n=15),
                    br_b[0:NC, :].unsqueeze(1).to_broadcast([NC, NCH, 15]), ALU.add))
            link(ts(bits[0:NC], bits[0:NC], 0.0, None, ALU.is_gt))
            for d in range(4):
                w = 2 ** d
                right = level[d + 1][0:NC].rearrange("p c (j t) -> p c j t", t=2)
                here = bits[0:NC, :, w - 1:2 * w - 1]
                if d == 0:
                    nc.vector.tensor_copy(right[:, :, :, 1], here)
                    link(ts(right[:, :, :, 0], here, -1.0, 1.0, ALU.mult, ALU.add))
                else:
                    link(tt(right[:, :, :, 1], level[d][0:NC], here, ALU.mult))
                    link(tt(right[:, :, :, 0], level[d][0:NC], right[:, :, :, 1], ALU.subtract))
            nc.vector.tensor_copy(oh16[0:NC], leaf[0:NC]).then_inc(s_oh, 1)

            cmp, extra, cum, cumx = sv(290, NE, MORE), sv(402, NE), sv(418, NE), sv(434, NE)
            pick, rk, ce, le, ge, key = sv(450, NCH, NE), sv(530, NCH), sv(535, NCH), sv(540, NCH), sv(545, NCH), sv(550, NCH)
            cmpq, eid, more = sv(560, TAB - NE, NE), sv(690, TAB), sv(720, 5)
            dve.wait_ge(s_rank, 1)
            link(nc.vector.tensor_copy(cum[0:NC, :], P[0:NC, 6, 128:128 + NE]))
            link(tt(cmp[0:NC], cum[0:NC, :].unsqueeze(2).to_broadcast([NC, NE, MORE]),
                    thr[0:NC, 0:MORE].unsqueeze(1).to_broadcast([NC, NE, MORE]), ALU.is_gt))
            link(nc.vector.tensor_reduce(extra[0:NC, :], cmp[0:NC], AX.X, ALU.add))
            link(nc.vector.tensor_tensor_scan(cum[0:NC, :], ones[0:NC, 0:NE], extra[0:NC, :], 0.0, ALU.mult, ALU.add))
            link(stt(cumx[0:NC, :], cum[0:NC, :], float(NE - 1), extra[0:NC, :], ALU.add, ALU.subtract))

            def picked(to, values):
                link(tt(pick[0:NC], leaf[0:NC], values, ALU.mult))
                link(nc.vector.tensor_reduce(to[0:NC, :], pick[0:NC], AX.X, ALU.add))

            picked(rk, P[0:NC, 6, 0:NCH * NE].rearrange("p (c e) -> p c e", e=NE))
            picked(ce, cumx[0:NC, :].unsqueeze(1).to_broadcast([NC, NCH, NE]))
            picked(le, iota[0:NC, 0:NE].unsqueeze(1).to_broadcast([NC, NCH, NE]))
            link(tt(ce[0:NC, :], ce[0:NC, :], le[0:NC, :], ALU.subtract))
            link(stt(ge[0:NC, :], rk[0:NC, :], float(SLOTS), ce[0:NC, :], ALU.is_ge, ALU.mult))
            link(tt(ge[0:NC, :], ge[0:NC, :], le[0:NC, :], ALU.add))
            nc.vector.tensor_copy(lidx[0:NC, :], le[0:NC, :])
            stt(gidx[0:NC, :], ge[0:NC, :], float(SLOTS), rk[0:NC, :], ALU.mult, ALU.add)
            nc.vector.tensor_copy(eid[0:1, 0:NE], iota[0:1, 0:NE])
            link(tt(cmpq[0:1], cum[0:1, :].unsqueeze(1).to_broadcast([1, TAB - NE, NE]),
                    iota[0:1, 0:TAB - NE].unsqueeze(2).to_broadcast([1, TAB - NE, NE]), ALU.is_le))
            link(nc.vector.tensor_reduce(eid[0:1, NE:TAB], cmpq[0:1], AX.X, ALU.add))
            ts(tab[0:1, :], eid[0:1, :], float(NE - 1), None, ALU.min)
            link(ts(more[0:1, 0:4], iota[0:1, 0:4], 2.0, cum[0:1, NE - 1:NE], ALU.mult, ALU.is_lt))
            link(nc.vector.tensor_reduce(more[0:1, 4:5], more[0:1, 0:4], AX.X, ALU.add))
            ts(npairs_t[0:1, :], more[0:1, 4:5], float(NE // 2), None, ALU.add).then_inc(s_table, 1)

            dve.wait_ge(s_b1T, 1)
            nc.vector.tensor_copy(b1T, P[:, 5, 0:256]).then_inc(s_b1Tc, 1)

            def copy_inputs(i, b):
                dve.wait_ge(s_xT, i + 1)
                nc.vector.tensor_copy(xT[b], P[:, 7, 0:KD * SLOTS].rearrange("p (k s) -> p k s", k=KD)).then_inc(s_xTc, 1)

            dve.wait_ge(s_table, 1)
            copy_inputs(0, 0)
            dve.wait_ge(s_b1Tc, 1)
            pairs = dve.value_load(npairs_t[0:1, 0:1], min_val=NE // 2, max_val=MAX_PAIRS)
            with dve.Fori(0, pairs) as p:
                for b in range(2):
                    i = 2 * p + b
                    e = dve.value_load(tab[0:1, bass.ds(i, 1)], min_val=0, max_val=NE - 1)
                    for t in range(2):
                        dve.wait_ge(s_h, 3 * i + t + 1)
                        nc.vector.tensor_copy(h_sb[:, t, :], P[:, t, :]).then_inc(s_hc, 1)
                    nc.vector.tensor_copy(bT[b], b1T[:, bass.ds(e * MH, MH)]).then_inc(s_bTc, 1)
                    dve.wait_ge(s_h, 3 * i + 3)
                    nc.vector.tensor_copy(h_sb[:, 2, :], P[:, 2, :]).then_inc(s_hc, 1)
                    copy_inputs(i + 1, 1 - b)
            dve.wait_ge(s_x3b, 1)
            for c in range(NCH):
                dve.wait_ge(s_gat[c], 16)
                tt(xs[0:NC, c, :], xs[0:NC, c, :], xn[0:NC, c, :], ALU.add).then_inc(s_fin, 1)


_INS = ["x", "src", "dst", "L0_gnn_W_conv", "L0_gnn_b_conv", "L0_gnn_W_lin", "L0_gnn_b_lin", "L0_ffn_Wa", "L0_ffn_ba",
        "L0_ffn_Ws", "L0_ffn_bs", "L1_gnn_W", "L1_gnn_b", "L1_ffn_Wr", "L1_ffn_br", "L1_ffn_W1", "L1_ffn_b1",
        "L1_ffn_W2", "L1_ffn_b2"]


def kernel(**inputs):
    import numpy as _np
    import concourse.bacc as _bacc
    from concourse import mybir as _mybir
    from concourse.bass_utils import run_bass_kernel_spmd as _run

    nc = _bacc.Bacc("TRN2", target_bir_lowering=False, num_devices=1)
    arrays, args = {}, []
    for name in _INS:
        a = _np.ascontiguousarray(inputs[name])
        arrays[f"in_{name}"] = a
        args.append(nc.dram_tensor(f"in_{name}", a.shape, _mybir.dt.from_np(a.dtype), kind="ExternalInput").ap())
    args.append(nc.dram_tensor("out_0", (N_NODES, DIM), _mybir.dt.float32, kind="ExternalOutput").ap())
    build(nc, *args)
    r = _run(nc, [arrays], core_ids=[0])
    return r.results[0]["out_0"]
```

```python
from contextlib import ExitStack

import numpy as np
import concourse.bass as bass
from concourse import mybir

F32 = mybir.dt.float32
BF16 = mybir.dt.bfloat16
F16 = mybir.dt.float16
I32 = mybir.dt.int32
U32 = mybir.dt.uint32
ALU = mybir.AluOpType
ACT = mybir.ActivationFunctionType
AX = mybir.AxisListType

N_NODES, DIM, N_EDGES = 625, 512, 20000
NCH = 5
NC = N_NODES // NCH
KD = DIM // 128
HALF = (N_NODES + 1) // 2
NPAD = 2 * HALF
HALVES = ((0, HALF), (HALF, N_NODES))
EPS = 1e-5

RING = 4
GROUP = RING * NC
EG = N_EDGES // GROUP
LAST = NC + 2
SW = NPAD + 2
DW = NC + 1
ACT_D = 2

GE = 160
GM, GT = 128, GE - 128
CASES = 4
NT = CASES + 1
NF = 5
RESULT = 100

NE, HID = 16, 2048
MH = HID // 128
SA, SB_ = 64, 32
SLOTS = SA + SB_
MORE = (N_NODES - 1) // SLOTS
MAX_PAIRS = NE // 2 + -(-MORE // 2)
TAB = 2 * MAX_PAIRS
ROUND = 12582912.0


def build(nc, x, src, dst, Wconv, bconv, Wlin, blin, Wa, ba, Ws, bs, Wg, bg, Wr, br, W1, b1, W2, b2, out):
    ctx = ExitStack()
    with ctx:
        ctx.enter_context(nc.allow_non_contiguous_dma(reason="small bias columns"))

        def sb(name, shape, dt=F32):
            return ctx.enter_context(nc.sbuf_tensor(name, shape, dt))

        def sem(name):
            return ctx.enter_context(nc.semaphore(name))

        w1_sb = [sb(f"w1_{b}", [128, KD, HID]) for b in range(2)]
        w2_sb = [sb(f"w2_{b}", [128, MH, DIM]) for b in range(2)]
        xs = sb("xs", [128, NCH, DIM])
        xn = sb("xn", [128, NCH, DIM])
        XT = sb("XT", [128, 4 * NPAD])
        H = sb("H", [128, NCH * DIM])
        FB = sb("FB", [128, 4 * NPAD])
        C = sb("C", [128, NCH, NPAD])
        G = sb("G", [128, KD * DIM])
        ident = sb("ident", [128, 128])
        ones = sb("ones", [128, 16])
        ones16 = sb("ones16", [128, 128], BF16)
        tri16 = sb("tri16", [128, 128], BF16)
        iota_i = XT[:, 1792:1792 + NPAD].bitcast(I32)
        rev_i = H[:, 1512:1512 + NCH * 64].bitcast(I32)
        iota = sb("iota", [128, NPAD], F16)
        rev = sb("rev", [128, NCH, 64], F16)
        stats = sb("stats", [128, NCH, 6])
        mv = sb("mv", [128, NCH, 2])
        rstd = sb("rstd", [128, NCH])
        bconv_c = sb("bconv_c", [128, 1])
        bg_c = sb("bg_c", [128, 2, KD])
        bf_c = sb("bf_c", [128, NT])
        b3_c = sb("b3_c", [2 * CASES, 1])
        br_b = sb("br_b", [128, 15])
        wr_T = sb("wr_T", [128, KD, 15])
        dis_c = sb("dis_c", [128, NCH])
        w3_T = sb("w3_T", [128, NT, 2 * CASES])
        feat = sb("feat", [128, NCH, NF, 2])
        small = sb("small", [128, 728])
        gidx = sb("gidx", [128, NCH], U32)
        ranges = sb("ranges", [1, 3, NCH], I32)
        tab = sb("tab", [1, TAB], I32)
        npairs_t = sb("npairs_t", [1, 1], I32)
        thr_i = sb("thr_i", [128, 16], I32)
        thr = sb("thr", [128, 16])
        lidx = sb("lidx", [128, NCH], U32)
        P = ctx.enter_context(nc.psum_tensor("P", [128, 8, 512], F32))

        sqd = H[:, 1512:1512 + ACT_D * DW // 2].bitcast(BF16).rearrange("p (r n) -> p r n", r=ACT_D)
        S = H[:, 0:RING * SW // 2].bitcast(BF16).rearrange("p (r n) -> p r n", r=RING)
        D = H[:, RING * SW // 2:RING * (SW + DW) // 2].bitcast(BF16).rearrange("p (r n) -> p r n", r=RING)
        assert RING * (SW + DW) // 2 <= 1512
        loops = G[:, 0:NCH * NC].bitcast(BF16)
        ident16 = loops[0:NC, GROUP:GROUP + NC]
        wconv = H[:, 1880:1880 + DIM].rearrange("p (k n) -> p k n", k=KD)
        h0 = FB[:, 1764:1764 + NCH * 128].rearrange("p (c n) -> p c n", c=NCH)
        ei = FB[0:EG, 0:2 * GROUP].bitcast(I32).rearrange("p (s e) -> p s e", s=2)
        er = FB[0:EG, 2 * GROUP:4 * GROUP].rearrange("p (s e) -> p s e", s=2)
        ew = 2 * EG - 1
        ef = small[:, 0:2 * RING * ew].rearrange("p (s j g) -> p s j g", s=2, j=RING)
        blin_b = H[:, 640:640 + DIM]
        ct = [FB[0:NC, b * NPAD:b * NPAD + N_NODES] for b in range(2)]
        XTn = XT[:, :].rearrange("p (k n) -> p k n", k=KD)
        Hn = H[:, :].rearrange("p (c n) -> p c n", c=NCH)
        Gw = G[:, :].rearrange("p (k n) -> p k n", k=KD)
        wlin = XT[:, 0:DIM]
        wnat = XT[:, 640:640 + 5 * 128].rearrange("p (b n) -> p b n", b=5)
        wmid = sb("wmid", [128, 5, 128])
        win = G[:, 1024:1024 + 4 * GE].rearrange("p (c o) -> p c o", c=CASES)
        win_tail = G[:, 1024 + CASES * GE:1024 + CASES * (GE + GT)].rearrange("p (c o) -> p c o", c=CASES)
        fT = G[:, 0:N_NODES]
        y3T = H[0:2 * CASES, 2 * N_NODES:3 * N_NODES]

        agg0 = H[:, 0:N_NODES]

        def ffn_features(layer, t):
            if t < CASES:
                return (FB if layer else XT)[:, t * N_NODES:(t + 1) * N_NODES]
            return H[:, layer * N_NODES:(layer + 1) * N_NODES]

        def ffn_group(g):
            layer, h, t = g // (2 * NT), g // NT % 2, g % NT
            return (layer, t) + HALVES[h]

        bg2_b = FB[:, 0:DIM]
        wr_nat = XT[0:15, 1280:1280 + DIM]
        h_sb = H[:, 0:3 * DIM].rearrange("p (t n) -> p t n", t=3)
        xT = [H[:, 1536 + b * KD * SLOTS:1536 + (b + 1) * KD * SLOTS].rearrange("p (k s) -> p k s", k=KD) for b in range(2)]
        hT = FB[:, 0:MH * SLOTS].rearrange("p (m s) -> p m s", m=MH)
        xr = [XT[0:SLOTS, b * DIM:(b + 1) * DIM] for b in range(2)]
        y_sb = [XT[:, 1024 + b * 384:1024 + (b + 1) * 384] for b in range(2)]
        sel = XT[:, 1792:1792 + NCH * SLOTS].rearrange("p (c s) -> p c s", c=NCH)
        b1_nat = G[:, 0:256].rearrange("p (h n) -> p h n", h=2)
        b1T = G[:, 256:512]
        bT = [G[:, 512 + b * MH:512 + (b + 1) * MH] for b in range(2)]
        b2g = C[0:NC, :, 0:DIM]
        x_dram = nc.dram_tensor("x_rows", [(TAB + 1) * SLOTS, DIM], F32, kind="Internal").ap()
        y_dram = nc.dram_tensor("y_rows", [TAB * SLOTS, DIM], F32, kind="Internal").ap()

        def sv(at, *dims):
            n = int(np.prod(dims))
            v = small[:, at:at + n]
            names = " ".join(f"d{i}" for i in range(len(dims)))
            if len(dims) > 1:
                v = v.rearrange(f"p ({names}) -> p {names}", **{f"d{i}": d for i, d in enumerate(dims)})
            return v

        leaf = sv(150, NCH, NE)
        oh16 = small[:, 230:230 + NCH * NE // 2].bitcast(BF16).rearrange("p (c e) -> p c e", e=NE)

        s_edges, s_x, s_wconv, s_blin, s_cols = (sem(n) for n in ("edges_in", "x_in", "wconv_in", "blin_in", "cols_in"))
        s_wlin, s_ffnw, s_win, s_gw, s_bg2 = (sem(n) for n in ("wlin_in", "ffnw_in", "win_in", "gnnw_in", "bg2_in"))
        s_w1 = [sem(f"w1_in{b}") for b in range(2)]
        s_w2 = [[sem(f"w2_in{b}_{q}") for q in range(4)] for b in range(2)]
        s_xr = [sem(f"tile_rows_in{b}") for b in range(2)]
        s_iota, s_ident, s_rev, s_ones, s_loops, s_winz, s_xb = (sem(n) for n in
            ("iota_ready", "ident_ready", "rev_ready", "ones_ready", "loops_ready", "win_cleared", "x_plus_blin"))
        s_pool = sem("pool_chain")
        s_zero, s_yz = sem("zeros_ready"), sem("zeros_stored")
        s_dve = sem("dve_chain")
        s_var, s_std, s_ln = sem("var_ready"), sem("std_ready"), sem("layernorm_ready")
        s_tp, s_tpc = sem("transposed"), sem("transposed_copied")
        s_h0, s_h0c = sem("h0_ready"), sem("h0_copied")
        s_onehot, s_used = sem("onehot_ready"), sem("onehot_used")
        s_er, s_mm, s_ecol, s_mmrow, s_range = (sem(n) for n in ("edge_floats", "group_min_max", "edge_columns", "min_max_rows", "ranges_ready"))
        s_near, s_dhot, s_go = sem("square_distances"), sem("target_onehot_ready"), sem("group_start")
        s_blk, s_h0s = sem("block_counted"), sem("h0_scaled")
        s_sq, s_disc, s_ct, s_turned, s_A = (sem(n) for n in
            ("sqrt_degree_ready", "inverse_ready", "block_scaled", "block_turned", "adjacency_ready"))
        s_agg0, s_agg0c, s_lin, s_x1 = sem("agg0_ready"), sem("agg0_copied"), sem("lin_ready"), sem("x1_ready")
        s_feat, s_fT, s_fTc, s_wmid, s_wmidc = (sem(n) for n in ("feat_ready", "featT", "featT_copied", "wmid_T", "wmid_copied"))
        s_fm, s_fd, s_fa, s_y3 = sem("ffn_mm"), sem("ffn_dve_copied"), sem("ffn_act_copied"), sem("ffn_out_ready")
        s_fTz = sem("inputs_cleared")
        s_keys, s_sel = sem("row_keys_ready"), sem("tile0_selector_ready")
        s_y3c, s_wint = sem("ffn_out_copied"), sem("win_tail_copied")
        s_xsum = sem("x1_plus_norm")
        s_gh, s_ghc, s_ga, s_gac, s_x3 = (sem(n) for n in ("gnn_h", "gnn_h_copied", "gnn_agg", "gnn_agg_copied", "x3_ready"))
        s_lg, s_oh, s_rank, s_table = (sem(n) for n in ("logits", "onehot16", "ranks", "table_ready"))
        s_scat, s_b2g, s_b1, s_b1T, s_b1Tc, s_x3b = (sem(n) for n in
            ("rows_scattered", "b2_gathered", "b1_in", "b1_transposed", "b1_copied", "x3_plus_b2"))
        s_xT, s_xTc = sem("tile_transposed"), sem("tile_copied")
        s_h, s_hc, s_hT, s_gelu, s_l2 = (sem(n) for n in ("hidden_bank", "hidden_copied", "hidden_transposed", "gelu_done", "expert_out"))
        s_bTc, s_ycp, s_w1u = sem("tile_bias_copied"), sem("y_copied"), sem("w1_rows_used")
        s_yst = [sem(f"y_stored{b}") for b in range(2)]
        s_gat, s_fin, s_out, s_stored = [sem(f"y_gathered{c}") for c in range(NCH)], sem("final_ready"), sem("out_stored"), sem("all_tiles_stored")

        block = ctx.enter_context(nc.Block())

        ALL_CHUNKS = ((0, NCH),)
        LAST_CHUNKS = ((0, 3), (3, 4), (4, 5))

        def rows16(n):
            return ((0, n // 16 * 16), (n // 16 * 16, n))

        n_zero, n_ffnw = [0], [0]

        @block.sync
        def _(sp):
            for i, e in enumerate((src, dst)):
                sp.dma_start(ei[:, i, :], e.rearrange("(g e) -> g e", e=GROUP)).then_inc(s_edges, 16)
            xv = x.rearrange("(c p) d -> p c d", p=NC)
            for a, b in rows16(NC):
                sp.dma_start(xs[a:b, :, :], xv[a:b]).then_inc(s_x, 16)
            sp.dma_start(wconv, Wconv.rearrange("(k p) n -> p k n", p=128)).then_inc(s_wconv, 16)
            sp.wait_ge(s_zero, 1)
            blk = SLOTS * NCH
            for rows, first in ((x_dram, 0), (y_dram, NE * SLOTS)):
                for at in range(first, rows.shape[0], blk):
                    k = min(blk, rows.shape[0] - at) // SLOTS
                    sp.dma_start(rows[at:at + k * SLOTS, :].rearrange("(p c) n -> p c n", p=SLOTS), xn[0:SLOTS, 0:k, :]).then_inc(s_yz, 16)
                    n_zero[0] += 16
            sp.dma_start(bconv_c[:, :], bconv.rearrange("(p a) -> p a", a=1)).then_inc(s_cols, 16)
            for l in range(2):
                sp.dma_start(bg_c[:, l, :], bg[l, :].rearrange("(k p) -> p k", p=128)).then_inc(s_cols, 16)
            sp.dma_start(br_b[0:NC, :], br.rearrange("(a n) -> a n", a=1).to_broadcast([NC, 15])).then_inc(s_cols, 16)
            for q, (w, b) in enumerate(((Wa, ba), (Ws, bs))):
                loads = [(wnat[:, q, :], w[1, 0:GM, 0:GM]),
                         (wnat[:, 2, 2 * q * GT:2 * (q + 1) * GT].rearrange("p (s n) -> p s n", s=2),
                          w[1, 0:GM, GM:GE].unsqueeze(1).to_broadcast([GM, 2, GT])),
                         (b3_c[4 * q:4 * q + 2, :], b[2, RESULT:RESULT + 2].rearrange("(p a) -> p a", a=1)),
                         (b3_c[4 * q + 2:4 * q + 4, :], b[2, RESULT:RESULT + 2].rearrange("(p a) -> p a", a=1))]
                for c in (2 * q, 2 * q + 1):
                    tail = slice(c * GT, (c + 1) * GT)
                    loads += [(wnat[tail, 3, :], w[1, GM:GE, 0:GM]),
                              (wnat[tail, 4, tail], w[1, GM:GE, GM:GE]),
                              (bf_c[:, c:c + 1], b[1, 0:GM].rearrange("(p a) -> p a", a=1)),
                              (bf_c[tail, CASES:NT], b[1, GM:GE].rearrange("(p a) -> p a", a=1)),
                              (w3_T[:, c, 2 * c:2 * c + 2], w[2, RESULT:RESULT + 2, 0:GM].rearrange("r p -> p r")),
                              (w3_T[tail, CASES, 2 * c:2 * c + 2], w[2, RESULT:RESULT + 2, GM:GE].rearrange("r p -> p r"))]
                for to, what in loads:
                    sp.dma_start(to, what).then_inc(s_ffnw, 16)
                    n_ffnw[0] += 16
            sp.dma_start(wr_nat, Wr).then_inc(s_ffnw, 16)
            n_ffnw[0] += 16
            sp.wait_ge(s_winz, 1)
            for q, (w, b) in enumerate(((Wa, ba), (Ws, bs))):
                for s in range(2):
                    for f0, i0 in ((0, 0), (2, 35)):
                        for f in range(2):
                            r = 2 * (f0 + f) + s
                            sp.dma_start(win[r:r + 1, 2 * q + s, :], w[0, :, i0 + f:i0 + f + 1].rearrange("o a -> a o")).then_inc(s_win, 16)
                    sp.dma_start(win[8 + s:9 + s, 2 * q + s, :], b[0:1, :]).then_inc(s_win, 16)
            for b in range(2):
                for k in range(KD):
                    sp.dma_start(w1_sb[b][:, k, :], W1[b, k * 128:(k + 1) * 128, :]).then_inc(s_w1[b], 16)
                for q in range(4):
                    sp.dma_start(w2_sb[b][:, 4 * q:4 * q + 4, :],
                                 W2[b, q * DIM:(q + 1) * DIM, :].rearrange("(m p) n -> p m n", p=128)).then_inc(s_w2[b][q], 16)
            sp.wait_ge(s_blk, NCH)
            sp.dma_start(blin_b[0:NC, :], blin.rearrange("(a n) -> a n", a=1).to_broadcast([NC, DIM])).then_inc(s_blin, 16)
            sp.wait_ge(s_h0, 2)
            sp.dma_start(wlin, Wlin).then_inc(s_wlin, 16)
            sp.wait_ge(s_y3, 3)
            for l in range(3):
                if l:
                    sp.wait_ge(s_gh, NCH * l)
                sp.dma_start(Gw, Wg[l].rearrange("(k p) n -> p k n", p=128)).then_inc(s_gw, 16)
                if l == 0:
                    sp.dma_start(bg2_b[0:NC, :], bg[2:3, :].to_broadcast([NC, DIM])).then_inc(s_bg2, 16)
            sp.wait_ge(s_gh, NCH * 3)
            sp.dma_start(b1_nat, b1.rearrange("e (m p) -> (e m) p", p=128).rearrange("(h r) p -> r h p", h=2)).then_inc(s_b1, 16)

            def load_rows(b, i):
                sp.dma_start(xr[b], x_dram[bass.ds(i * SLOTS, SLOTS), :]).then_inc(s_xr[b], 16)

            sp.wait_ge(s_scat, 16 * NCH)
            load_rows(1, 1)
            load_rows(0, 2)
            sp.wait_ge(s_table, 1)
            pairs = sp.value_load(npairs_t[0:1, 0:1], min_val=NE // 2, max_val=MAX_PAIRS)
            with sp.Fori(0, pairs - 1) as p:
                for b in range(2):
                    done = 2 * p + b + 1
                    e = sp.value_load(tab[0:1, bass.ds(done + 1, 1)], min_val=0, max_val=NE - 1)
                    for k in range(KD):
                        if k < KD - 1:
                            sp.wait_ge(s_w1u, (done - 1) * (KD - 1) + k + 1)
                        else:
                            sp.wait_ge(s_h, done * 3)
                        sp.dma_start(w1_sb[b][:, k, :], W1[bass.ds(e, 1), k * 128:(k + 1) * 128, :].rearrange("a p n -> (a p) n")).then_inc(s_w1[b], 16)
                    sp.wait_ge(s_xT, done + 1)
                    load_rows(1 - b, done + 2)
                    for q in range(4):
                        sp.wait_ge(s_l2, 4 * (done - 1) + q + 1)
                        sp.dma_start(w2_sb[b][:, 4 * q:4 * q + 4, :],
                                     W2[bass.ds(e, 1), q * DIM:(q + 1) * DIM, :].rearrange("a (m p) n -> p (a m) n", p=128)).then_inc(s_w2[b][q], 16)
            for c in range(NCH):
                sp.wait_ge(s_fin, c + 1)
                for i, (a, b) in enumerate(rows16(NC)):
                    sp.dma_start(out[c * NC + a:c * NC + b, :], xs[a:b, c, :]).then_inc(s_out, 16)
            sp.wait_ge(s_out, 16 * 2 * NCH)

        @block.gpsimd
        def _(pool):
            n = [0]

            def link(ins):
                n[0] += 1
                ins.then_inc(s_pool, 1)
                pool.wait_ge(s_pool, n[0])

            nc.gpsimd.iota(iota_i[:, :], pattern=[[1, NPAD]], base=0, channel_multiplier=0).then_inc(s_iota, 1)
            nc.gpsimd.iota(rev_i, pattern=[[0, NCH * 4], [-1, 16]], base=16, channel_multiplier=0).then_inc(s_rev, 1)
            nc.gpsimd.memset(wnat[:, 4, :], 0.0)
            nc.gpsimd.memset(w3_T[:, :, :], 0.0)
            nc.gpsimd.memset(xn[:, :, :], 0.0).then_inc(s_zero, 1)
            link(nc.gpsimd.memset(ident[:, :], 0.0))
            nc.gpsimd.affine_select(out=ident[:, :], in_=ident[:, :], compare_op=ALU.not_equal, fill=1.0, base=0,
                                    pattern=[[-1, 128]], channel_multiplier=1).then_inc(s_ident, 1)
            nc.gpsimd.iota(thr_i[:, :], pattern=[[SLOTS, 16]], base=SLOTS, channel_multiplier=0).then_inc(s_iota, 1)
            nc.gpsimd.memset(ones[:, :], 1.0).then_inc(s_ones, 1)
            link(nc.gpsimd.memset(ones16[:, :], 1.0))
            nc.gpsimd.affine_select(out=tri16[:, :], in_=ones16[:, :], compare_op=ALU.is_gt, fill=0.0, base=0,
                                    pattern=[[1, 128]], channel_multiplier=-1).then_inc(s_ones, 1)
            nc.gpsimd.memset(S[:, :, NPAD:SW], 1.0).then_inc(s_ones, 1)
            link(nc.gpsimd.memset(loops[:, :], 0.0))
            nc.gpsimd.affine_select(out=ident16, in_=ident16, compare_op=ALU.not_equal, fill=1.0, base=0,
                                    pattern=[[-1, NC]], channel_multiplier=1).then_inc(s_loops, 1)
            nc.gpsimd.memset(G[:, 1024:1024 + 4 * GE], 0.0).then_inc(s_winz, 1)
            pool.wait_ge(s_blk, NCH)
            nc.gpsimd.memset(fT, 0.0).then_inc(s_fTz, 1)
            pool.wait_ge(s_blin, 16)
            pool.wait_ge(s_ln, NCH)
            nc.gpsimd.tensor_tensor(xs[0:NC, :, :], xs[0:NC, :, :],
                                    blin_b[0:NC, :].unsqueeze(1).to_broadcast([NC, NCH, DIM]), ALU.add).then_inc(s_xb, 1)
            pool.wait_ge(s_ln, 2 * NCH)
            nc.gpsimd.tensor_tensor(xs[0:NC, :, :], xs[0:NC, :, :], xn[0:NC, :, :], ALU.add).then_inc(s_xsum, 1)
            pool.wait_ge(s_keys, 1)
            for c in range(NCH):
                nc.gpsimd.indirect_dma_start(out=x_dram[:, :], out_offset=bass.IndirectOffsetOnAxis(ap=gidx[0:NC, c:c + 1], axis=0),
                                             in_=xn[0:NC, c, :], in_offset=None).then_inc(s_scat, 16)
            for c in range(NCH):
                nc.gpsimd.indirect_dma_start(out=b2g[:, c, :], out_offset=None, in_=b2,
                                             in_offset=bass.IndirectOffsetOnAxis(ap=lidx[0:NC, c:c + 1], axis=0)).then_inc(s_b2g, 16)
            pool.wait_ge(s_b2g, 16 * NCH)
            nc.gpsimd.tensor_tensor(xs[0:NC, :, :], xs[0:NC, :, :], b2g, ALU.add).then_inc(s_x3b, 1)
            pool.wait_ge(s_table, 1)
            pairs = pool.value_load(npairs_t[0:1, 0:1], min_val=NE // 2, max_val=MAX_PAIRS)
            for b in range(2):
                pool.wait_ge(s_yst[b], 32 * pairs + 32)
            pool.sem_inc(s_stored, 1)
            pool.wait_ge(s_stored, 1)
            for c in range(NCH):
                nc.gpsimd.indirect_dma_start(out=xn[0:NC, c, :], out_offset=None, in_=y_dram[:, :],
                                             in_offset=bass.IndirectOffsetOnAxis(ap=gidx[0:NC, c:c + 1], axis=0)).then_inc(s_gat[c], 16)
            for c in range(NCH):
                pool.wait_ge(s_gat[c], 16)

        @block.scalar
        def _(act):
            batch_no = [0]

            def sqrt_var(batches=ALL_CHUNKS):
                for first, end in batches:
                    batch_no[0] += 1
                    act.wait_ge(s_var, batch_no[0])
                    nc.scalar.activation(rstd[0:NC, first:end], rstd[0:NC, first:end], ACT.Sqrt).then_inc(s_std, 1)

            tp_no = [0]

            def copy_chunk(c, bank):
                tp_no[0] += 1
                act.wait_ge(s_tp, tp_no[0])
                nc.scalar.activation(XTn[:, :, c * NC:(c + 1) * NC], P[:, bank, 0:KD * NC].rearrange("p (k n) -> p k n", k=KD),
                                     ACT.Copy).then_inc(s_tpc, 1)

            def copy_transposed(bank=0):
                for c in range(NCH):
                    copy_chunk(c, bank + c)

            act.wait_ge(s_range, 1)
            act.wait_ge(s_ones, 3)

            def target_onehots(t):
                lo_g = act.value_load(ranges[0:1, 0, t:t + 1], min_val=0, max_val=EG - 1)
                length = act.value_load(ranges[0:1, 1, t:t + 1], min_val=1, max_val=EG)
                base = act.value_load(ranges[0:1, 2, t:t + 1], min_val=0, max_val=NCH * EG)
                even = t * NC - t % 2
                with act.Fori(0, length) as u:
                    act.wait_ge(s_dhot, (base + u) * ACT_D + ACT_D)
                    act.sem_inc(s_go, 1)
                    for j in range(ACT_D):
                        near = nc.scalar.activation(sqd[0:NC, j, :], iota[0:NC, even:even + DW], ACT.Square,
                                                    bias=ef[0:NC, 1, j, bass.ds(lo_g + u, 1)], scale=-1.0)
                    near.then_inc(s_near, 1)
                    act.wait_ge(s_near, base + u + 1)
                    for j in range(ACT_D):
                        act.wait_ge(s_used, (base + u) * RING + j + 1)
                        nc.scalar.activation(D[0:NC, j, :], sqd[0:NC, j, :], ACT.Relu, bias=ones[0:NC, 0:1], scale=-1.0).then_inc(s_dhot, 1)

            target_onehots(0)
            sqrt_var()
            def into_c(t):
                b0, cols = 2 * (t % 3), slice(t * NC, (t + 1) * NC)
                act.wait_ge(s_turned, t + 1)
                nc.scalar.activation(C[0:NC, 0:4, cols], P[0:NC, b0, 0:4 * NC].rearrange("p (m n) -> p m n", m=4), ACT.Copy)
                nc.scalar.activation(C[0:NC, 4, cols], P[0:NC, b0 + 1, 0:NC], ACT.Copy).then_inc(s_A, 1)

            for t in range(NCH):
                if t < NCH - 1:
                    target_onehots(t + 1)
                    if t > 0:
                        into_c(t - 1)
                b0 = 2 * (t % 3)
                act.wait_ge(s_blk, t + 1)
                nc.scalar.activation(dis_c[0:NC, t:t + 1], P[0:NC, b0 + 1, LAST - 1:LAST], ACT.Sqrt, bias=ones[0:NC, 0:1]).then_inc(s_sq, 1)
                if t == 0:
                    act.wait_ge(s_wmid, 1)
                    nc.scalar.activation(wmid[:, 0:4, :], P[:, 6, :].rearrange("p (b n) -> p b n", b=4), ACT.Copy).then_inc(s_wmidc, 1)
                    nc.scalar.activation(wmid[:, 4, :], P[:, 7, 128:256], ACT.Copy).then_inc(s_wmidc, 1)
                    nc.scalar.activation(wr_T[:, :, :], P[:, 7, 0:KD * 15].rearrange("p (k o) -> p k o", k=KD), ACT.Copy).then_inc(s_wmidc, 1)
                else:
                    copy_chunk(t - 1, 6)
                act.wait_ge(s_disc, t + 1)
                if t >= 2:
                    act.wait_ge(s_turned, t - 1)
                nc.scalar.activation(ct[t % 2][:, 0:GROUP], P[0:NC, b0, 0:GROUP], ACT.Copy, scale=dis_c[0:NC, t:t + 1])
                nc.scalar.activation(ct[t % 2][:, GROUP:N_NODES], P[0:NC, b0 + 1, 0:NC], ACT.Copy, scale=dis_c[0:NC, t:t + 1]).then_inc(s_ct, 1)
            into_c(3)
            copy_chunk(4, 6)
            act.wait_ge(s_h0, 1)
            nc.scalar.activation(h0[0:NC, 0:4, :], P[0:NC, 7, :].rearrange("p (c n) -> p c n", c=4), ACT.Copy).then_inc(s_h0c, 1)
            act.wait_ge(s_h0, 2)
            nc.scalar.activation(h0[0:NC, 4, :], P[0:NC, 4, 0:128], ACT.Copy).then_inc(s_h0c, 1)
            act.wait_ge(s_cols, 16 * 4)
            for i, (a, b) in enumerate(HALVES):
                act.wait_ge(s_agg0, i + 1)
                nc.scalar.activation(agg0[:, a:b], P[:, 2 + i, 0:b - a], ACT.Identity, bias=bconv_c[:, 0:1]).then_inc(s_agg0c, 1)
            sqrt_var()
            act.wait_ge(s_ffnw, n_ffnw[0])
            for g in range(1, 4 * NT, 2):
                layer, t, a, b = ffn_group(g)
                act.wait_ge(s_fm, g + 1)
                nc.scalar.activation(ffn_features(layer, t)[:, a:b], P[:, g % 8, 0:b - a], ACT.Relu,
                                     bias=(bf_c[:, t:t + 1] if layer else 0.0)).then_inc(s_fa, 1)
            act.wait_ge(s_y3, 2)
            nc.scalar.activation(y3T[:, HALF:N_NODES], P[0:2 * CASES, 5, 0:N_NODES - HALF], ACT.Identity, bias=b3_c[:, 0:1]).then_inc(s_y3c, 1)
            sqrt_var()
            copy_transposed()
            for l in range(2):
                for g in range(2 * KD):
                    m, (a, b) = g // 2, HALVES[g % 2]
                    act.wait_ge(s_ga, l * (2 * KD) + g + 1)
                    nc.scalar.activation(XTn[:, m, a:b], P[:, (5 + g) % 8, 0:b - a], ACT.Relu,
                                         bias=bg_c[:, l, m:m + 1]).then_inc(s_gac, 1)
            sqrt_var(LAST_CHUNKS)
            copy_transposed(2)
            act.sem_inc(s_ycp, 1)
            for b in range(2):
                act.sem_inc(s_yst[b], 32)
            act.wait_ge(s_table, 1)
            pairs = act.value_load(npairs_t[0:1, 0:1], min_val=NE // 2, max_val=MAX_PAIRS)
            with act.Fori(0, pairs) as p:
                for b in range(2):
                    i = 2 * p + b
                    act.wait_ge(s_bTc, i + 1)
                    for rd in range(2):
                        act.wait_ge(s_hT, 3 * i + rd + 1)
                        for c in range(8):
                            m = 8 * rd + c
                            g = nc.scalar.activation(hT[:, m, 0:SA], P[:, 3 + rd, c * SA:(c + 1) * SA], ACT.Gelu, bias=bT[b][:, m:m + 1])
                            if c % 4 == 3:
                                g.then_inc(s_gelu, 1)
                    act.wait_ge(s_hT, 3 * i + 3)
                    for m in range(MH):
                        g = nc.scalar.activation(hT[:, m, SA:SLOTS], P[:, 0, m * SB_:(m + 1) * SB_], ACT.Gelu, bias=bT[b][:, m:m + 1])
                        if m % 4 == 3:
                            g.then_inc(s_gelu, 1)
                    act.wait_ge(s_l2, 4 * i + 4)
                    act.wait_ge(s_yst[b], 32 * p + 32)
                    nc.scalar.activation(y_sb[b][:, 256:384], P[:, 5, 0:128], ACT.Copy)
                    nc.scalar.activation(y_sb[b][:, 0:256], P[:, 7, 0:256], ACT.Copy).then_inc(s_ycp, 1)
                    act.wait_ge(s_ycp, i + 2)
                    act.dma_start(y_dram[bass.ds(i * SLOTS, SA), :].rearrange("s (g n) -> g s n", g=2),
                                  y_sb[b][:, 0:256]).then_inc(s_yst[b], 16)
                    act.dma_start(y_dram[bass.ds(i * SLOTS + SA, SB_), :].rearrange("s (g n) -> g s n", g=4),
                                  y_sb[b][:, 256:384]).then_inc(s_yst[b], 16)

        @block.tensor
        def _(pe):
            def keep_warm(n, data, bank=7):
                for _ in range(n):
                    nc.tensor.matmul(P[:, bank, 0:DIM], ident[0:NC, :], data, start=True, stop=True)

            pe.wait_ge(s_ident, 1)
            pe.wait_ge(s_er, 1)
            for i in range(2):
                for j in range(RING):
                    at = (i * RING + j) * EG
                    t = nc.tensor.transpose(P[0:NC, 6, at:at + EG], er[:, i, j * NC:(j + 1) * NC], ident[0:EG, 0:EG])
            t.then_inc(s_ecol, 1)
            pe.wait_ge(s_mm, 1)
            for i in range(2):
                mm = nc.tensor.matmul(P[0:1, 7, i * EG:(i + 1) * EG], stats[0:EG, 0, i:i + 1], ident[0:EG, 0:EG], start=True, stop=True)
            mm.then_inc(s_mmrow, 1)
            pe.wait_ge(s_ones, 3)
            pe.wait_ge(s_loops, 1)
            pe.wait_ge(s_range, 1)

            def count_block(t):
                b0 = 2 * (t % 3)
                odd = t % 2
                if t >= 3:
                    pe.wait_ge(s_A, t - 2)
                length = pe.value_load(ranges[0:1, 1, t:t + 1], min_val=1, max_val=EG)
                base = pe.value_load(ranges[0:1, 2, t:t + 1], min_val=0, max_val=NCH * EG)
                nc.tensor.matmul(P[0:NC, b0, 0:4 * NC], ident16, loops[0:NC, 0:4 * NC], start=True, stop=False, skip_group_check=True)
                nc.tensor.matmul(P[0:NC, b0 + 1, 0:LAST], ident16, loops[0:NC, 0:LAST], start=True, stop=False, skip_group_check=True)
                with pe.Fori(0, length) as u:
                    for j in range(RING):
                        pe.wait_ge(s_onehot, (base + u) * RING + j + 1)
                        if j < ACT_D:
                            pe.wait_ge(s_dhot, (base + u) * ACT_D + ACT_D + j + 1)
                        hot = D[0:NC, j, odd:odd + NC]
                        nc.tensor.matmul(P[0:NC, b0, 0:GROUP], hot, S[0:NC, j, 0:GROUP], start=False, stop=False, skip_group_check=True)
                        nc.tensor.matmul(P[0:NC, b0 + 1, 0:LAST], hot, S[0:NC, j, GROUP:GROUP + LAST],
                                         start=False, stop=False, skip_group_check=True).then_inc(s_used, 1)
                w = GROUP - t * NC
                nc.tensor.matmul(P[0:NC, b0, 0:4 * NC], ident16, loops[0:NC, w:w + 4 * NC], start=False, stop=True, skip_group_check=True)
                nc.tensor.matmul(P[0:NC, b0 + 1, 0:LAST], ident16, loops[0:NC, w + 4 * NC:w + 4 * NC + LAST],
                                 start=False, stop=True, skip_group_check=True).then_inc(s_blk, 1)

            def turn_block(t):
                pe.wait_ge(s_ct, t + 1)
                for m in range(NCH):
                    tr = nc.tensor.transpose(P[0:NC, 2 * (t % 3) + m // 4, (m % 4) * NC:(m % 4 + 1) * NC],
                                             ct[t % 2][:, m * NC:(m + 1) * NC], ident[0:NC, 0:NC])
                tr.then_inc(s_turned, 1)

            def transpose_chunk(c, bank):
                for k in range(KD):
                    t = nc.tensor.transpose(P[:, bank, k * NC:(k + 1) * NC], xn[0:NC, c, k * 128:(k + 1) * 128], ident[0:NC, 0:NC])
                t.then_inc(s_tp, 1)

            def conv_chunk(c, bank, at):
                pe.wait_ge(s_tpc, c + 1)
                for k in range(KD):
                    mm = nc.tensor.matmul(P[0:NC, bank, at:at + 128], XTn[:, k, c * NC:(c + 1) * NC],
                                          wconv[:, k, :], start=(k == 0), stop=(k == KD - 1))
                if c >= 3:
                    mm.then_inc(s_h0, 1)

            count_block(0)
            pe.wait_ge(s_ffnw, n_ffnw[0])
            pe.wait_ge(s_range, 1)
            for k in range(5):
                bank, at = (6, k * 128) if k < 4 else (7, 128)
                nc.tensor.transpose(P[:, bank, at:at + 128], wnat[:, k, :], ident[:, :])
            for k in range(KD):
                t = nc.tensor.transpose(P[:, 7, k * 15:(k + 1) * 15], wr_nat[:, k * 128:(k + 1) * 128], ident[0:15, 0:15])
            t.then_inc(s_wmid, 1)
            count_block(1)
            pe.wait_ge(s_wmidc, 3)
            pe.wait_ge(s_ln, NCH)
            pe.wait_ge(s_wconv, 16)
            transpose_chunk(0, 6)
            turn_block(0)
            for t in range(2, NCH):
                count_block(t)
                conv_chunk(t - 2, 7, (t - 2) * 128)
                transpose_chunk(t - 1, 6)
                turn_block(t - 1)
            turn_block(4)
            pe.wait_ge(s_tpc, 4)
            transpose_chunk(4, 6)
            conv_chunk(3, 7, 3 * 128)
            pe.wait_ge(s_A, 3)
            conv_chunk(4, 4, 0)

            ln_no = [1]

            def transpose_norm(bank=0):
                ln_no[0] += 1
                for c in range(NCH):
                    pe.wait_ge(s_ln, (ln_no[0] - 1) * NCH + c + 1)
                    transpose_chunk(c, bank + c)

            pe.wait_ge(s_h0s, 1)
            pe.wait_ge(s_A, NCH)
            for c in range(NCH):
                for i, (a, b) in enumerate(HALVES):
                    mm = nc.tensor.matmul(P[:, 2 + i, 0:b - a], h0[0:NC, c, :], C[0:NC, c, a:b], start=(c == 0), stop=(c == NCH - 1))
                    if c == NCH - 1:
                        mm.then_inc(s_agg0, 1)
            pe.wait_ge(s_agg0c, 2)
            pe.wait_ge(s_wlin, 16)
            for c in range(NCH):
                nc.tensor.matmul(P[0:NC, c, :], agg0[:, c * NC:(c + 1) * NC], wlin, start=True, stop=True).then_inc(s_lin, 1)
            keep_warm(9, C[0:NC, 0, 0:DIM])
            pe.wait_ge(s_feat, 1)
            for c in range(NCH):
                t = nc.tensor.transpose(P[0:2 * NF, c // 4, (c % 4) * NC:(c % 4 + 1) * NC],
                                        feat[0:NC, c, :, :].rearrange("p f s -> p (f s)"), ident[0:NC, 0:NC])
            t.then_inc(s_fT, 1)
            pe.wait_ge(s_fTc, 1)
            pe.wait_ge(s_win, 16 * 20)
            pe.wait_ge(s_wint, 1)
            evicted = (s_fd, s_fa)
            for g in range(4 * NT):
                layer, t, a, b = ffn_group(g)
                if g >= 8:
                    pe.wait_ge(evicted[g % 2], (g - 8) // 2 + 1)
                if layer and t == 0:
                    done = g - 2 * NT + NT
                    pe.wait_ge(s_fd, (done + 1) // 2)
                    pe.wait_ge(s_fa, done // 2)
                bank = P[:, g % 8, 0:b - a]
                if layer == 0:
                    w = win[:, t, 0:GM] if t < CASES else win_tail.rearrange("p c n -> p (c n)")
                    mm = nc.tensor.matmul(bank, w, fT[:, a:b], start=True, stop=True)
                elif t < CASES:
                    tail = slice(t * GT, (t + 1) * GT)
                    nc.tensor.matmul(bank, wmid[:, t // 2, :], ffn_features(0, t)[:, a:b], start=True, stop=False)
                    mm = nc.tensor.matmul(bank, wmid[tail, 2, :], ffn_features(0, CASES)[tail, a:b], start=False, stop=True)
                else:
                    nc.tensor.matmul(bank, wmid[:, 4, :], ffn_features(0, CASES)[:, a:b], start=True, stop=False, skip_group_check=True)
                    for c in range(CASES):
                        mm = nc.tensor.matmul(P[c * GT:(c + 1) * GT, g % 8, 0:b - a], wmid[:, 3, c * GT:(c + 1) * GT],
                                              ffn_features(0, c)[:, a:b], start=False, stop=True, skip_group_check=True)
                mm.then_inc(s_fm, 1)
            for h, (a, b) in enumerate(HALVES):
                done = 2 * NT + (h + 1) * NT
                pe.wait_ge(s_fd, (done + 1) // 2)
                pe.wait_ge(s_fa, done // 2)
                for t in range(NT):
                    mm = nc.tensor.matmul(P[0:2 * CASES, 4 + h, 0:b - a], w3_T[:, t, :], ffn_features(1, t)[:, a:b],
                                          start=(t == 0), stop=(t == NT - 1))
                mm.then_inc(s_y3, 1)
            pe.wait_ge(s_y3c, 2)
            for c in range(NCH):
                t = nc.tensor.transpose(P[0:NC, 6, c * 2 * CASES:(c + 1) * 2 * CASES], y3T[:, c * NC:(c + 1) * NC],
                                        ident[0:2 * CASES, 0:2 * CASES])
            t.then_inc(s_y3, 1)

            keep_warm(7, C[0:NC, 0, 0:DIM])
            ln_no[0] += 1
            transpose_norm()

            def gnn_h(l, first=False):
                pe.wait_ge(s_gw, 16 * (l + 1))
                for c in range(NCH):
                    if first:
                        pe.wait_ge(s_tpc, NCH + c + 1)
                    for k in range(KD):
                        if not first and c == 0 and k in (0, KD - 1):
                            pe.wait_ge(s_gac, l * (2 * KD) - (2 if k == 0 else 0))
                        mm = nc.tensor.matmul(P[0:NC, c, :], XTn[:, k, c * NC:(c + 1) * NC], Gw[:, k, :], start=(k == 0), stop=(k == KD - 1))
                    mm.then_inc(s_gh, 1)

            gnn_h(0, first=True)
            with pe.Fori(0, 2) as l:
                for g in range(2 * KD):
                    m, (a, b) = g // 2, HALVES[g % 2]
                    for c in range(NCH):
                        if g == 0:
                            pe.wait_ge(s_ghc, l * NCH + c + 1)
                        mm = nc.tensor.matmul(P[:, (5 + g) % 8, 0:b - a], Hn[0:NC, c, m * 128:(m + 1) * 128], C[0:NC, c, a:b],
                                              start=(c == 0), stop=(c == NCH - 1))
                    mm.then_inc(s_ga, 1)
                gnn_h(l + 1)
            for t in range(NCH):
                for c in range(NCH):
                    if t == 0:
                        pe.wait_ge(s_ghc, 2 * NCH + c + 1)
                    mm = nc.tensor.matmul(P[0:NC, (5 + t) % 8, :], C[0:NC, c, t * NC:(t + 1) * NC], Hn[0:NC, c, :],
                                          start=(c == 0), stop=(c == NCH - 1))
                mm.then_inc(s_ga, 1)

            transpose_norm(2)
            for c in range(NCH):
                pe.wait_ge(s_tpc, 2 * NCH + c + 1)
                for k in range(KD):
                    mm = nc.tensor.matmul(P[0:NC, 7, c * 15:(c + 1) * 15], XTn[:, k, c * NC:(c + 1) * NC], wr_T[:, k, :],
                                          start=(k == 0), stop=(k == KD - 1))
            mm.then_inc(s_lg, 1)
            keep_warm(2, xn[0:NC, 0, :], bank=0)
            pe.wait_ge(s_oh, 1)
            for c in range(NCH):
                for j in range(c + 1):
                    nc.tensor.matmul(P[0:NC, 6, c * NE:(c + 1) * NE], (tri16 if j == c else ones16)[0:NC, 0:NC], oh16[0:NC, j, :],
                                     start=(j == 0), stop=(j == c))
            for c in range(NCH):
                mm = nc.tensor.matmul(P[0:NC, 6, 128:128 + NE], ones16[0:NC, 0:NC], oh16[0:NC, c, :], start=(c == 0), stop=(c == NCH - 1))
            mm.then_inc(s_rank, 1)

            pe.wait_ge(s_b1, 16)
            for h in range(2):
                t = nc.tensor.transpose(P[:, 5, h * 128:(h + 1) * 128], b1_nat[:, h, :], ident[:, :])
            t.then_inc(s_b1T, 1)

            def transpose_rows(use, b):
                pe.wait_ge(s_xr[b], 16 * use)
                for k in range(KD):
                    t = nc.tensor.transpose(P[:, 6, k * SLOTS:(k + 1) * SLOTS], xr[b][:, k * 128:(k + 1) * 128], ident[0:SLOTS, 0:SLOTS])
                t.then_inc(s_xT, 1)

            keep_warm(4, xn[0:NC, 0, :], bank=4)
            pe.wait_ge(s_sel, 1)
            for k in range(KD):
                for c in range(NCH):
                    mm = nc.tensor.matmul(P[:, 6, k * SLOTS:(k + 1) * SLOTS], xn[0:NC, c, k * 128:(k + 1) * 128], sel[0:NC, c, :],
                                          start=(c == 0), stop=(c == NCH - 1))
            mm.then_inc(s_xT, 1)
            pe.wait_ge(s_table, 1)
            pairs = pe.value_load(npairs_t[0:1, 0:1], min_val=NE // 2, max_val=MAX_PAIRS)
            with pe.Fori(0, pairs) as p:
                for b in range(2):
                    i = 2 * p + b
                    pe.wait_ge(s_xTc, i + 1)
                    pe.wait_ge(s_w1[b], 16 * KD * (p + 1))
                    w1a = w1_sb[b][:, :, :].rearrange("p k (h j g n) -> p k h g j n", h=2, j=4, g=2)
                    w1b = w1_sb[b][:, :, :].rearrange("p k (j r n) -> p k r j n", j=4, r=4)

                    def first_a(h, k):
                        for g in range(2):
                            mm = nc.tensor.matmul(P[g * SA:(g + 1) * SA, h, :], xT[b][:, k, 0:SA], w1a[:, k, h, g],
                                                  start=(k == 0), stop=(k == KD - 1))
                        if k == KD - 1:
                            mm.then_inc(s_h, 1)

                    def turn(to, h, count):
                        pe.wait_ge(s_hc, 3 * i + count)
                        for j in range(4):
                            t = nc.tensor.transpose(P[:, to, j * 128:(j + 1) * 128], h_sb[:, h, j * 128:(j + 1) * 128], ident[:, :])
                        t.then_inc(s_hT, 1)

                    for k in range(KD):
                        first_a(0, k)
                    for k in range(KD):
                        first_a(1, k)
                        for g in range(4):
                            mm = nc.tensor.matmul(P[g * SB_:(g + 1) * SB_, 2, :], xT[b][:, k, SA:SLOTS], w1b[:, k, g],
                                                  start=(k == 0), stop=(k == KD - 1))
                        mm.then_inc(s_h if k == KD - 1 else s_w1u, 1)
                        if k == 0:
                            turn(3, 0, 1)
                    turn(4, 1, 2)
                    transpose_rows(p + 1, 1 - b)

                    def second_a(q):
                        pe.wait_ge(s_w2[b][q], 16 * (p + 1))
                        pe.wait_ge(s_gelu, 8 * i + q + 1)
                        for m in range(4 * q, 4 * q + 4):
                            for g in range(2):
                                nc.tensor.matmul(P[g * SA:(g + 1) * SA, 7, 0:256], hT[:, m, 0:SA], w2_sb[b][:, m, g * 256:(g + 1) * 256],
                                                 start=(m == 0), stop=(m == MH - 1))

                    def second_b(q):
                        pe.wait_ge(s_gelu, 8 * i + 4 + q + 1)
                        for m in range(4 * q, 4 * q + 4):
                            for g in range(4):
                                mm = nc.tensor.matmul(P[g * SB_:(g + 1) * SB_, 5, 0:128], hT[:, m, SA:SLOTS], w2_sb[b][:, m, g * 128:(g + 1) * 128],
                                                      start=(m == 0), stop=(m == MH - 1))
                        mm.then_inc(s_l2, 1)

                    pe.wait_ge(s_ycp, i + 1)
                    second_a(0)
                    turn(0, 2, 3)
                    second_a(1)
                    for q in range(2, 4):
                        second_a(q)
                        second_b(q - 2)
                    for q in range(2, 4):
                        second_b(q)

        @block.vector
        def _(dve):
            n = [0]

            def link(ins):
                n[0] += 1
                ins.then_inc(s_dve, 1)
                dve.wait_ge(s_dve, n[0])

            tt, ts, stt = nc.vector.tensor_tensor, nc.vector.tensor_scalar, nc.vector.scalar_tensor_tensor

            dve.wait_ge(s_edges, 32)
            link(nc.vector.tensor_copy(er, ei))
            dve.sem_inc(s_er, 1)
            nc.vector.tensor_reduce(stats[0:EG, 0, 0:1], er[:, 1, :], AX.X, ALU.min)
            nc.vector.tensor_reduce(stats[0:EG, 0, 1:2], er[:, 1, :], AX.X, ALU.max).then_inc(s_mm, 1)
            dve.wait_ge(s_iota, 2)
            nc.vector.tensor_copy(thr[:, :], thr_i[:, :])
            link(nc.vector.tensor_copy(iota[:, :], iota_i[:, :]))
            dve.wait_ge(s_rev, 1)
            nc.vector.tensor_copy(rev[:, :, :].rearrange("p c n -> p (c n)"), rev_i[:, 0:NCH * 64])
            up, down = FB[0:1, 2400:2400 + EG], FB[0:1, 2440:2440 + EG]
            dif, occ = (FB[0:1, 2000 + i * NCH * EG:2000 + (i + 1) * NCH * EG].rearrange("p (t g) -> p t g", g=EG) for i in range(2))
            lo, hi, cnt, cum5 = (small[0:1, 640 + 5 * i:645 + 5 * i] for i in range(4))
            first = iota[0:1, 0:NCH * NC].rearrange("p (t n) -> p t n", n=NC)[:, :, 0:1].to_broadcast([1, NCH, EG])
            ts(up, iota[0:1, 0:EG], 1.0, None, ALU.add)
            ts(down, iota[0:1, 0:EG], -1.0, float(EG), ALU.mult, ALU.add)
            dve.wait_ge(s_ecol, 1)
            nc.vector.tensor_copy(ef[0:NC, :, :, 0:EG], P[0:NC, 6, 0:2 * RING * EG].rearrange("p (s j g) -> p s j g", s=2, j=RING))
            dve.wait_ge(s_mmrow, 1)
            link(tt(dif, P[0:1, 7, EG:2 * EG].unsqueeze(1).to_broadcast([1, NCH, EG]), first, ALU.subtract))
            link(ts(occ, dif, 0.0, None, ALU.is_ge))
            link(tt(dif, P[0:1, 7, 0:EG].unsqueeze(1).to_broadcast([1, NCH, EG]), first, ALU.subtract))
            link(stt(occ, dif, float(NC), occ, ALU.is_lt, ALU.mult))
            link(tt(dif, occ, down.unsqueeze(1).to_broadcast([1, NCH, EG]), ALU.mult))
            link(tt(occ, occ, up.unsqueeze(1).to_broadcast([1, NCH, EG]), ALU.mult))
            nc.vector.tensor_reduce(lo, dif, AX.X, ALU.max)
            link(nc.vector.tensor_reduce(hi, occ, AX.X, ALU.max))
            link(ts(lo, lo, -1.0, float(EG), ALU.mult, ALU.add))
            link(ts(lo, lo, float(EG - 1), None, ALU.min))
            link(tt(cnt, hi, lo, ALU.subtract))
            link(ts(cnt, cnt, 1.0, None, ALU.max))
            dve.wait_ge(s_ones, 3)
            link(nc.vector.tensor_tensor_scan(cum5, ones[0:1, 0:NCH], cnt, 0.0, ALU.mult, ALU.add))
            nc.vector.tensor_copy(ranges[0:1, 0, :], lo)
            nc.vector.tensor_copy(ranges[0:1, 1, :], cnt)
            tt(ranges[0:1, 2, :], cum5, cnt, ALU.subtract).then_inc(s_range, 1)
            dve.wait_ge(s_range, 1)
            dve.sem_inc(s_used, RING)
            dve.sem_inc(s_dhot, ACT_D)

            def onehots(t):
                lo_g = dve.value_load(ranges[0:1, 0, t:t + 1], min_val=0, max_val=EG - 1)
                length = dve.value_load(ranges[0:1, 1, t:t + 1], min_val=1, max_val=EG)
                base = dve.value_load(ranges[0:1, 2, t:t + 1], min_val=0, max_val=NCH * EG)
                even = t * NC - t % 2
                with dve.Fori(0, length) as u:
                    for j in range(RING):
                        dve.wait_ge(s_used, (base + u) * RING + j + 1)
                        hot = ts(S[0:NC, j, 0:NPAD], iota[0:NC, :], ef[0:NC, 0, j, bass.ds(lo_g + u, 1)], None, ALU.is_equal)
                        if j >= ACT_D:
                            hot = ts(D[0:NC, j, :], iota[0:NC, even:even + DW], ef[0:NC, 1, j, bass.ds(lo_g + u, 1)], None, ALU.is_equal)
                        hot.then_inc(s_onehot, 1)

            def invert(t):
                dve.wait_ge(s_sq, t + 1)
                nc.vector.reciprocal(dis_c[0:NC, t:t + 1], dis_c[0:NC, t:t + 1]).then_inc(s_disc, 1)

            batch_no = [0]

            def norm(chunk_ready=None, batches=ALL_CHUNKS):
                for first, end in batches:
                    for c in range(first, end):
                        if chunk_ready:
                            chunk_ready(c)
                        last = nc.vector.bn_stats(stats[0:NC, c, :], xs[0:NC, c, :])
                    link(last)
                    for c in range(first, end):
                        last = nc.vector.bn_aggr(mv[0:NC, c, :], stats[0:NC, c, :])
                    link(last)
                    ts(rstd[0:NC, first:end], mv[0:NC, first:end, 1], EPS, None, ALU.add).then_inc(s_var, 1)
                    batch_no[0] += 1
                    dve.wait_ge(s_std, batch_no[0])
                    link(nc.vector.reciprocal(rstd[0:NC, first:end], rstd[0:NC, first:end]))
                    for c in range(first, end):
                        ts(xn[0:NC, c, :], xs[0:NC, c, :], mv[0:NC, c, 0:1], rstd[0:NC, c:c + 1], ALU.subtract, ALU.mult).then_inc(s_ln, 1)

            onehots(0)
            dve.wait_ge(s_x, 32)
            dve.wait_ge(s_yz, n_zero[0])
            norm()
            for t in range(1, NCH):
                onehots(t)
                invert(t - 1)
            invert(NCH - 1)
            dve.wait_ge(s_turned, NCH)
            cols = slice((NCH - 1) * NC, NCH * NC)
            nc.vector.tensor_copy(C[0:NC, 0:4, cols], P[0:NC, 2, 0:4 * NC].rearrange("p (m n) -> p m n", m=4))
            nc.vector.tensor_copy(C[0:NC, 4, cols], P[0:NC, 3, 0:NC]).then_inc(s_A, 1)
            dve.wait_ge(s_disc, NCH)
            dve.wait_ge(s_h0c, 2)
            tt(h0[0:NC], h0[0:NC], dis_c[0:NC, :].unsqueeze(2).to_broadcast([NC, NCH, 128]), ALU.mult).then_inc(s_h0s, 1)

            dve.wait_ge(s_xb, 1)

            def x1_chunk(c):
                dve.wait_ge(s_lin, c + 1)
                tt(xs[0:NC, c, :], xs[0:NC, c, :], P[0:NC, c, :], ALU.add).then_inc(s_x1, 1)
                dve.wait_ge(s_x1, c + 1)

            norm(x1_chunk)
            dve.wait_ge(s_ln, 2 * NCH)

            dve.wait_ge(s_win, 16 * 20)
            nc.vector.tensor_copy(win_tail, win[:, :, GM:GE]).then_inc(s_wint, 1)
            gt, mx, t1 = sv(0, NCH, 64), sv(320, 4 * NCH), sv(340, 4 * NCH)
            m3, madd, msub, act2, nadd = sv(380, NCH, 3), sv(400, NCH), sv(405, NCH), sv(410, NCH), sv(415, NCH)
            stt(gt[0:NC], xn[0:NC, :, 16:80], 0.5, rev[0:NC, :, :], ALU.is_gt, ALU.mult)
            ts(m3[0:NC], xn[0:NC, :, 0:3], 0.5, None, ALU.is_gt)
            nc.vector.memset(feat[0:NC, :, 4, :], 1.0)
            link(nc.vector.tensor_copy(feat[0:NC, :, 2:4, :], xn[0:NC, :, 105:107].unsqueeze(3).to_broadcast([NC, NCH, 2, 2])))
            link(nc.vector.tensor_reduce(mx[0:NC, :], gt[0:NC].rearrange("p c (g n) -> p (c g) n", n=16), AX.X, ALU.max))
            link(ts(t1[0:NC, :], mx[0:NC, :], -1.0, 16.0, ALU.mult, ALU.add))
            stt(feat[0:NC, :, 0:2, :].rearrange("p c f s -> p c (f s)"), mx[0:NC, :].rearrange("p (c g) -> p c g", g=4), 0.0,
                t1[0:NC, :].rearrange("p (c g) -> p c g", g=4), ALU.is_gt, ALU.mult).then_inc(s_feat, 1)
            link(tt(madd[0:NC, :], m3[0:NC, :, 0], m3[0:NC, :, 1], ALU.mult))
            link(tt(nadd[0:NC, :], m3[0:NC, :, 0], madd[0:NC, :], ALU.subtract))
            link(tt(msub[0:NC, :], nadd[0:NC, :], m3[0:NC, :, 2], ALU.mult))
            link(tt(act2[0:NC, :], madd[0:NC, :], msub[0:NC, :], ALU.add))
            dve.wait_ge(s_fT, 1)
            dve.wait_ge(s_fTz, 1)
            nc.vector.tensor_copy(fT[0:2 * NF, 0:4 * NC], P[0:2 * NF, 0, 0:4 * NC])
            nc.vector.tensor_copy(fT[0:2 * NF, 4 * NC:N_NODES], P[0:2 * NF, 1, 0:NC]).then_inc(s_fTc, 1)
            dve.wait_ge(s_ffnw, n_ffnw[0])
            for g in range(0, 4 * NT, 2):
                layer, t, a, b = ffn_group(g)
                dve.wait_ge(s_fm, g + 1)
                ts(ffn_features(layer, t)[:, a:b], P[:, g % 8, 0:b - a], bf_c[:, t:t + 1] if layer else 0.0, 0.0,
                   ALU.add, ALU.max).then_inc(s_fd, 1)
            ya, ys, ysel = sv(460, NCH, 4), sv(480, NCH, 4), sv(500, NCH, 4)
            res, oh, car = sv(520, NCH, 2), sv(540, NCH * 2, 16), sv(700, NCH)
            dve.wait_ge(s_y3, 1)
            ts(y3T[:, 0:HALF], P[0:2 * CASES, 4, 0:HALF], b3_c[:, 0:1], None, ALU.add).then_inc(s_y3c, 1)
            dve.wait_ge(s_y3, 3)
            y3 = P[0:NC, 6, 0:2 * CASES * NCH].rearrange("p (c n) -> p c n", c=NCH)
            tt(ya[0:NC], y3[:, :, 0:4], madd[0:NC, :].unsqueeze(2).to_broadcast([NC, NCH, 4]), ALU.mult)
            link(tt(ys[0:NC], y3[:, :, 4:8], msub[0:NC, :].unsqueeze(2).to_broadcast([NC, NCH, 4]), ALU.mult))
            link(tt(ysel[0:NC], ya[0:NC], ys[0:NC], ALU.add))
            link(ts(res[0:NC], ysel[0:NC].rearrange("p c (s r) -> p c s r", s=2)[:, :, :, 0], 0.0, 15.0, ALU.max, ALU.min))
            link(ts(res[0:NC], res[0:NC], ROUND, None, ALU.add))
            link(ts(res[0:NC], res[0:NC], -ROUND, None, ALU.add))
            stt(car[0:NC, :], ysel[0:NC, :, 3], 0.5, act2[0:NC, :], ALU.is_gt, ALU.mult)
            link(ts(act2[0:NC, :], act2[0:NC, :], 2.0, None, ALU.mult))
            link(tt(oh[0:NC], iota[0:NC, 0:16].unsqueeze(1).to_broadcast([NC, NCH * 2, 16]),
                    res[0:NC].rearrange("p c s -> p (c s)").unsqueeze(2).to_broadcast([NC, NCH * 2, 16]), ALU.is_equal))
            link(tt(oh[0:NC].rearrange("p (c s) n -> p c (s n)", s=2), oh[0:NC].rearrange("p (c s) n -> p c (s n)", s=2),
                    act2[0:NC, :].unsqueeze(2).to_broadcast([NC, NCH, 32]), ALU.mult))
            dve.wait_ge(s_xsum, 1)
            tt(xs[0:NC, :, 128:160], xs[0:NC, :, 128:160], oh[0:NC].rearrange("p (c s) n -> p c (s n)", s=2), ALU.add)
            link(tt(xs[0:NC, :, 160:161], xs[0:NC, :, 160:161], car[0:NC, :].unsqueeze(2), ALU.add))
            norm()

            with dve.Fori(0, 3) as l:
                for c in range(NCH):
                    dve.wait_ge(s_gh, l * NCH + c + 1)
                    ts(Hn[0:NC, c, :], P[0:NC, c, :], dis_c[0:NC, c:c + 1], None, ALU.mult).then_inc(s_ghc, 1)
            dve.wait_ge(s_bg2, 16)

            def x3_chunk(c):
                dve.wait_ge(s_ga, 4 * KD + c + 1)
                link(tt(xn[0:NC, c, :], P[0:NC, (5 + c) % 8, :], bg2_b[0:NC, :], ALU.add))
                stt(xs[0:NC, c, :], xn[0:NC, c, :], 0.0, xs[0:NC, c, :], ALU.max, ALU.add).then_inc(s_x3, 1)
                dve.wait_ge(s_x3, c + 1)

            norm(x3_chunk, LAST_CHUNKS)

            bits = sv(0, NCH, 15)
            level = [None, sv(80, NCH, 2), sv(90, NCH, 4), sv(110, NCH, 8), leaf]
            dve.wait_ge(s_lg, 1)
            dve.wait_ge(s_cols, 16 * 4)
            link(tt(bits[0:NC], P[0:NC, 7, 0:NCH * 15].rearrange("p (c n) -> p c n", n=15),
                    br_b[0:NC, :].unsqueeze(1).to_broadcast([NC, NCH, 15]), ALU.add))
            link(ts(bits[0:NC], bits[0:NC], 0.0, None, ALU.is_gt))
            for d in range(4):
                w = 2 ** d
                right = level[d + 1][0:NC].rearrange("p c (j t) -> p c j t", t=2)
                here = bits[0:NC, :, w - 1:2 * w - 1]
                if d == 0:
                    nc.vector.tensor_copy(right[:, :, :, 1], here)
                    link(ts(right[:, :, :, 0], here, -1.0, 1.0, ALU.mult, ALU.add))
                else:
                    link(tt(right[:, :, :, 1], level[d][0:NC], here, ALU.mult))
                    link(tt(right[:, :, :, 0], level[d][0:NC], right[:, :, :, 1], ALU.subtract))
            nc.vector.tensor_copy(oh16[0:NC], leaf[0:NC]).then_inc(s_oh, 1)

            cmp, extra, cum, cumx = sv(290, NE, MORE), sv(402, NE), sv(418, NE), sv(434, NE)
            pick, rk, ce, le, ge, key = sv(450, NCH, NE), sv(530, NCH), sv(535, NCH), sv(540, NCH), sv(545, NCH), sv(550, NCH)
            cmpq, eid, more = sv(560, TAB - NE, NE), sv(690, TAB), sv(720, 5)
            dve.wait_ge(s_rank, 1)
            link(nc.vector.tensor_copy(cum[0:NC, :], P[0:NC, 6, 128:128 + NE]))
            link(tt(cmp[0:NC], cum[0:NC, :].unsqueeze(2).to_broadcast([NC, NE, MORE]),
                    thr[0:NC, 0:MORE].unsqueeze(1).to_broadcast([NC, NE, MORE]), ALU.is_gt))
            link(nc.vector.tensor_reduce(extra[0:NC, :], cmp[0:NC], AX.X, ALU.add))
            link(nc.vector.tensor_tensor_scan(cum[0:NC, :], ones[0:NC, 0:NE], extra[0:NC, :], 0.0, ALU.mult, ALU.add))
            link(stt(cumx[0:NC, :], cum[0:NC, :], float(NE - 1), extra[0:NC, :], ALU.add, ALU.subtract))

            def picked(to, values):
                link(tt(pick[0:NC], leaf[0:NC], values, ALU.mult))
                link(nc.vector.tensor_reduce(to[0:NC, :], pick[0:NC], AX.X, ALU.add))

            picked(rk, P[0:NC, 6, 0:NCH * NE].rearrange("p (c e) -> p c e", e=NE))
            picked(ce, cumx[0:NC, :].unsqueeze(1).to_broadcast([NC, NCH, NE]))
            picked(le, iota[0:NC, 0:NE].unsqueeze(1).to_broadcast([NC, NCH, NE]))
            link(tt(ce[0:NC, :], ce[0:NC, :], le[0:NC, :], ALU.subtract))
            link(stt(ge[0:NC, :], rk[0:NC, :], float(SLOTS), ce[0:NC, :], ALU.is_ge, ALU.mult))
            link(tt(ge[0:NC, :], ge[0:NC, :], le[0:NC, :], ALU.add))
            nc.vector.tensor_copy(lidx[0:NC, :], le[0:NC, :])
            link(stt(key[0:NC, :], ge[0:NC, :], float(SLOTS), rk[0:NC, :], ALU.mult, ALU.add))
            nc.vector.tensor_copy(gidx[0:NC, :], key[0:NC, :]).then_inc(s_keys, 1)
            tt(sel[0:NC], iota[0:NC, 0:SLOTS].unsqueeze(1).to_broadcast([NC, NCH, SLOTS]),
               key[0:NC, :].unsqueeze(2).to_broadcast([NC, NCH, SLOTS]), ALU.is_equal).then_inc(s_sel, 1)
            nc.vector.tensor_copy(eid[0:1, 0:NE], iota[0:1, 0:NE])
            link(tt(cmpq[0:1], cum[0:1, :].unsqueeze(1).to_broadcast([1, TAB - NE, NE]),
                    iota[0:1, 0:TAB - NE].unsqueeze(2).to_broadcast([1, TAB - NE, NE]), ALU.is_le))
            link(nc.vector.tensor_reduce(eid[0:1, NE:TAB], cmpq[0:1], AX.X, ALU.add))
            ts(tab[0:1, :], eid[0:1, :], float(NE - 1), None, ALU.min)
            link(ts(more[0:1, 0:4], iota[0:1, 0:4], 2.0, cum[0:1, NE - 1:NE], ALU.mult, ALU.is_lt))
            link(nc.vector.tensor_reduce(more[0:1, 4:5], more[0:1, 0:4], AX.X, ALU.add))
            ts(npairs_t[0:1, :], more[0:1, 4:5], float(NE // 2), None, ALU.add).then_inc(s_table, 1)

            dve.wait_ge(s_b1T, 1)
            nc.vector.tensor_copy(b1T, P[:, 5, 0:256]).then_inc(s_b1Tc, 1)

            def copy_inputs(i, b):
                dve.wait_ge(s_xT, i + 1)
                nc.vector.tensor_copy(xT[b], P[:, 6, 0:KD * SLOTS].rearrange("p (k s) -> p k s", k=KD)).then_inc(s_xTc, 1)

            dve.wait_ge(s_table, 1)
            copy_inputs(0, 0)
            dve.wait_ge(s_b1Tc, 1)
            pairs = dve.value_load(npairs_t[0:1, 0:1], min_val=NE // 2, max_val=MAX_PAIRS)
            with dve.Fori(0, pairs) as p:
                for b in range(2):
                    i = 2 * p + b
                    e = dve.value_load(tab[0:1, bass.ds(i, 1)], min_val=0, max_val=NE - 1)
                    for t in range(2):
                        dve.wait_ge(s_h, 3 * i + t + 1)
                        nc.vector.tensor_copy(h_sb[:, t, :], P[:, t, :]).then_inc(s_hc, 1)
                        if t == 0:
                            nc.vector.tensor_copy(bT[b], b1T[:, bass.ds(e * MH, MH)]).then_inc(s_bTc, 1)
                    dve.wait_ge(s_h, 3 * i + 3)
                    nc.vector.tensor_copy(h_sb[:, 2, :], P[:, 2, :]).then_inc(s_hc, 1)
                    copy_inputs(i + 1, 1 - b)
            dve.wait_ge(s_x3b, 1)
            for c in range(NCH):
                dve.wait_ge(s_gat[c], 16)
                tt(xs[0:NC, c, :], xs[0:NC, c, :], xn[0:NC, c, :], ALU.add).then_inc(s_fin, 1)


_INS = ["x", "src", "dst", "L0_gnn_W_conv", "L0_gnn_b_conv", "L0_gnn_W_lin", "L0_gnn_b_lin", "L0_ffn_Wa", "L0_ffn_ba",
        "L0_ffn_Ws", "L0_ffn_bs", "L1_gnn_W", "L1_gnn_b", "L1_ffn_Wr", "L1_ffn_br", "L1_ffn_W1", "L1_ffn_b1",
        "L1_ffn_W2", "L1_ffn_b2"]


def kernel(**inputs):
    import numpy as _np
    import concourse.bacc as _bacc
    from concourse import mybir as _mybir
    from concourse.bass_utils import run_bass_kernel_spmd as _run

    nc = _bacc.Bacc("TRN2", target_bir_lowering=False, num_devices=1)
    arrays, args = {}, []
    for name in _INS:
        a = _np.ascontiguousarray(inputs[name])
        arrays[f"in_{name}"] = a
        args.append(nc.dram_tensor(f"in_{name}", a.shape, _mybir.dt.from_np(a.dtype), kind="ExternalInput").ap())
    args.append(nc.dram_tensor("out_0", (N_NODES, DIM), _mybir.dt.float32, kind="ExternalOutput").ap())
    build(nc, *args)
    r = _run(nc, [arrays], core_ids=[0])
    return r.results[0]["out_0"]
```
